# Optimizing a Trainium2 kernel written in Bass

```python
import numpy as np
import jax
import jax.numpy as jnp

def _softmax(x, axis=-1):
    return jax.nn.softmax(x, axis=axis)

def _gelu(x):
    return jax.nn.gelu(x, approximate=True)

def _silu(x):
    return jax.nn.silu(x)

def _sigmoid(x):
    return jax.nn.sigmoid(x)

def _layernorm(x, axis=-1, eps=1e-05):
    m = jnp.mean(x, axis=axis, keepdims=True)
    v = jnp.var(x, axis=axis, keepdims=True)
    return (x - m) / jnp.sqrt(v + eps)

def _scatter_add(tgt, idx, src, axis=0):
    return tgt.at[idx].add(src)

def _segment_sum(src, seg, n):
    return jax.ops.segment_sum(src, seg, n)
kernel_name = 'mk_decoder_postln_d1_seqx_r4_e13aba'

def setup_inputs(seed: int=0):
    np.random.seed(seed)
    _w = jnp.asarray

    def _rec_inputs():
        import jax
        import jax.numpy as jnp
        _rk = jax.random.key(seed)
        x = -0.0002928 + 1 * jax.random.normal(jax.random.fold_in(_rk, 1), (32, 112, 256), jnp.float32)
        _lenS = 112 - jax.random.randint(jax.random.fold_in(_rk, 7), (32,), 0, max(1, 112 // 4) + 1, jnp.int32)
        _lenS2 = 375 - jax.random.randint(jax.random.fold_in(_rk, 8), (32,), 0, max(1, 375 // 4) + 1, jnp.int32)
        _ctx_1024P = jax.random.normal(jax.random.fold_in(_rk, 11), (32, 16, 256), jnp.float32)
        _ctx_1024c = jax.random.dirichlet(jax.random.fold_in(_rk, 511), 0.3 * jnp.ones((16,), jnp.float32), (32, 375))
        _ctx_1024t = jnp.einsum('bsk,bkd->bsd', _ctx_1024c, _ctx_1024P)
        _ctx_1024t = _ctx_1024t * jax.lax.rsqrt(jnp.mean(jnp.square(_ctx_1024t)) + 1e-12) * 0.953939
        ctx_1024 = -1.39393e-06 + 0.999914 * (_ctx_1024t + 0.3 * jax.random.normal(jax.random.fold_in(_rk, 611), (32, 375, 256), jnp.float32))
        return (x, ctx_1024)
    x, ctx_1024 = _rec_inputs()

    def _L0_attn_setup():
        import jax, jax.numpy as jnp
        import numpy as np
        D_MODEL = 256
        N_HEADS = 16
        HEAD_DIM = D_MODEL // N_HEADS
        BATCH = 2
        SEQ = 512

        def _alibi_bias(seq_len, n_heads, dtype):
            slopes = 1.0 / 2.0 ** (jnp.arange(n_heads, dtype=dtype) / n_heads)
            rel = jnp.arange(seq_len, dtype=dtype)[None, :] - jnp.arange(seq_len, dtype=dtype)[:, None]
            return slopes[:, None, None] * rel[None, :, :]
        key = jax.random.key(seed)
        ks = jax.random.split(key, 9)
        s = 0.02
        return {'x': jax.random.normal(ks[0], (BATCH, SEQ, D_MODEL), dtype=jnp.float32), 'Wq': jax.random.normal(ks[1], (D_MODEL, D_MODEL), dtype=jnp.float32) * s, 'bq': jnp.zeros((D_MODEL,), dtype=jnp.float32), 'Wk': jax.random.normal(ks[2], (D_MODEL, D_MODEL), dtype=jnp.float32) * s, 'bk': jnp.zeros((D_MODEL,), dtype=jnp.float32), 'Wv': jax.random.normal(ks[3], (D_MODEL, D_MODEL), dtype=jnp.float32) * s, 'bv': jnp.zeros((D_MODEL,), dtype=jnp.float32), 'Wo': jax.random.normal(ks[4], (D_MODEL, D_MODEL), dtype=jnp.float32) * s, 'bo': jnpp_zeros() if False else jnp.zeros((D_MODEL,), dtype=jnp.float32)}
    _L0_attn_all = _L0_attn_setup()
    _L0_attn_in = {k: v for k, v in _L0_attn_all.items() if k in ('Wq', 'bq', 'Wk', 'bk', 'Wv', 'bv', 'Wo', 'bo')}
    del _L0_attn_all

    def _L0_xattn_setup():
        import jax, jax.numpy as jnp
        import numpy as np
        import math
        D_MODEL = 256
        N_HEADS = 16
        D_HEAD = D_MODEL // N_HEADS
        key = jax.random.key(seed)
        ks = jax.random.split(key, 11)
        N, L, S = (2, 512, 512)
        inp = {'queries': jax.random.normal(ks[0], (N, L, D_MODEL), dtype=jnp.float32), 'keys': jax.random.normal(ks[1], (N, S, D_MODEL), dtype=jnp.float32), 'values': jax.random.normal(ks[2], (N, S, D_MODEL), dtype=jnp.float32), 'Wq': jax.random.normal(ks[3], (D_MODEL, N_HEADS * D_HEAD), dtype=jnp.float32) / math.sqrt(D_MODEL), 'bq': jnp.zeros((N_HEADS * D_HEAD,), dtype=jnp.float32), 'Wk': jax.random.normal(ks[4], (D_MODEL, N_HEADS * D_HEAD), dtype=jnp.float32) / math.sqrt(D_MODEL), 'bk': jnp.zeros((N_HEADS * D_HEAD,), dtype=jnp.float32), 'Wv': jax.random.normal(ks[5], (D_MODEL, N_HEADS * D_HEAD), dtype=jnp.float32) / math.sqrt(D_MODEL), 'bv': jnp.zeros((N_HEADS * D_HEAD,), dtype=jnp.float32), 'Wo': jax.random.normal(ks[6], (N_HEADS * D_HEAD, D_MODEL), dtype=jnp.float32) / math.sqrt(N_HEADS * D_HEAD), 'bo': jnp.zeros((D_MODEL,), dtype=jnp.float32)}
        return inp
    _L0_xattn_all = _L0_xattn_setup()
    _L0_xattn_in = {k: v for k, v in _L0_xattn_all.items() if k in ('Wq', 'bq', 'Wk', 'bk', 'Wv', 'bv', 'Wo', 'bo')}
    del _L0_xattn_all

    def _L0_ffn_setup():
        import jax, jax.numpy as jnp
        import numpy as np
        BLOCK = 32
        W_BITS = 4
        ACT_BITS = 16

        def act_qdq(x):
            qmax = 2.0 ** (ACT_BITS - 1) - 1.0
            scale = jnp.maximum(jnp.max(jnp.abs(x)) / qmax, 1e-12)
            return jnp.clip(jnp.round(x / scale), -qmax - 1.0, qmax) * scale

        def fixed_qdq_u16(x):
            scale = 1.0 / 65536.0
            return jnp.clip(jnp.round(x / scale), 0.0, 65535.0) * scale

        def lpbq_dequant(w):
            O, I = w.shape
            qmax = 2.0 ** (W_BITS - 1) - 1.0
            wb = w.reshape(O, I // BLOCK, BLOCK)
            s = jnp.maximum(jnp.max(jnp.abs(wb), axis=-1, keepdims=True) / qmax, 1e-12)
            wq = jnp.clip(jnp.round(wb / s), -qmax - 1.0, qmax) * s
            return wq.reshape(O, I)
        key = jax.random.key(seed)
        k1, k2, k3, k4 = jax.random.split(key, 4)
        B, S, H, I = (2, 1024, 256, 768)
        x = jax.random.normal(k1, (B, S, H), jnp.float32)
        w_gate = jax.random.normal(k2, (I, H), jnp.float32) * 0.02
        w_up = jax.random.normal(k3, (I, H), jnp.float32) * 0.02
        w_down = jax.random.normal(k4, (H, I), jnp.float32) * 0.02
        return {'x': x, 'w_gate': w_gate, 'w_up': w_up, 'w_down': w_down}
    _L0_ffn_all = _L0_ffn_setup()
    _L0_ffn_in = {k: v for k, v in _L0_ffn_all.items() if k in ('w_gate', 'w_up', 'w_down')}
    del _L0_ffn_all
    return {'x': x, 'ctx_1024': ctx_1024, 'L0_attn_Wq': _L0_attn_in['Wq'], 'L0_attn_bq': _L0_attn_in['bq'], 'L0_attn_Wk': _L0_attn_in['Wk'], 'L0_attn_bk': _L0_attn_in['bk'], 'L0_attn_Wv': _L0_attn_in['Wv'], 'L0_attn_bv': _L0_attn_in['bv'], 'L0_attn_Wo': _L0_attn_in['Wo'], 'L0_attn_bo': _L0_attn_in['bo'], 'L0_xattn_Wq': _L0_xattn_in['Wq'], 'L0_xattn_bq': _L0_xattn_in['bq'], 'L0_xattn_Wk': _L0_xattn_in['Wk'], 'L0_xattn_bk': _L0_xattn_in['bk'], 'L0_xattn_Wv': _L0_xattn_in['Wv'], 'L0_xattn_bv': _L0_xattn_in['bv'], 'L0_xattn_Wo': _L0_xattn_in['Wo'], 'L0_xattn_bo': _L0_xattn_in['bo'], 'L0_ffn_w_gate': _L0_ffn_in['w_gate'], 'L0_ffn_w_up': _L0_ffn_in['w_up'], 'L0_ffn_w_down': _L0_ffn_in['w_down']}

def reference(x, ctx_1024, L0_attn_Wq, L0_attn_bq, L0_attn_Wk, L0_attn_bk, L0_attn_Wv, L0_attn_bv, L0_attn_Wo, L0_attn_bo, L0_xattn_Wq, L0_xattn_bq, L0_xattn_Wk, L0_xattn_bk, L0_xattn_Wv, L0_xattn_bv, L0_xattn_Wo, L0_xattn_bo, L0_ffn_w_gate, L0_ffn_w_up, L0_ffn_w_down):
    import jax
    import jax.numpy as jnp

    def _L0_attn_ref(x, Wq, bq, Wk, bk, Wv, bv, Wo, bo):
        import jax, jax.numpy as jnp
        import numpy as np
        D_MODEL = 256
        N_HEADS = 16
        HEAD_DIM = D_MODEL // N_HEADS
        BATCH = 2
        SEQ = 512

        def _alibi_bias(seq_len, n_heads, dtype):
            slopes = 1.0 / 2.0 ** (jnp.arange(n_heads, dtype=dtype) / n_heads)
            rel = jnp.arange(seq_len, dtype=dtype)[None, :] - jnp.arange(seq_len, dtype=dtype)[:, None]
            return slopes[:, None, None] * rel[None, :, :]
        B, S, D = x.shape
        H, Hd = (N_HEADS, HEAD_DIM)
        scale = Hd ** (-0.5)
        Q = (x @ Wq + bq).reshape(B, S, H, Hd)
        K = (x @ Wk + bk).reshape(B, S, H, Hd)
        V = (x @ Wv + bv).reshape(B, S, H, Hd)
        scores = jnp.einsum('bqhd,bkhd->bhqk', Q, K) * scale
        scores = scores + _alibi_bias(S, H, x.dtype)[None]
        attn = jax.nn.softmax(scores, axis=-1)
        out = jnp.einsum('bhqk,bkhd->bqhd', attn, V).reshape(B, S, D)
        return out @ Wo + bo

    def _L0_xattn_ref(queries, keys, values, Wq, bq, Wk, bk, Wv, bv, Wo, bo):
        import jax, jax.numpy as jnp
        import numpy as np
        import math
        D_MODEL = 256
        N_HEADS = 16
        D_HEAD = D_MODEL // N_HEADS
        N, L, _ = queries.shape
        S = keys.shape[1]
        H, D = (N_HEADS, D_HEAD)
        q = (queries @ Wq + bq).reshape(N, L, H, D)
        k = (keys @ Wk + bk).reshape(N, S, H, D)
        v = (values @ Wv + bv).reshape(N, S, H, D)
        sm = jnp.einsum('nlhd,nshd->nlhs', q, k) / math.sqrt(D)
        sm = jax.nn.softmax(sm, axis=1)
        attn = jnp.einsum('nlhs,nshd->nlhd', sm, v).reshape(N, L, H * D)
        return attn @ Wo + bo

    def _L0_ffn_ref(x, w_gate, w_up, w_down):
        import jax, jax.numpy as jnp
        import numpy as np
        BLOCK = 32
        W_BITS = 4
        ACT_BITS = 16

        def act_qdq(x):
            qmax = 2.0 ** (ACT_BITS - 1) - 1.0
            scale = jnp.maximum(jnp.max(jnp.abs(x)) / qmax, 1e-12)
            return jnp.clip(jnp.round(x / scale), -qmax - 1.0, qmax) * scale

        def fixed_qdq_u16(x):
            scale = 1.0 / 65536.0
            return jnp.clip(jnp.round(x / scale), 0.0, 65535.0) * scale

        def lpbq_dequant(w):
            O, I = w.shape
            qmax = 2.0 ** (W_BITS - 1) - 1.0
            wb = w.reshape(O, I // BLOCK, BLOCK)
            s = jnp.maximum(jnp.max(jnp.abs(wb), axis=-1, keepdims=True) / qmax, 1e-12)
            wq = jnp.clip(jnp.round(wb / s), -qmax - 1.0, qmax) * s
            return wq.reshape(O, I)
        x = act_qdq(x)
        up = act_qdq(x @ lpbq_dequant(w_up).T)
        gate = act_qdq(x @ lpbq_dequant(w_gate).T)
        sig = fixed_qdq_u16(jax.nn.sigmoid(gate))
        gate = act_qdq(gate * sig)
        o = act_qdq(gate * up)
        return o @ lpbq_dequant(w_down).T
    x = _layernorm(x + _L0_attn_ref(x, L0_attn_Wq, L0_attn_bq, L0_attn_Wk, L0_attn_bk, L0_attn_Wv, L0_attn_bv, L0_attn_Wo, L0_attn_bo), axis=-1)
    x = _layernorm(x + _L0_xattn_ref(x, ctx_1024, ctx_1024, L0_xattn_Wq, L0_xattn_bq, L0_xattn_Wk, L0_xattn_bk, L0_xattn_Wv, L0_xattn_bv, L0_xattn_Wo, L0_xattn_bo), axis=-1)
    x = _layernorm(x + _L0_ffn_ref(x, L0_ffn_w_gate, L0_ffn_w_up, L0_ffn_w_down), axis=-1)
    return x

_drawn_inputs = setup_inputs


def setup_inputs(seed=0):
    import zlib

    import numpy as np

    out = dict(_drawn_inputs(seed))
    spreads = {'L0_attn_bq': (0.0, 2.0),
     'L0_attn_bk': (0.0, 2.0),
     'L0_attn_bv': (0.0, 0.548),
     'L0_attn_bo': (0.0, 0.1),
     'L0_xattn_bq': (0.0, 2.0),
     'L0_xattn_bk': (0.0, 0.1),
     'L0_xattn_bv': (0.0, 0.1),
     'L0_xattn_bo': (0.0, 0.1)}
    factors = {'L0_attn_Wq': 8.0, 'L0_attn_Wk': 8.0}
    for name, (base, spread) in spreads.items():
        noise = np.random.default_rng([zlib.crc32(name.encode()), seed]).standard_normal(out[name].shape)
        drawn = base * np.exp(spread * noise) if base else spread * noise
        out[name] = jnp.asarray(drawn.astype(out[name].dtype))
    for name, factor in factors.items():
        out[name] = (out[name] * factor).astype(out[name].dtype)
    return out
```

```python
from contextlib import ExitStack

import numpy as np
import concourse.bass as bass
from concourse import mybir

F32 = mybir.dt.float32
F32R = mybir.dt.float32r
BF16 = mybir.dt.bfloat16
I16 = mybir.dt.int16
U16 = mybir.dt.uint16
ALU = mybir.AluOpType
ACT = mybir.ActivationFunctionType
AX = mybir.AxisListType

B, L, S, D = 32, 112, 375, 256
H, HD = 16, 16
P = 128
KT = D // P
OCT, QUAD = 8, 4
NC = 3
C = S // NC
SP = S + 1
NU = KT * NC
QW = QUAD * L
BANK = 512
SCALE = HD ** -0.5
EPS = 1e-5
F = 768
FT = F // P
GT = 4 * L
NG = B * L // GT
QBLK = 32
QMAX = 2.0 ** 15 - 1.0
WMAX = 2.0 ** 3 - 1.0
TINY = 1e-12
SIGQ = 65536.0
LOW = 15
HIGH = -16


class Batch:

    def __init__(self, pair, off):
        self.pair, self.off = pair, off
        self.par = off % 2

    def plus(self, d):
        return Batch(self.pair, self.off + d)

    def times(self, per, more=0):
        fixed = per * self.off + more
        return fixed if isinstance(self.pair, int) else self.pair * (2 * per) + fixed

    def loads(self):
        fixed = 16 * (self.off // 2 + 1)
        return fixed if isinstance(self.pair, int) else self.pair * 16 + fixed


def wait(eng, sem, value):
    if isinstance(value, int) and value <= 0:
        return
    eng.wait_ge(sem, value)


BANK_USES = {
    0: [("ctxT1", "next"), ("K1", "next"), ("PT1", "next"), ("Ox", "tail"), ("V1", "next"), ("PT2", "next"),
        ("Ks", "pre"), ("Qs", "pre"), ("Os", "next"), ("Vs", "pre"), ("Qx", "next")],
    1: [("ctxT0", "next"), ("K0", "next"), ("PT0", "next"), ("V0", "next"), ("AVs0", "next"), ("xTs", "pre"),
        ("PT3", "next"), ("AVs1", "next"), ("V2", "next"), ("x2T", "tail"), ("x1T", "next")],
}
BANK_OF = {name: bank for bank, uses in BANK_USES.items() for name, _ in uses}
PART_SPAN = {"pre": (-2, B - 3), "next": (-1, B - 2), "cross": (0, B - 1), "tail": (1, B)}


class Iteration:

    def __init__(self, pair, off):
        self.i = Batch(pair, off)
        self.looped = not isinstance(pair, int)
        self.has = {p: self.looped or a <= off <= b for p, (a, b) in PART_SPAN.items()}
        self.tail, self.next, self.pre = self.i.plus(-1), self.i.plus(1), self.i.plus(2)

    def fills(self, use):
        bank, before = BANK_OF[use], 0
        for name, part in BANK_USES[bank]:
            if name == use:
                break
            before += self.has[part]
        if self.looped:
            per, more = 0, before
            for _, part in BANK_USES[bank]:
                per += 1
                more -= PART_SPAN[part][0]
            return self.i.times(per, more)
        for _, part in BANK_USES[bank]:
            a, b = PART_SPAN[part]
            before += max(0, min(self.i.off - a, b - a + 1))
        return before


def decoder(nc, a, out, x2_dram):
    with ExitStack() as persist:
        def keep(name, shape, dt=F32):
            return persist.enter_context(nc.sbuf_tensor(name, shape, dt))

        ident = keep("ident", [P, P])
        x2T_all = keep("x2T_all", [P, KT, B * L])
        xmax_all = keep("xmax_all", [P, B])
        wT = {n: [keep(f"{n}T_{p}", [P, KT, F], F32R) for p in ("hi", "lo")] for n in ("w_up", "w_gate")}
        w_down = keep("w_down", [P, KT, F])
        quantise_weights(nc, a, ident, wT, w_down)
        attention(nc, a, ident, x2T_all, xmax_all, x2_dram)
        feed_forward(nc, out, x2_dram, ident, x2T_all, xmax_all, wT, w_down)


def quantise_weights(nc, a, ident, wT, w_down):
    NB = KT * F // QBLK
    with ExitStack() as ctx:
        def sb(name, shape, dt=F32):
            return ctx.enter_context(nc.sbuf_tensor(name, shape, dt))

        def sem(name):
            return ctx.enter_context(nc.semaphore(name))

        order = ("w_up", "w_gate", "w_down")
        raw = {n: sb(f"raw_{n}", [P, NB, QBLK]) for n in order}
        quant = {n: sb(f"quant_{n}", [P, NB, QBLK], I16) for n in order}
        value = {n: sb(f"value_{n}", [P, NB, QBLK]) for n in order[:2]}
        scale = {n: sb(f"scale_{n}", [P, NB]) for n in order}
        inverse = {n: sb(f"inverse_{n}", [P, NB]) for n in order}
        bank = [ctx.enter_context(nc.psum_tensor(f"wbank{p}", [P, BANK], F32)) for p in range(2)]
        HALF = F // 2
        N_FILLS = 2 * KT
        loaded = {n: sem(f"loaded_{n}") for n in order}
        ident_ld, step_done, value_done = sem("ident_ld"), sem("step_done"), sem("value_done")
        turned, hi_done, lo_done = sem("turned"), sem("hi_done"), sem("lo_done")
        block = ctx.enter_context(nc.Block())

        @block.sync
        def _(sp):
            for n in order:
                sp.dma_start(raw[n][:].rearrange("p (t b) e -> p t (b e)", t=a[n].shape[0] // P),
                             a[n].rearrange("(t p) i -> p t i", p=P)).then_inc(loaded[n], 16)
            sp.dma_start(ident[:], a["ident"]).then_inc(ident_ld, 16)

        @block.vector
        def _(dve):
            def lo_half(f):
                n, k, h = order[f // N_FILLS], (f // 2) % KT, f % 2
                cols = slice(h * HALF, (h + 1) * HALF)
                dve.wait_ge(hi_done, f + 1)
                dve.tensor_tensor(wT[n][1][:, k, cols], bank[f % 2][:, 0:HALF], wT[n][0][:, k, cols].bitcast(F32),
                                  ALU.subtract).then_inc(lo_done, 1)

            for e, n in enumerate(order):
                dve.wait_ge(loaded[n], 16)
                dve.tensor_reduce(scale[n][:], raw[n][:], AX.X, ALU.max, apply_absolute_value=True)\
                    .then_inc(step_done, 1)
                dve.wait_ge(step_done, 4 * e + 1)
                dve.tensor_scalar(scale[n][:], scale[n][:], 1.0 / WMAX, TINY, ALU.mult, ALU.max).then_inc(step_done, 1)
                dve.wait_ge(step_done, 4 * e + 2)
                dve.reciprocal(inverse[n][:], scale[n][:]).then_inc(step_done, 1)
                dve.wait_ge(step_done, 4 * e + 3)
                dve.tensor_tensor(quant[n][:], raw[n][:],
                                  inverse[n][:].rearrange("p (b o) -> p b o", o=1).broadcast_to([P, NB, QBLK]),
                                  ALU.mult).then_inc(step_done, 1)
                dve.wait_ge(step_done, 4 * e + 4)
                dst = value[n][:] if n in value else w_down[:].rearrange("p t (b e) -> p (t b) e", e=QBLK)
                dve.tensor_tensor(dst, quant[n][:],
                                  scale[n][:].rearrange("p (b o) -> p b o", o=1).broadcast_to([P, NB, QBLK]),
                                  ALU.mult).then_inc(value_done, 1)
            for f in range(2 * N_FILLS):
                lo_half(f)

        @block.scalar
        def _(act):
            for f in range(2 * N_FILLS):
                n, k, h = order[f // N_FILLS], (f // 2) % KT, f % 2
                act.wait_ge(turned, f + 1)
                act.activation(wT[n][0][:, k, h * HALF:(h + 1) * HALF], bank[f % 2][:, 0:HALF], ACT.Copy)\
                    .then_inc(hi_done, 1)

        @block.tensor
        def _(pe):
            pe.wait_ge(ident_ld, 16)
            for f in range(2 * N_FILLS):
                e, k, h = f // N_FILLS, (f // 2) % KT, f % 2
                pe.wait_ge(value_done, e + 1)
                if f >= 2:
                    pe.wait_ge(lo_done, f - 1)
                rows = value[order[e]][:].rearrange("p (t b) e -> p t (b e)", t=FT)
                for j in range(FT // 2):
                    ins = pe.transpose(bank[f % 2][:, j * P:(j + 1) * P],
                                       rows[:, h * (FT // 2) + j, k * P:(k + 1) * P], ident[:])
                ins.then_inc(turned, 1)


def attention(nc, a, ident, x2T_all, xmax_all, x2_dram):
    with ExitStack() as ctx:
        def sb(name, shape, dt=F32):
            return ctx.enter_context(nc.sbuf_tensor(name, shape, dt))

        def sem(name):
            return ctx.enter_context(nc.semaphore(name))

        names = ("aWq", "aWk", "aWv", "aWo", "xWq", "xWk", "xWv", "xWo")
        early = {"xWk": 0, "xWv": KT * D}
        w = {n: sb(n, [P, KT, D]) for n in names if n not in early}
        for n, at in early.items():
            w[n] = x2T_all[:, 0, at:at + KT * D].rearrange("p (k n) -> p k n", k=KT)
        split = {n: [sb(f"{n}_{p}", [P, KT, D], F32R) for p in ("hi", "lo")] for n in ("xWk", "xWv")}
        bcol = {n: sb(n, [P, KT]) for n in ("abq", "abk", "xbq", "xbk")}
        brow = {n: sb(n, [P, D]) for n in ("abv", "abo", "xbv", "xbo")}
        mask8 = sb("mask8", [P, OCT])
        even_odd = sb("even_odd", [P, 2])
        sel_raw = x2T_all[:, 1, 0:OCT * L]
        sel = sb("sel", [P, OCT * L], F32R)
        alibi_l = sb("alibi_l", [6, L], BF16)
        alibi_r = sb("alibi_r", [6, H * L], BF16)
        half = sb("half", [P, 1])
        warm = sb("warm", [P, 2])

        x_in = [sb(f"x_in{p}", [L, D]) for p in range(2)]
        ctx_in = [sb(f"ctx_in{p}", [C, NC, D]) for p in range(2)]
        ctxT = [sb(f"ctxT_{p}", [P, KT, SP], F32R) for p in ("hi", "lo")]
        KxT = [[sb(f"KxT{q}_{p}", [P, KT, S], F32R) for p in ("hi", "lo")] for q in range(2)]
        Vx = [sb(f"Vx{p}", [C, NC, D]) for p in range(2)]
        Qx = [sb(f"Qx_{p}", [P, KT, L], F32R) for p in ("hi", "lo")]
        Qbd = [sb(f"Qbd_{p}", [P, H, L], F32R) for p in ("hi", "lo")]
        Qs = [sb(f"Qs_{p}", [P, KT, L], F32R) for p in ("hi", "lo")]
        Ks = [sb(f"Ks_{p}", [P, KT, L], F32R) for p in ("hi", "lo")]
        Kbd = [sb(f"Kbd_{p}", [P, H, L], F32R) for p in ("hi", "lo")]
        xT = sb("xT", [P, KT, L])
        Vs = sb("Vs", [L, D])
        Ps = sb("Ps", [L, H, L])
        PsT = sb("PsT", [L, H, L])
        nmax_s = sb("nmax_s", [L, H])
        Zs = sb("Zs", [L, H])
        rZs = sb("rZs", [L, H])
        rZrep = sb("rZrep", [L, KT, OCT, HD])
        evenT = sb("evenT", [P, KT, L])
        sumT = sb("sumT", [P, KT, L])
        attnT = sb("attnT", [P, KT, L])
        xb = sb("xb", [L, D])
        r1 = sb("r1", [L, D])
        x1 = sb("x1", [L, D])
        x1T = sb("x1T", [P, KT, L])
        x1b = [sb(f"x1b{p}", [L, D]) for p in range(2)]
        nmax_c = [sb(f"nmax_c{p}", [C, P]) for p in range(2)]
        nmaxT = [sb(f"nmaxT{p}", [P, SP // NC + 1], F32R) for p in range(2)]
        Px = [sb(f"Px{p}", [C, OCT, L]) for p in range(2)]
        Zc = [sb(f"Zc{p}", [C, OCT]) for p in range(2)]
        rZc = [sb(f"rZc{p}", [C, OCT]) for p in range(2)]
        Vn = [sb(f"Vn{p}", [C, OCT, HD]) for p in range(2)]
        evenX = sb("evenX", [P, KT, L])
        OxT = sb("OxT", [P, KT, L])
        r2 = sb("r2", [L, D])
        x2 = sb("x2", [L, D])
        carrier = sb("carrier", [1, 1])
        stats = [sb(f"stats{p}", [L, 6]) for p in range(2)]
        mv = [sb(f"mv{p}", [L, 2]) for p in range(2)]
        vare = [sb(f"vare{p}", [L, 1]) for p in range(2)]
        rstd = [sb(f"rstd{p}", [L, 1]) for p in range(2)]

        score = [ctx.enter_context(nc.psum_tensor(f"score{p}", [P, 2, BANK], F32)) for p in range(2)]
        work = [ctx.enter_context(nc.psum_tensor(f"work{p}", [P, BANK], F32)) for p in range(2)]
        outX = ctx.enter_context(nc.psum_tensor("outX", [P, KT, 2 * L], F32))
        maxT = ctx.enter_context(nc.psum_tensor("maxT", [P, 2, BANK // 2], F32))

        const_ld = sem("const_ld")
        consts = sem("consts")
        x_ld = [sem(f"x_ld{p}") for p in range(2)]
        ctx_ld = [sem(f"ctx_ld{p}") for p in range(2)]
        filled = [sem(f"filled{p}") for p in range(2)]
        drained = [sem(f"drained{p}") for p in range(2)]
        ctx_hi, kx_hi, ks_hi, qs_hi, qx_hi = (sem(n) for n in ("ctx_hi", "kx_hi", "ks_hi", "qs_hi", "qx_hi"))
        kbd_done, qbd_done = sem("kbd_done"), sem("qbd_done")
        scores_s, nmax_s_done, exp_s = sem("scores_s"), sem("nmax_s_done"), sem("exp_s")
        rz_s, rzrep_s, even_s, sum_s = sem("rz_s"), sem("rzrep_s"), sem("even_s"), sem("sum_s")
        scores_c, nmax_c_done, nmaxT_done = sem("scores_c"), sem("nmax_c_done"), sem("nmaxT_done")
        nmaxT_copied, shifted, exp_c = sem("nmaxT_copied"), sem("shifted"), sem("exp_c")
        z_c, rz_c, vn_done, av_done = sem("z_c"), sem("rz_c"), sem("vn_done"), sem("av_done")
        even_x, oxT_done = sem("even_x"), sem("oxT_done")
        xb_done, x1b_done = sem("xb_done"), sem("x1b_done")
        bn_done = [sem(f"bn_done{p}") for p in (1, 2)]
        mv_done = [sem(f"mv_done{p}") for p in (1, 2)]
        var_done = [sem(f"var_done{p}") for p in (1, 2)]
        rstd_done = [sem(f"rstd_done{p}") for p in (1, 2)]
        x1_done, x2_done, x2T_copied, x2_saved = sem("x1_done"), sem("x2_done"), sem("x2T_copied"), sem("x2_saved")

        x_dram, ctx_dram = a["x"], a["ctx"]
        columns = {"abq": "a_bq", "abk": "a_bk", "xbq": "x_bq", "xbk": "x_bk"}
        rows = {"abv": "a_bv", "abo": "a_bo", "xbv": "x_bv", "xbo": "x_bo"}
        N_CONST = len(names) + len(columns) + len(rows) + 5

        def pairs_loop(eng, step):
            for k in (-2, -1, 0):
                step(Iteration(0, k))
            with eng.Fori(0, (B - 4) // 2) as r:
                step(Iteration(r, 1))
                step(Iteration(r, 2))
            for k in range(B - 3, B + 1):
                step(Iteration(0, k))

        def wait_fill(eng, it, use):
            n = it.fills(use)
            eng.wait_ge(filled[BANK_OF[use]], n + 1)

        def wait_drain(eng, it, use):
            n = it.fills(use)
            eng.wait_ge(drained[BANK_OF[use]], n + 1)

        block = ctx.enter_context(nc.Block())

        @block.sync
        def _(sp):
            for n in names[:4]:
                sp.dma_start(w[n] if n in early else w[n][:], a[n].rearrange("(k p) n -> p k n", p=P)).then_inc(const_ld, 16)
            for n, src in columns.items():
                sp.dma_start(bcol[n][:], a[src].rearrange("(m p) -> p m", p=P), allow_slow_non_contiguous=True).then_inc(const_ld, 16)

            def load_x(n):
                sp.dma_start(x_in[n.par][:], x_dram[bass.ds(n.times(1), 1)].rearrange("o l d -> (o l) d"))\
                    .then_inc(x_ld[n.par], 16)

            def load_ctx(n):
                sp.dma_start(ctx_in[n.par][:],
                             ctx_dram[bass.ds(n.times(1), 1)].rearrange("o (c s) d -> s (o c) d", c=NC))\
                    .then_inc(ctx_ld[n.par], 16)

            def step(it):
                if it.has["next"] and (it.looped or it.i.off + 3 < B):
                    wait_fill(sp, it, "ctxT1")
                    load_ctx(it.i.plus(3))
                if it.has["tail"]:
                    sp.wait_ge(x2_done, it.tail.times(1, 1))
                    sp.dma_start(x2_dram[bass.ds(it.tail.times(1), 1)].rearrange("o l d -> (o l) d"), x2[:])\
                        .then_inc(x2_saved, 16)
                if it.has["next"] and (it.looped or it.i.off + 3 < B):
                    sp.wait_ge(xb_done, it.next.times(1, 1))
                    load_x(it.i.plus(3))

            for k in range(2):
                load_x(Batch(0, k))
                load_ctx(Batch(0, k))
            for k in (-2, -1, 0):
                step(Iteration(0, k))
            with sp.Fori(0, (B - 4) // 2) as r:
                step(Iteration(r, 1))
                step(Iteration(r, 2))
            for k in range(B - 3, B + 1):
                step(Iteration(0, k))
            sp.wait_ge(x2_saved, 16 * B)

        @block.gpsimd
        def _(pool):
            pool.memset(half[:], -0.5).then_inc(consts, 1)
            for h in range(2):
                pool.memset(nmax_c[h][:], 0.0).then_inc(consts, 1)
                pool.memset(ctxT[h][:, :, S:SP].bitcast(F32), 0.0).then_inc(consts, 1)
            pool.wait_ge(const_ld, 16 * N_CONST)
            pool.wait_ge(consts, 5)

            def block_diagonal(dst, src, t, done):
                for h in range(2):
                    ins = pool.tensor_tensor(
                        dst[h][:, OCT * t:OCT * (t + 1), :],
                        src[h][:, t:t + 1, :].bitcast(F32).broadcast_to([P, OCT, L]),
                        mask8[:].rearrange("p (h o) -> p h o", o=1).broadcast_to([P, OCT, L]), ALU.mult)
                ins.then_inc(done, 1)

            def inverse_root(k, n):
                pool.wait_ge(var_done[k], n.times(1, 1))
                pool.tensor_tensor(rstd[k][:], vare[k][:], half[0:L, :], ALU.pow).then_inc(rstd_done[k], 1)

            def step(it):
                if it.has["tail"]:
                    inverse_root(1, it.tail)
                if it.has["next"]:
                    pool.wait_ge(x_ld[it.next.par], it.next.loads())
                    if not (not it.looped and it.i.off < 0):
                        pool.wait_ge(x1_done, it.next.times(1))
                    pool.tensor_tensor(xb[:], x_in[it.next.par][:], brow["abo"][0:L, :], ALU.add)\
                        .then_inc(xb_done, 1)
                if it.has["pre"]:
                    wait_drain(pool, it, "Ks")
                    block_diagonal(Kbd, Ks, 0, kbd_done)
                    block_diagonal(Kbd, Ks, 1, kbd_done)
                if it.has["next"]:
                    inverse_root(0, it.next)
                    pool.wait_ge(x1_done, it.next.times(1, 1))
                    pool.tensor_tensor(x1b[it.next.par][:], x1[:], brow["xbo"][0:L, :], ALU.add)\
                        .then_inc(x1b_done, 1)
                    wait_drain(pool, it, "Qx")
                    block_diagonal(Qbd, Qx, 0, qbd_done)
                    block_diagonal(Qbd, Qx, 1, qbd_done)

            pairs_loop(pool, step)

        @block.scalar
        def _(act):
            for n in names[4:]:
                act.dma_start(w[n] if n in early else w[n][:], a[n].rearrange("(k p) n -> p k n", p=P)).then_inc(const_ld, 16)
            for n, src in rows.items():
                act.dma_start(brow[n][:], a[src].rearrange("(o n) -> o n", o=1).broadcast_to([P, D]))\
                    .then_inc(const_ld, 16)
            for dst, src in ((mask8, "mask8"), (even_odd, "even_odd"), (sel_raw, "sel"),
                             (alibi_l, "alibi_l"), (alibi_r, "alibi_r")):
                act.dma_start(dst if src == "sel" else dst[:], a[src]).then_inc(const_ld, 16)
            act.wait_ge(const_ld, 16 * N_CONST)
            act.activation(warm[:, 0:1], mask8[:, 0:1], ACT.Exp)
            for n in ("xWk", "xWv"):
                act.activation(split[n][0][:], w[n], ACT.Copy).then_inc(consts, 1)
            act.activation(sel[:], sel_raw, ACT.Copy).then_inc(consts, 1)

            def exp_units(n, t):
                act.wait_ge(nmax_s_done, n.times(KT, t + 1))
                for h in range(OCT):
                    g = OCT * t + h
                    ins = act.activation(Ps[:, g, :], score[0][0:L, h // QUAD, (h % QUAD) * L:(h % QUAD + 1) * L],
                                         ACT.Exp, bias=nmax_s[:, g:g + 1], accum_out=Zs[:, g:g + 1])
                ins.then_inc(exp_s, 1)

            def exp_cross(n, u, slot):
                act.wait_ge(shifted, n.times(NU, u + 1))
                act.activation(Px[u % 2][:].rearrange("s (q h) l -> s q (h l)", q=2), score[slot][0:C, :, 0:QW],
                               ACT.Exp).then_inc(exp_c, 1)

            def copy_max(n, u):
                act.wait_ge(nmaxT_done, n.times(NU, u + 1))
                act.activation(nmaxT[u % 2][:, 0:C], maxT[:, u % 2, 0:C], ACT.Copy).then_inc(nmaxT_copied, 1)

            def hi_with_bias(it, use, dst, bias, cols, done):
                wait_fill(act, it, use)
                for m in range(KT):
                    ins = act.activation(dst[:, m, :], work[BANK_OF[use]][:, m * L:(m + 1) * L], ACT.Identity,
                                         bias=bias[:, m:m + 1])
                ins.then_inc(done, 1)

            def drain_copy(it, use, dst, rows_, cols):
                b = BANK_OF[use]
                wait_fill(act, it, use)
                act.activation(dst, work[b][0:rows_, 0:cols], ACT.Copy).then_inc(drained[b], 1)

            def even_heads(it, use, t):
                wait_fill(act, it, use)
                act.activation(evenT[:, t, :], work[BANK_OF[use]][:, 0:L], ACT.Copy,
                               scale=even_odd[:, 0:1]).then_inc(even_s, 1)

            def step(it):
                i, n, tail = it.i, it.next, it.tail
                if it.has["tail"]:
                    exp_cross(tail, NU - 1, 1)
                if it.has["next"]:
                    for k in range(KT):
                        wait_fill(act, it, f"ctxT{k}")
                        act.activation(ctxT[0][:, k, 0:S], work[BANK_OF[f"ctxT{k}"]][:, 0:S], ACT.Copy)\
                            .then_inc(ctx_hi, 1)
                    exp_units(n, 0)
                if it.has["tail"]:
                    act.wait_ge(av_done, tail.times(NU, NU))
                    act.activation(evenX[:], outX[:, :, 0:L], ACT.Copy, scale=even_odd[:, 0:1]).then_inc(even_x, 1)
                if it.has["next"]:
                    for m in range(KT):
                        use = f"K{m}"
                        wait_fill(act, it, use)
                        act.activation(KxT[n.par][0][:, m, :], work[BANK_OF[use]][:, 0:S], ACT.Identity,
                                       bias=bcol["xbk"][:, m:m + 1]).then_inc(kx_hi, 1)
                    for j in range(2):
                        drain_copy(it, f"PT{j}", PsT[:, QUAD * j:QUAD * (j + 1), :].rearrange("k h q -> k (h q)"), L, QW)
                if it.has["cross"]:
                    copy_max(i, 0)
                    exp_cross(i, 0, 1)
                if it.has["next"]:
                    exp_units(n, 1)
                    even_heads(it, "AVs0", 0)
                if it.has["pre"]:
                    drain_copy(it, "xTs", xT[:].rearrange("p k l -> p (k l)"), P, KT * L)
                if it.has["cross"]:
                    copy_max(i, 1)
                    exp_cross(i, 1, 1)
                if it.has["next"]:
                    for j in range(2, 4):
                        drain_copy(it, f"PT{j}", PsT[:, QUAD * j:QUAD * (j + 1), :].rearrange("k h q -> k (h q)"), L, QW)
                if it.has["cross"]:
                    copy_max(i, 2)
                if it.has["pre"]:
                    hi_with_bias(it, "Ks", Ks[0], bcol["abk"], L, ks_hi)
                if it.has["cross"]:
                    exp_cross(i, 2, 0)
                if it.has["next"]:
                    even_heads(it, "AVs1", 1)
                if it.has["pre"]:
                    hi_with_bias(it, "Qs", Qs[0], bcol["abq"], L, qs_hi)
                if it.has["cross"]:
                    copy_max(i, 3)
                    exp_cross(i, 3, 1)
                if it.has["tail"]:
                    wait_fill(act, it, "x2T")
                    act.activation(x2T_all[:, :, bass.ds(tail.times(L), L)],
                                   work[BANK_OF["x2T"]][:, 0:KT * L].rearrange("p (k l) -> p k l", k=KT),
                                   ACT.Copy).then_inc(x2T_copied, 1)
                if it.has["cross"]:
                    copy_max(i, 4)
                    exp_cross(i, 4, 0)
                if it.has["next"]:
                    drain_copy(it, "x1T", x1T[:].rearrange("p k l -> p (k l)"), P, KT * L)
                    hi_with_bias(it, "Qx", Qx[0], bcol["xbq"], L, qx_hi)
                if it.has["cross"]:
                    copy_max(i, 5)

            pairs_loop(act, step)

        @block.vector
        def _(dve):
            dve.wait_ge(const_ld, 16 * N_CONST)
            for n in ("aWq", "xWq"):
                dve.tensor_scalar(w[n][:], w[n][:], SCALE, None, ALU.mult).then_inc(consts, 1)
            for n in ("abq", "xbq"):
                dve.tensor_scalar(bcol[n][:], bcol[n][:], SCALE, None, ALU.mult).then_inc(consts, 1)
            dve.wait_ge(consts, 12)
            for n in ("xWk", "xWv"):
                dve.tensor_tensor(split[n][1][:], w[n], split[n][0][:].bitcast(F32), ALU.subtract)\
                    .then_inc(consts, 1)

            def normalised_v(n, u):
                t, c = divmod(u, NC)
                p = u % 2
                dve.wait_ge(exp_c, n.times(NU, u + 1))
                dve.tensor_reduce(Zc[p][:], Px[p][:], AX.X, ALU.add).then_inc(z_c, 1)
                dve.wait_ge(z_c, n.times(NU, u + 1))
                dve.reciprocal(rZc[p][:], Zc[p][:]).then_inc(rz_c, 1)
                dve.wait_ge(rz_c, n.times(NU, u + 1))
                dve.tensor_tensor(Vn[p][:], Vx[n.par][:, c, P * t:P * (t + 1)].rearrange("s (h e) -> s h e", h=OCT),
                                  rZc[p][:].rearrange("s (h o) -> s h o", o=1).broadcast_to([C, OCT, HD]), ALU.mult)\
                    .then_inc(vn_done, 1)

            def max_cross(n, u, slot):
                dve.wait_ge(scores_c, n.times(NU, u + 1))
                dve.tensor_reduce(nmax_c[u % 2][:, 0:OCT].rearrange("s (q h) -> s q h", q=2),
                                  score[slot][0:C, :, 0:QW].rearrange("s q (h l) -> s q h l", h=QUAD),
                                  AX.X, ALU.max, negate=True).then_inc(nmax_c_done, 1)

            def max_self(n, t):
                dve.wait_ge(scores_s, n.times(KT, t + 1))
                dve.tensor_reduce(nmax_s[:, OCT * t:OCT * (t + 1)].rearrange("s (q h) -> s q h", q=2),
                                  score[0][0:L, :, 0:QW].rearrange("s q (h l) -> s q h l", h=QUAD),
                                  AX.X, ALU.max, negate=True).then_inc(nmax_s_done, 1)

            def lo_with_bias(it, use, dst, hi, bias, hi_sem, n):
                b = BANK_OF[use]
                dve.wait_ge(hi_sem, n.times(1, 1))
                for m in range(KT):
                    ins = dve.scalar_tensor_tensor(dst[:, m, :], work[b][:, m * L:(m + 1) * L], bias[:, m:m + 1],
                                                   hi[:, m, :].bitcast(F32), ALU.add, ALU.subtract)
                ins.then_inc(drained[b], 1)

            def add_bias(it, use, dst, rows_, bias):
                b = BANK_OF[use]
                wait_fill(dve, it, use)
                dve.tensor_tensor(dst, work[b][0:rows_, 0:D], bias, ALU.add).then_inc(drained[b], 1)

            def reciprocal_self(n, t):
                dve.wait_ge(exp_s, n.times(KT, t + 1))
                h = slice(OCT * t, OCT * (t + 1))
                dve.reciprocal(rZs[:, h], Zs[:, h]).then_inc(rz_s, 1)
                dve.wait_ge(rz_s, n.times(KT, t + 1))
                dve.tensor_copy(rZrep[:, t], rZs[:, h].rearrange("q (h o) -> q h o", o=1).broadcast_to([L, OCT, HD]))\
                    .then_inc(rzrep_s, 1)

            def combine_self(it, use, t):
                n, b = it.next, BANK_OF[use]
                dve.wait_ge(even_s, n.times(KT, t + 1))
                dve.scalar_tensor_tensor(sumT[:, t, :], work[b][:, L:2 * L], even_odd[:, 1:2], evenT[:, t, :],
                                         ALU.mult, ALU.add).then_inc(sum_s, 1)
                dve.wait_ge(sum_s, n.times(KT, t + 1))
                dve.tensor_tensor(attnT[:, t, :], sumT[:, t, :], work[b][:, 2 * L:3 * L], ALU.mult)\
                    .then_inc(drained[b], 1)

            def residual_stats(it, use, k, r, xb_, n):
                b = BANK_OF[use]
                wait_fill(dve, it, use)
                dve.tensor_tensor(r[:], work[b][0:L, 0:D], xb_[:], ALU.add).then_inc(drained[b], 1)
                wait_drain(dve, it, use)
                dve.bn_stats(stats[k][:], r[:]).then_inc(bn_done[k], 1)
                dve.wait_ge(bn_done[k], n.times(1, 1))
                dve.memset(carrier[:], 0.0)
                dve.bn_aggr(mv[k][:], stats[k][:]).then_inc(mv_done[k], 1)
                dve.wait_ge(mv_done[k], n.times(1, 1))
                dve.tensor_scalar(vare[k][:], mv[k][:, 1:2], EPS, None, ALU.add).then_inc(var_done[k], 1)

            def step(it):
                i, n, w_, tail = it.i, it.next, it.pre, it.tail
                if it.has["tail"]:
                    normalised_v(tail, NU - 1)
                if it.has["next"]:
                    max_self(n, 0)
                    for k in range(KT):
                        b = BANK_OF[f"ctxT{k}"]
                        dve.wait_ge(ctx_hi, n.times(KT, k + 1))
                        dve.tensor_tensor(ctxT[1][:, k, 0:S], work[b][:, 0:S], ctxT[0][:, k, 0:S].bitcast(F32),
                                          ALU.subtract).then_inc(drained[b], 1)
                    for m in range(KT):
                        b = BANK_OF[f"K{m}"]
                        dve.wait_ge(kx_hi, n.times(KT, m + 1))
                        dve.scalar_tensor_tensor(KxT[n.par][1][:, m, :], work[b][:, 0:S], bcol["xbk"][:, m:m + 1],
                                                 KxT[n.par][0][:, m, :].bitcast(F32), ALU.add, ALU.subtract)\
                            .then_inc(drained[b], 1)
                if it.has["tail"]:
                    dve.wait_ge(even_x, tail.times(1, 1))
                    dve.scalar_tensor_tensor(OxT[:], outX[:, :, L:2 * L], even_odd[:, 1:2], evenX[:],
                                             ALU.mult, ALU.add).then_inc(oxT_done, 1)
                if it.has["cross"]:
                    max_cross(i, 0, 1)
                if it.has["next"]:
                    reciprocal_self(n, 0)
                    add_bias(it, "V0", Vx[n.par][:, 0, :], C, brow["xbv"][0:C, :])
                    max_self(n, 1)
                if it.has["cross"]:
                    normalised_v(i, 0)
                if it.has["tail"]:
                    if it.looped or it.tail.off > 0:
                        dve.wait_ge(x2_saved, tail.times(16))
                    dve.wait_ge(x1b_done, tail.times(1, 1))
                    residual_stats(it, "Ox", 1, r2, x1b[tail.par], tail)
                if it.has["next"]:
                    combine_self(it, "AVs0", 0)
                    if it.has["cross"]:
                        max_cross(i, 1, 1)
                    add_bias(it, "V1", Vx[n.par][:, 1, :], C, brow["xbv"][0:C, :])
                elif it.has["cross"]:
                    max_cross(i, 1, 1)
                if it.has["tail"]:
                    dve.wait_ge(rstd_done[1], tail.times(1, 1))
                    dve.tensor_scalar(x2[:], r2[:], mv[1][:, 0:1], rstd[1][:, 0:1], ALU.subtract, ALU.mult)\
                        .then_inc(x2_done, 1)
                if it.has["cross"]:
                    max_cross(i, 2, 0)
                    normalised_v(i, 1)
                if it.has["pre"]:
                    lo_with_bias(it, "Ks", Ks[1], Ks[0], bcol["abk"], ks_hi, w_)
                if it.has["next"]:
                    reciprocal_self(n, 1)
                if it.has["cross"]:
                    max_cross(i, 3, 1)
                if it.has["next"]:
                    combine_self(it, "AVs1", 1)
                if it.has["pre"]:
                    lo_with_bias(it, "Qs", Qs[1], Qs[0], bcol["abq"], qs_hi, w_)
                if it.has["cross"]:
                    normalised_v(i, 2)
                if it.has["next"]:
                    add_bias(it, "V2", Vx[n.par][:, 2, :], C, brow["xbv"][0:C, :])
                    dve.wait_ge(xb_done, n.times(1, 1))
                    residual_stats(it, "Os", 0, r1, xb, n)
                if it.has["cross"]:
                    max_cross(i, 4, 0)
                if it.has["tail"]:
                    b = BANK_OF["x2T"]
                    dve.wait_ge(x2T_copied, tail.times(1, 1))
                    dve.tensor_reduce(xmax_all[:, bass.ds(tail.times(1), 1)], work[b][:, 0:KT * L], AX.X, ALU.max,
                                      apply_absolute_value=True).then_inc(drained[b], 1)
                if it.has["cross"]:
                    normalised_v(i, 3)
                if it.has["next"]:
                    dve.wait_ge(rstd_done[0], n.times(1, 1))
                    dve.tensor_scalar(x1[:], r1[:], mv[0][:, 0:1], rstd[0][:, 0:1], ALU.subtract, ALU.mult)\
                        .then_inc(x1_done, 1)
                if it.has["pre"]:
                    add_bias(it, "Vs", Vs[:], L, brow["abv"][0:L, :])
                if it.has["next"]:
                    lo_with_bias(it, "Qx", Qx[1], Qx[0], bcol["xbq"], qx_hi, n)
                if it.has["cross"]:
                    max_cross(i, 5, 1)
                    normalised_v(i, 4)

            pairs_loop(dve, step)

        @block.tensor
        def _(pe):
            pe.wait_ge(consts, 14)

            def fill(it, use):
                wait(pe, drained[BANK_OF[use]], it.fills(use))
                return work[BANK_OF[use]]

            def three(dst, lhs, rhs, first, last):
                pe.matmul(dst, lhs[0], rhs[0], start=first, stop=False)
                pe.matmul(dst, lhs[0], rhs[1], start=False, stop=False)
                return pe.matmul(dst, lhs[1], rhs[0], start=False, stop=last)

            def transpose_rows(it, use, src, rows_):
                b = fill(it, use)
                for k in range(KT):
                    ins = pe.transpose(b[:, k * L:(k + 1) * L], src[:, k * P:(k + 1) * P], ident[0:rows_, 0:rows_])
                ins.then_inc(filled[BANK_OF[use]], 1)

            def project_T(it, use, weight, src):
                b = fill(it, use)
                for m in range(KT):
                    for k in range(KT):
                        ins = pe.matmul(b[:, m * L:(m + 1) * L], weight[:, k, m * P:(m + 1) * P], src[:, k, :],
                                        start=(k == 0), stop=(k == KT - 1))
                ins.then_inc(filled[BANK_OF[use]], 1)

            def project(it, use, srcT, weight):
                b = fill(it, use)
                for k in range(KT):
                    ins = pe.matmul(b[0:L, 0:D], srcT[:, k, :], weight[:, k, :], start=(k == 0), stop=(k == KT - 1))
                ins.then_inc(filled[BANK_OF[use]], 1)

            def values_ready(it):
                return Iteration(it.i.pair, it.i.off - 1).fills("Vs") + 1

            def self_scores(it, t):
                n = it.next
                if t == 0:
                    wait(pe, exp_c, it.i.times(NU, -1) if it.has["cross"] else 0)
                    wait(pe, drained[BANK_OF["Vs"]], values_ready(it))
                else:
                    pe.wait_ge(exp_s, n.times(KT, 1))
                pe.wait_ge(kbd_done, n.times(KT, t + 1))
                for q in range(2):
                    j = 2 * t + q
                    dst = score[0][0:L, q, 0:QW]
                    pe.matmul(dst, alibi_l[:], alibi_r[:, j * QW:(j + 1) * QW], start=True, stop=False)
                    rhs = [x[:, QUAD * j:QUAD * (j + 1), :].rearrange("p h k -> p (h k)") for x in Kbd]
                    ins = three(dst, [x[:, t, :] for x in Qs], rhs, False, True)
                ins.then_inc(scores_s, 1)

            def cross_scores(it, u, slot, before):
                t, c = divmod(u, NC)
                i = it.i
                wait(pe, *before)
                if c == 0:
                    pe.wait_ge(qbd_done, i.times(KT, t + 1))
                for q in range(2):
                    j = 2 * t + q
                    rhs = [x[:, QUAD * j:QUAD * (j + 1), :].rearrange("p h l -> p (h l)") for x in Qbd]
                    dst = score[slot][0:C, q, 0:QW]
                    lhs = [x[:, t, c * C:(c + 1) * C] for x in KxT[i.par]]
                    ins = three(dst, lhs, rhs, True, True)
                ins.then_inc(scores_c, 1)

            def transpose_max(it, u):
                i = it.i
                pe.wait_ge(nmax_c_done, i.times(NU, u + 1))
                pe.transpose(maxT[:, u % 2, 0:C], nmax_c[u % 2][:], ident[0:C, 0:C]).then_inc(nmaxT_done, 1)

            def shift(it, u, slot):
                i = it.i
                pe.wait_ge(nmaxT_copied, i.times(NU, u + 1))
                for q in range(2):
                    ins = pe.matmul(score[slot][0:C, q, 0:QW], nmaxT[u % 2][:, 0:C], sel[:, q * QW:(q + 1) * QW],
                                    start=False, stop=True, skip_group_check=True)
                ins.then_inc(shifted, 1)

            def cross_values(n, u):
                t, c = divmod(u, NC)
                pe.wait_ge(vn_done, n.times(NU, u + 1))
                if u == 0:
                    wait(pe, oxT_done, n.times(1))
                for g in range(4):
                    ins = pe.matmul(outX[32 * g:32 * (g + 1), t, :],
                                    Vn[u % 2][:, 2 * g:2 * g + 2, :].rearrange("s h e -> s (h e)"),
                                    Px[u % 2][:, 2 * g:2 * g + 2, :].rearrange("s h l -> s (h l)"),
                                    start=(c == 0), stop=(c == NC - 1))
                ins.then_inc(av_done, 1)

            def transpose_ctx(it, k):
                n, use = it.next, f"ctxT{k}"
                b = fill(it, use)
                pe.wait_ge(ctx_ld[n.par], n.loads())
                for c in range(NC):
                    ins = pe.transpose(b[:, c * C:(c + 1) * C], ctx_in[n.par][:, c, k * P:(k + 1) * P], ident[0:C, 0:C])
                ins.then_inc(filled[BANK_OF[use]], 1)

            def keys_cross(it, m):
                use = f"K{m}"
                b = fill(it, use)
                if m == 0:
                    wait_drain(pe, it, "ctxT0")
                    wait_drain(pe, it, "ctxT1")
                for k in range(KT):
                    ins = three(b[:, 0:SP], [x[:, k, m * P:(m + 1) * P] for x in split["xWk"]],
                                [x[:, k, :] for x in ctxT], k == 0, k == KT - 1)
                ins.then_inc(filled[BANK_OF[use]], 1)

            def values_ctx(it, c):
                use = f"V{c}"
                b = fill(it, use)
                for k in range(KT):
                    ins = three(b[0:C, 0:D], [x[:, k, c * C:(c + 1) * C] for x in ctxT],
                                [x[:, k, :] for x in split["xWv"]], k == 0, k == KT - 1)
                ins.then_inc(filled[BANK_OF[use]], 1)

            def transpose_probs(it, j):
                use = f"PT{j}"
                b = fill(it, use)
                pe.wait_ge(exp_s, it.next.times(KT, j // 2 + 1))
                for h in range(QUAD):
                    ins = pe.transpose(b[0:L, h * L:(h + 1) * L], Ps[:, QUAD * j + h, :], ident[0:L, 0:L])
                ins.then_inc(filled[BANK_OF[use]], 1)

            def self_values(it, t):
                use = f"AVs{t}"
                b = fill(it, use)
                wait_drain(pe, it, f"PT{2 * t}")
                wait_drain(pe, it, f"PT{2 * t + 1}")
                pe.wait_ge(rzrep_s, it.next.times(KT, t + 1))
                pe.transpose(b[:, 2 * L:3 * L], rZrep[:, t].rearrange("q h e -> q (h e)"), ident[0:L, 0:L])
                for g in range(4):
                    h = OCT * t + 2 * g
                    ins = pe.matmul(b[32 * g:32 * (g + 1), 0:2 * L], Vs[:, h * HD:(h + 2) * HD],
                                    PsT[:, h:h + 2, :].rearrange("k h q -> k (h q)"), start=True, stop=True)
                ins.then_inc(filled[BANK_OF[use]], 1)

            def step(it):
                i, n, tail = it.i, it.next, it.tail
                has = it.has
                if has["next"]:
                    self_scores(it, 0)
                    transpose_ctx(it, 0)
                    transpose_ctx(it, 1)
                if has["tail"]:
                    cross_values(tail, NU - 1)
                if has["next"]:
                    keys_cross(it, 0)
                    keys_cross(it, 1)
                if has["cross"]:
                    cross_scores(it, 0, 1, (exp_c, i.times(NU)))
                if has["next"]:
                    transpose_probs(it, 0)
                    transpose_probs(it, 1)
                if has["cross"]:
                    transpose_max(it, 0)
                if has["next"]:
                    values_ctx(it, 0)
                if has["cross"]:
                    shift(it, 0, 1)
                if has["next"]:
                    self_scores(it, 1)
                if has["tail"]:
                    pe.wait_ge(oxT_done, tail.times(1, 1))
                    project(it, "Ox", OxT, w["xWo"])
                if has["next"]:
                    self_values(it, 0)
                if has["cross"]:
                    cross_scores(it, 1, 1, (exp_c, i.times(NU, 1)))
                if has["next"]:
                    values_ctx(it, 1)
                if has["pre"]:
                    pe.wait_ge(x_ld[it.pre.par], it.pre.loads())
                    transpose_rows(it, "xTs", x_in[it.pre.par], L)
                if has["cross"]:
                    transpose_max(it, 1)
                    cross_values(i, 0)
                    shift(it, 1, 1)
                    cross_scores(it, 2, 0, (exp_s, n.times(KT, KT)) if has["next"] else (exp_c, i.times(NU, -1)))
                if has["next"]:
                    transpose_probs(it, 2)
                    transpose_probs(it, 3)
                if has["cross"]:
                    transpose_max(it, 2)
                if has["pre"]:
                    wait_drain(pe, it, "xTs")
                    project_T(it, "Ks", w["aWk"], xT)
                if has["cross"]:
                    shift(it, 2, 0)
                    cross_values(i, 1)
                    cross_scores(it, 3, 1, (exp_c, i.times(NU, 2)))
                if has["next"]:
                    self_values(it, 1)
                if has["pre"]:
                    project_T(it, "Qs", w["aWq"], xT)
                if has["cross"]:
                    transpose_max(it, 3)
                if has["next"]:
                    values_ctx(it, 2)
                if has["cross"]:
                    shift(it, 3, 1)
                    cross_values(i, 2)
                if has["next"]:
                    wait_drain(pe, it, "AVs0")
                    wait_drain(pe, it, "AVs1")
                    project(it, "Os", attnT, w["aWo"])
                if has["cross"]:
                    cross_scores(it, 4, 0, (exp_c, i.times(NU, 3)))
                if has["tail"]:
                    pe.wait_ge(x2_done, tail.times(1, 1))
                    transpose_rows(it, "x2T", x2, L)
                if has["pre"]:
                    project(it, "Vs", xT, w["aWv"])
                if has["cross"]:
                    transpose_max(it, 4)
                    cross_values(i, 3)
                    shift(it, 4, 0)
                if has["next"]:
                    pe.wait_ge(x1_done, n.times(1, 1))
                    transpose_rows(it, "x1T", x1, L)
                if has["cross"]:
                    cross_scores(it, 5, 1, (exp_c, i.times(NU, 4)))
                if has["next"]:
                    wait_drain(pe, it, "x1T")
                    project_T(it, "Qx", w["xWq"], x1T)
                if has["cross"]:
                    transpose_max(it, 5)
                    cross_values(i, 4)
                    shift(it, 5, 1)

            pairs_loop(pe, step)


def feed_forward(nc, out, x2_dram, ident, x2T_all, xmax_all, wT, w_down):
    with ExitStack() as keep:
        U = keep.enter_context(nc.sbuf_tensor("U", [P, NG, FT, GT], F32))
        up_q = keep.enter_context(nc.sbuf_tensor("up_q", [P, NG, FT, GT], I16))
        tiny = {n: keep.enter_context(nc.sbuf_tensor(n, [P, 1], F32)) for n in (
            "x_scale", "x_inv", "up_scale", "up_inv", "gate_scale", "gate_inv",
            "glu_unit", "glu_scale", "glu_inv", "h_unit", "h_scale", "h_inv")}
        ones = keep.enter_context(nc.sbuf_tensor("ones", [P, P], F32))
        up_and_gate(nc, x2T_all, xmax_all, wT, ident, ones, U, up_q, tiny)
        gate_and_down(nc, out, x2_dram, x2T_all, ident, ones, wT, w_down, U, up_q, tiny)


class GlobalMax:

    def __init__(self, ctx, nc, name, ones, ident, bank):
        self.ones, self.ident, self.bank = ones, ident, bank
        self.diag = ctx.enter_context(nc.sbuf_tensor(f"{name}_diag", [P, P], F32))
        self.col = ctx.enter_context(nc.sbuf_tensor(f"{name}_col", [P, 1], F32))
        self.top = ctx.enter_context(nc.sbuf_tensor(f"{name}_top", [P, 1], F32))
        self.col_done = ctx.enter_context(nc.semaphore(f"{name}_col_done"))
        self.diag_done = ctx.enter_context(nc.semaphore(f"{name}_diag_done"))
        self.spread = ctx.enter_context(nc.semaphore(f"{name}_spread"))
        self.top_done = ctx.enter_context(nc.semaphore(f"{name}_top_done"))

    def vector(self, dve, maxima):
        dve.tensor_reduce(self.col[:], maxima, AX.X, ALU.max).then_inc(self.col_done, 1)
        dve.wait_ge(self.col_done, 1)
        dve.tensor_scalar(self.diag[:], self.ident[:], self.col[:, 0:1], None, ALU.mult).then_inc(self.diag_done, 1)
        dve.wait_ge(self.spread, 1)
        dve.tensor_reduce(self.top[:], self.bank, AX.X, ALU.max).then_inc(self.top_done, 1)
        dve.wait_ge(self.top_done, 1)

    def tensor(self, pe):
        pe.wait_ge(self.diag_done, 1)
        pe.matmul(self.bank, self.ones[:], self.diag[:], start=True, stop=True).then_inc(self.spread, 1)


def up_and_gate(nc, x2T_all, xmax_all, wT, ident, ones, U, up_q, tiny):
    with ExitStack() as ctx:
        def sb(name, shape, dt=F32):
            return ctx.enter_context(nc.sbuf_tensor(name, shape, dt))

        def sem(name):
            return ctx.enter_context(nc.semaphore(name))

        xq = sb("xq", [P, KT, GT], I16)
        xh = [[sb(f"xq{q}_{p}", [P, KT, GT], F32R) for p in ("hi", "lo")] for q in range(2)]
        maxima = [sb(f"maxima{p}", [P, NG]) for p in range(2)]
        bank = [ctx.enter_context(nc.psum_tensor(f"ubank{m}", [P, BANK], F32)) for m in range(FT)]
        spread = [ctx.enter_context(nc.psum_tensor(f"spread{p}", [P, BANK], F32)) for p in range(2)]
        ones_done, x_inv_done, steps = sem("ones_done"), sem("x_inv_done"), sem("steps")
        xq_done, xpart_done = sem("xq_done"), sem("xpart_done")
        x_parts = sem("x_parts")
        product = [sem(f"product{m}") for m in range(FT)]
        stored = [sem(f"stored{m}") for m in range(FT)]
        maxed = sem("maxed")
        up_q_done = sem("up_q_done")
        top = [GlobalMax(ctx, nc, n, ones, ident, spread[k % 2][:, 0:P])
               for k, n in enumerate(("x_top", "up_top", "gate_top"))]
        block = ctx.enter_context(nc.Block())

        def xpart(g, part_):
            return x2T_all[:].bitcast(I16)[:, :, bass.ds(g.times(2 * GT, part_ * GT), GT)]

        class Group:
            def __init__(self, which, pair, off):
                self.which, self.pair, self.off, self.par = which, pair, off, off % 2
                self.g = Batch(pair, off)

            def count(self, more=0):
                return self.g.times(1, NG * self.which + more)

        def groups(eng, which, step):
            if which == 0:
                step(Group(0, 0, 0))
                step(Group(0, 0, 1))
                with eng.Fori(0, NG // 2 - 1) as r:
                    step(Group(0, r, 2))
                    step(Group(0, r, 3))
            else:
                with eng.Fori(0, NG // 2) as r:
                    step(Group(1, r, 0))
                    step(Group(1, r, 1))

        @block.gpsimd
        def _(pool):
            pool.memset(ones[:], 1.0).then_inc(ones_done, 1)

        @block.scalar
        def _(act):
            def float_parts(g, par, made, used):
                if made is not None:
                    act.wait_ge(xpart_done, made)
                wait(act, product[FT - 1], used)
                act.activation(xh[par][0][:], xpart(g, 0), ACT.Copy)
                act.activation(xh[par][1][:], xpart(g, 1), ACT.Copy).then_inc(x_parts, 1)

            def step(s, wraps=False, last=False):
                if not last:
                    float_parts(Batch(0, 0) if wraps else s.g.plus(1), 1 - s.par,
                            s.count(2) if s.which == 0 and not wraps else None, s.count())
                if s.which == 1:
                    act.wait_ge(up_q_done, s.g.times(1, 1))
                for m in range(FT):
                    act.wait_ge(product[m], s.count(1))
                    act.activation(U[:, bass.ds(s.g.times(1), 1), m, :].rearrange("p o t -> p (o t)"),
                                   bank[m][:, 0:GT], ACT.Copy).then_inc(stored[m], 1)

            float_parts(Batch(0, 0), 0, 1, 0)
            step(Group(0, 0, 0))
            step(Group(0, 0, 1))
            with act.Fori(0, NG // 2 - 2) as r:
                step(Group(0, r, 2))
                step(Group(0, r, 3))
            step(Group(0, 0, NG - 2))
            step(Group(0, 0, NG - 1), wraps=True)
            with act.Fori(0, NG // 2 - 1) as r:
                step(Group(1, r, 0))
                step(Group(1, r, 1))
            step(Group(1, 0, NG - 2))
            step(Group(1, 0, NG - 1), last=True)

        @block.vector
        def _(dve):
            def quantiser(top_, scale, inv, base):
                dve.tensor_scalar(tiny[scale][:], top_.top[:], 1.0 / QMAX, TINY, ALU.mult, ALU.max).then_inc(steps, 1)
                dve.wait_ge(steps, base + 1)
                dve.reciprocal(tiny[inv][:], tiny[scale][:]).then_inc(steps, 1)
                dve.wait_ge(steps, base + 2)

            def quantise_x(g, count):
                wait(dve, xpart_done, count)
                dve.tensor_scalar(xq[:], x2T_all[:, :, bass.ds(g.times(GT), GT)], tiny["x_inv"][:, 0:1], None,
                                  ALU.mult).then_inc(xq_done, 1)
                dve.wait_ge(xq_done, count + 1)
                dve.tensor_scalar(xpart(g, 0), xq[:], HIGH, None, ALU.bitwise_and)
                dve.tensor_scalar(xpart(g, 1), xq[:], LOW, None, ALU.bitwise_and).then_inc(xpart_done, 1)

            def step(s, ahead=True):
                if s.which == 0 and ahead:
                    quantise_x(s.g.plus(1), s.count(1))
                if s.which == 1:
                    dve.tensor_scalar(up_q[:, bass.ds(s.g.times(1), 1)], U[:, bass.ds(s.g.times(1), 1)],
                                      tiny["up_inv"][:, 0:1], None, ALU.mult).then_inc(up_q_done, 1)
                dve.wait_ge(stored[FT - 1], s.count(1))
                dve.tensor_reduce(maxima[s.which][:, bass.ds(s.g.times(1), 1)], U[:, bass.ds(s.g.times(1), 1)],
                                  AX.XYZ, ALU.max, apply_absolute_value=True).then_inc(maxed, 1)

            top[0].vector(dve, xmax_all[:])
            quantiser(top[0], "x_scale", "x_inv", 0)
            quantise_x(Batch(0, 0), 0)
            step(Group(0, 0, 0))
            step(Group(0, 0, 1))
            with dve.Fori(0, NG // 2 - 2) as r:
                step(Group(0, r, 2))
                step(Group(0, r, 3))
            step(Group(0, 0, NG - 2))
            step(Group(0, 0, NG - 1), ahead=False)
            dve.wait_ge(maxed, NG)
            top[1].vector(dve, maxima[0][:])
            dve.tensor_scalar(tiny["up_scale"][:], top[1].top[:], tiny["x_scale"][:, 0:1], None, ALU.mult)\
                .then_inc(steps, 1)
            dve.wait_ge(steps, 3)
            dve.tensor_scalar(tiny["up_scale"][:], tiny["up_scale"][:], 1.0 / QMAX, TINY, ALU.mult, ALU.max)\
                .then_inc(steps, 1)
            dve.wait_ge(steps, 4)
            dve.reciprocal(tiny["up_inv"][:], tiny["up_scale"][:]).then_inc(steps, 1)
            dve.wait_ge(steps, 5)
            dve.tensor_scalar(tiny["up_inv"][:], tiny["up_inv"][:], tiny["x_scale"][:, 0:1], None, ALU.mult)\
                .then_inc(steps, 1)
            dve.wait_ge(steps, 6)
            groups(dve, 1, step)
            dve.wait_ge(maxed, 2 * NG)
            top[2].vector(dve, maxima[1][:])
            dve.tensor_scalar(tiny["gate_scale"][:], top[2].top[:], tiny["x_scale"][:, 0:1], None, ALU.mult)\
                .then_inc(steps, 1)
            dve.wait_ge(steps, 7)
            dve.tensor_scalar(tiny["gate_scale"][:], tiny["gate_scale"][:], 1.0 / QMAX, TINY, ALU.mult, ALU.max)\
                .then_inc(steps, 1)
            dve.wait_ge(steps, 8)
            dve.reciprocal(tiny["gate_inv"][:], tiny["gate_scale"][:]).then_inc(steps, 1)
            dve.wait_ge(steps, 9)
            dve.tensor_scalar(tiny["gate_inv"][:], tiny["gate_inv"][:], tiny["x_scale"][:, 0:1], None, ALU.mult)\
                .then_inc(steps, 1)

        @block.tensor
        def _(pe):
            def step(s):
                w = wT["w_up" if s.which == 0 else "w_gate"]
                pe.wait_ge(x_parts, s.count(1))
                for m in range(FT):
                    wait(pe, stored[m], s.count())
                    for k in range(KT):
                        lhs = [x[:, k, m * P:(m + 1) * P] for x in w]
                        rhs = [x[:, k, :] for x in xh[s.par]]
                        dst = bank[m][:, 0:GT]
                        pe.matmul(dst, lhs[0], rhs[0], start=(k == 0), stop=False)
                        pe.matmul(dst, lhs[0], rhs[1], start=False, stop=False)
                        ins = pe.matmul(dst, lhs[1], rhs[0], start=False, stop=(k == KT - 1))
                    ins.then_inc(product[m], 1)

            pe.wait_ge(ones_done, 1)
            top[0].tensor(pe)
            groups(pe, 0, step)
            top[1].tensor(pe)
            groups(pe, 1, step)
            top[2].tensor(pe)


def gate_and_down(nc, out, x2_dram, x2T_all, ident, ones, wT, w_down, U, up_q, tiny):
    TG = GT // L
    with ExitStack() as ctx:
        def sb(name, shape, dt=F32):
            return ctx.enter_context(nc.sbuf_tensor(name, shape, dt))

        def sem(name):
            return ctx.enter_context(nc.semaphore(name))

        HG = FT // 2
        flat = {n: [t[:].rearrange("p k n -> p (k n)") for t in wT[n]] for n in wT}
        wd = [t.rearrange("p (m n) -> p m n", m=FT) for t in flat["w_up"]]
        room = x2T_all[:].rearrange("p k n -> p (k n)")
        sig = room[:, 0:HG * GT].rearrange("p (m t) -> p m t", m=HG)
        x2, r, res = ([room[0:L, HG * GT + (2 * k + p) * D:HG * GT + (2 * k + p + 1) * D] for p in range(2)]
                      for k in range(3))
        ints = [room[:, HG * GT + 6 * D + k * (HG * GT // 2):][:, 0:HG * GT // 2] for k in range(4)]
        gate_q = [v.bitcast(I16).rearrange("p (m t) -> p m t", m=HG) for v in ints[:2]]
        sig_q = [v.bitcast(U16).rearrange("p (m t) -> p m t", m=HG) for v in ints[2:]]
        maxima = [sb(f"hmaxima{p}", [P, 2 * NG]) for p in range(2)]
        hq = sb("hq", [P, FT, L], I16)
        hpart = [[sb(f"hpart{q}_{p}", [P, FT, L], I16) for p in ("hi", "lo")] for q in range(2)]
        hh = [[t[:, q * FT * L:(q + 1) * FT * L].rearrange("p (m t) -> p m t", m=FT) for t in flat["w_gate"]]
              for q in range(2)]
        carrier = sb("fcarrier", [1, 1])
        stats = [sb(f"fstats{p}", [L, 6]) for p in range(2)]
        mv = [sb(f"fmv{p}", [L, 2]) for p in range(2)]
        vare = [sb(f"fvare{p}", [L, 1]) for p in range(2)]
        rstd = [sb(f"frstd{p}", [L, 1]) for p in range(2)]
        half = sb("fhalf", [L, 1])
        wbank = [ctx.enter_context(nc.psum_tensor(f"dbank{p}", [P, BANK], F32)) for p in range(2)]
        obank = [ctx.enter_context(nc.psum_tensor(f"obank{p}", [P, BANK], F32)) for p in range(4)]
        spread = [ctx.enter_context(nc.psum_tensor(f"dspread{p}", [P, BANK], F32)) for p in range(2)]
        half_done, steps = sem("half_done"), sem("dsteps")
        turned, hi_done, lo_done = sem("dturned"), sem("dhi_done"), sem("dlo_done")
        gate_q_done, sig_done, sig_q_done = sem("gate_q_done"), sem("sig_done"), sem("sig_q_done")
        glu_done, glu_maxed = sem("glu_done"), sem("glu_maxed")
        glu_q_done, h_done, h_maxed = sem("glu_q_done"), sem("h_done"), sem("h_maxed")
        hq_done, hpart_done, h_parts = sem("hq_done"), sem("hpart_done"), sem("h_parts")
        down_done, resid_done, fbn_done, fmv_done = sem("down_done"), sem("resid_done"), sem("fbn_done"), sem("fmv_done")
        fvar_done, frstd_done, res_done = sem("fvar_done"), sem("frstd_done"), sem("res_done")
        x2_ld = [sem(f"x2_ld{p}") for p in range(2)]
        out_st = [sem(f"out_st{p}") for p in range(2)]
        top = [GlobalMax(ctx, nc, n, ones, ident, spread[k][:, 0:P]) for k, n in enumerate(("glu_top", "h_top"))]
        glu_q = gate_q
        block = ctx.enter_context(nc.Block())
        NH = 2 * NG

        def part(t, pair, h):
            return t[:, bass.ds(pair, 1), h * HG:(h + 1) * HG, :].rearrange("p o m t -> p (o m) t")

        @block.sync
        def _(sp):
            def load(n, par):
                sp.dma_start(x2[par], x2_dram[bass.ds(n, 1)].rearrange("o l d -> (o l) d")).then_inc(x2_ld[par], 16)

            def store(n, par, count):
                sp.wait_ge(res_done, count)
                sp.dma_start(out[bass.ds(n, 1)].rearrange("o l d -> (o l) d"), res[par]).then_inc(out_st[par], 16)

            load(0, 0)
            load(1, 1)
            with sp.Fori(0, B // 2 - 1) as q:
                for p in range(2):
                    sp.wait_ge(resid_done, q * 2 + (p + 1))
                    load(q * 2 + (p + 2), p)
                    store(q * 2 + p, p, q * 2 + (p + 1))
            for p in range(2):
                store(B - 2 + p, p, B - 1 + p)
            for p in range(2):
                sp.wait_ge(out_st[p], 16 * (B // 2))

        @block.gpsimd
        def _(pool):
            pool.memset(half[:], -0.5).then_inc(half_done, 1)
            pool.wait_ge(half_done, 1)

            def root(count, p):
                pool.wait_ge(fvar_done, count)
                pool.tensor_tensor(rstd[p][:], vare[p][:], half[:], ALU.pow).then_inc(frstd_done, 1)

            with pool.Fori(0, B // 2) as q:
                for p in range(2):
                    root(q * 2 + (p + 1), p)

        @block.scalar
        def _(act):
            for f in range(4):
                act.wait_ge(turned, f + 1)
                act.activation(wd[0][:, (f % 2) * HG:(f % 2 + 1) * HG, (f // 2) * P:(f // 2 + 1) * P],
                               wbank[f % 2][:, 0:HG * P].rearrange("p (m n) -> p m n", m=HG), ACT.Copy)\
                    .then_inc(hi_done, 1)

            def sigmoid(q, h, first):
                if not (first or isinstance(q, int)):
                    act.wait_ge(glu_done, q * 2 + (h - 1))
                act.activation(gate_q[h], part(U, q, h), ACT.Copy, scale=tiny["gate_inv"][:, 0:1]).then_inc(gate_q_done, 1)
                act.wait_ge(gate_q_done, q * 2 + (h + 1))
                if not first:
                    act.wait_ge(sig_q_done, q * 2 + h)
                act.activation(sig, gate_q[h], ACT.Sigmoid, scale=tiny["gate_scale"][:, 0:1]).then_inc(sig_done, 1)

            sigmoid(0, 0, True)
            sigmoid(0, 1, False)
            with act.Fori(1, NG) as q:
                sigmoid(q, 0, False)
                sigmoid(q, 1, False)

            def glu_ints(q, h, first):
                if not first:
                    act.wait_ge(h_done, q * 2 + (h - 1))
                act.activation(glu_q[h], part(U, q, h), ACT.Copy, scale=tiny["glu_inv"][:, 0:1])\
                    .then_inc(glu_q_done, 1)

            act.wait_ge(steps, 5)
            glu_ints(0, 0, True)
            glu_ints(0, 1, True)
            with act.Fori(1, NG) as q:
                glu_ints(q, 0, False)
                glu_ints(q, 1, False)

            def tile(q, p, first):
                act.wait_ge(hpart_done, q * 2 + (p + 1))
                if not first:
                    act.wait_ge(down_done, q * 2 + (p - 1))
                act.activation(hh[p][0], hpart[p][0][:], ACT.Copy)
                act.activation(hh[p][1], hpart[p][1][:], ACT.Copy).then_inc(h_parts, 1)

            tile(0, 0, True)
            tile(0, 1, True)
            with act.Fori(1, B // 2) as q:
                tile(q, 0, False)
                tile(q, 1, False)

        @block.vector
        def _(dve):
            for f in range(4):
                dst = [w[:, (f % 2) * HG:(f % 2 + 1) * HG, (f // 2) * P:(f // 2 + 1) * P] for w in wd]
                dve.wait_ge(hi_done, f + 1)
                dve.tensor_tensor(dst[1], wbank[f % 2][:, 0:HG * P].rearrange("p (m n) -> p m n", m=HG),
                                  dst[0].bitcast(F32), ALU.subtract).then_inc(lo_done, 1)

            def glu(q, h, first):
                dve.wait_ge(sig_done, q * 2 + (h + 1))
                dve.tensor_scalar(sig_q[h], sig, SIGQ, SIGQ - 1.0, ALU.mult, ALU.min).then_inc(sig_q_done, 1)
                dve.wait_ge(sig_q_done, q * 2 + (h + 1))
                dve.tensor_tensor(part(U, q, h), gate_q[h], sig_q[h], ALU.mult).then_inc(glu_done, 1)
                dve.wait_ge(glu_done, q * 2 + (h + 1))
                dve.tensor_reduce(maxima[0][:, bass.ds(q * 2 + h, 1)], part(U, q, h), AX.XY, ALU.max,
                                  apply_absolute_value=True).then_inc(glu_maxed, 1)

            with dve.Fori(0, NG) as q:
                glu(q, 0, False)
                glu(q, 1, False)
            dve.wait_ge(glu_maxed, NH)
            top[0].vector(dve, maxima[0][:])

            dve.tensor_scalar(tiny["glu_unit"][:], tiny["gate_scale"][:], 1.0 / SIGQ, None, ALU.mult).then_inc(steps, 1)
            dve.wait_ge(steps, 1)
            dve.tensor_scalar(tiny["glu_scale"][:], top[0].top[:], tiny["glu_unit"][:, 0:1], None, ALU.mult)\
                .then_inc(steps, 1)
            dve.wait_ge(steps, 2)
            dve.tensor_scalar(tiny["glu_scale"][:], tiny["glu_scale"][:], 1.0 / QMAX, TINY, ALU.mult, ALU.max)\
                .then_inc(steps, 1)
            dve.wait_ge(steps, 3)
            dve.reciprocal(tiny["glu_inv"][:], tiny["glu_scale"][:]).then_inc(steps, 1)
            dve.wait_ge(steps, 4)
            dve.tensor_scalar(tiny["glu_inv"][:], tiny["glu_inv"][:], tiny["glu_unit"][:, 0:1], None, ALU.mult)\
                .then_inc(steps, 1)

            def hidden(q, h):
                dve.wait_ge(glu_q_done, q * 2 + (h + 1))
                dve.tensor_tensor(part(U, q, h), glu_q[h], part(up_q, q, h), ALU.mult).then_inc(h_done, 1)
                dve.wait_ge(h_done, q * 2 + (h + 1))
                dve.tensor_reduce(maxima[1][:, bass.ds(q * 2 + h, 1)], part(U, q, h), AX.XY, ALU.max,
                                  apply_absolute_value=True).then_inc(h_maxed, 1)

            with dve.Fori(0, NG) as q:
                hidden(q, 0)
                hidden(q, 1)
            dve.wait_ge(h_maxed, NH)
            top[1].vector(dve, maxima[1][:])
            dve.tensor_scalar(tiny["h_unit"][:], tiny["glu_scale"][:], tiny["up_scale"][:, 0:1], None, ALU.mult)\
                .then_inc(steps, 1)
            dve.wait_ge(steps, 6)
            dve.tensor_scalar(tiny["h_scale"][:], top[1].top[:], tiny["h_unit"][:, 0:1], None, ALU.mult)\
                .then_inc(steps, 1)
            dve.wait_ge(steps, 7)
            dve.tensor_scalar(tiny["h_scale"][:], tiny["h_scale"][:], 1.0 / QMAX, TINY, ALU.mult, ALU.max)\
                .then_inc(steps, 1)
            dve.wait_ge(steps, 8)
            dve.reciprocal(tiny["h_inv"][:], tiny["h_scale"][:]).then_inc(steps, 1)
            dve.wait_ge(steps, 9)
            dve.tensor_scalar(tiny["h_inv"][:], tiny["h_inv"][:], tiny["h_unit"][:, 0:1], None, ALU.mult)\
                .then_inc(steps, 1)
            dve.wait_ge(steps, 10)

            def hidden_ints(g, t, p, made):
                wait(dve, hpart_done, made)
                dve.tensor_scalar(hq[:], U[:, bass.ds(g, 1), :, t * L:(t + 1) * L].rearrange("p o m t -> p (o m) t"),
                                  tiny["h_inv"][:, 0:1], None, ALU.mult).then_inc(hq_done, 1)
                dve.wait_ge(hq_done, made + 1)
                if not isinstance(made, int) or made >= 2:
                    dve.wait_ge(h_parts, made - 1)
                dve.tensor_scalar(hpart[p][0][:], hq[:], HIGH, None, ALU.bitwise_and)
                dve.tensor_scalar(hpart[p][1][:], hq[:], LOW, None, ALU.bitwise_and).then_inc(hpart_done, 1)

            def residual(count, half_count, p):
                dve.wait_ge(down_done, count)
                dve.wait_ge(x2_ld[p], half_count)
                wait(dve, res_done, count - 2)
                dve.scalar_tensor_tensor(r[p], obank[p][0:L, 0:D], tiny["h_scale"][:, 0:1][0:L], x2[p],
                                         ALU.mult, ALU.add).then_inc(resid_done, 1)
                dve.wait_ge(resid_done, count)
                dve.bn_stats(stats[p][:], r[p]).then_inc(fbn_done, 1)
                dve.wait_ge(fbn_done, count)
                dve.memset(carrier[:], 0.0)
                dve.bn_aggr(mv[p][:], stats[p][:]).then_inc(fmv_done, 1)
                dve.wait_ge(fmv_done, count)
                dve.tensor_scalar(vare[p][:], mv[p][:, 1:2], EPS, None, ALU.add).then_inc(fvar_done, 1)

            def norm(count, p, stored):
                dve.wait_ge(frstd_done, count)
                if stored is not None:
                    dve.wait_ge(out_st[p], stored)
                dve.tensor_scalar(res[p], r[p], mv[p][:, 0:1], rstd[p][:, 0:1], ALU.subtract, ALU.mult)\
                    .then_inc(res_done, 1)

            hidden_ints(0, 0, 0, 0)
            hidden_ints(0, 1, 1, 1)
            residual(1, 16, 0)
            hidden_ints(0, 2, 0, 2)
            residual(2, 16, 1)
            norm(1, 0, None)
            hidden_ints(0, 3, 1, 3)
            residual(3, 32, 0)
            norm(2, 1, None)
            hidden_ints(1, 0, 0, 4)
            residual(4, 32, 1)
            norm(3, 0, 16)
            hidden_ints(1, 1, 1, 5)
            with dve.Fori(1, NG - 1) as g:
                for t in range(TG):
                    n = g * TG + t
                    p = t % 2
                    residual(n + 1, g * (8 * TG) + 16 * (t // 2 + 1), p)
                    norm(n, 1 - p, g * (8 * TG) + 16 * ((t - 1) // 2))
                    hidden_ints(g if t < 2 else g + 1, (t + 2) % TG, p, n + 2)
            g = NG - 1
            for t in range(TG):
                n, p = g * TG + t, t % 2
                residual(n + 1, g * (8 * TG) + 16 * (t // 2 + 1), p)
                norm(n, 1 - p, g * (8 * TG) + 16 * ((t - 1) // 2))
                if t < 2:
                    hidden_ints(g, t + 2, p, n + 2)
            norm(B, 1, 16 * (B // 2 - 1))

        @block.tensor
        def _(pe):
            for f in range(4):
                if f >= 2:
                    pe.wait_ge(lo_done, f - 1)
                for j in range(HG):
                    m = (f % 2) * HG + j
                    ins = pe.transpose(wbank[f % 2][:, j * P:(j + 1) * P], w_down[:, f // 2, m * P:(m + 1) * P], ident[:])
                ins.then_inc(turned, 1)
            pe.wait_ge(lo_done, 4)
            top[0].tensor(pe)
            top[1].tensor(pe)

            def tile(q, p, first):
                pe.wait_ge(h_parts, q * 2 + (p + 1))
                if not first:
                    pe.wait_ge(resid_done, q * 2 + (p - 1))
                for m in range(FT):
                    lhs, rhs = [x[:, m, :] for x in hh[p]], [x[:, m, :] for x in wd]
                    dst = obank[p][0:L, 0:D]
                    pe.matmul(dst, lhs[0], rhs[0], start=(m == 0), stop=False)
                    pe.matmul(dst, lhs[0], rhs[1], start=False, stop=False)
                    ins = pe.matmul(dst, lhs[1], rhs[0], start=False, stop=(m == FT - 1))
                ins.then_inc(down_done, 1)

            tile(0, 0, True)
            tile(0, 1, True)
            with pe.Fori(1, B // 2) as q:
                tile(q, 0, False)
                tile(q, 1, False)


_INS = {"x": "x", "ctx_1024": "ctx",
        "L0_attn_Wq": "aWq", "L0_attn_Wk": "aWk", "L0_attn_Wv": "aWv", "L0_attn_Wo": "aWo",
        "L0_attn_bq": "a_bq", "L0_attn_bk": "a_bk", "L0_attn_bv": "a_bv", "L0_attn_bo": "a_bo",
        "L0_xattn_Wq": "xWq", "L0_xattn_Wk": "xWk", "L0_xattn_Wv": "xWv", "L0_xattn_Wo": "xWo",
        "L0_xattn_bq": "x_bq", "L0_xattn_bk": "x_bk", "L0_xattn_bv": "x_bv", "L0_xattn_bo": "x_bo",
        "L0_ffn_w_gate": "w_gate", "L0_ffn_w_up": "w_up", "L0_ffn_w_down": "w_down"}


def shape_constants():
    bf16 = mybir.dt.np(BF16)

    def pieces(v):
        got, rest = [], v.astype(np.float32)
        for _ in range(3):
            got.append(rest.astype(bf16))
            rest = (rest - got[-1].astype(np.float32)).astype(np.float32)
        return got

    row = np.arange(P)
    slopes = (np.float32(1.0) / np.float32(2.0) ** (np.arange(H, dtype=np.float32) / np.float32(H))).astype(np.float32)
    key = np.arange(L, dtype=np.float32)
    sel = np.zeros((P, OCT * L), np.float32)
    for h in range(OCT):
        sel[h, h * L:(h + 1) * L] = 1.0
    alibi_l = np.stack([np.ones(L)] * 3 + [-key] * 3).astype(bf16)
    alibi_r = np.stack([p.reshape(-1) for p in pieces(slopes[:, None] * key[None, :])]
                       + [np.repeat(p, L) for p in pieces(slopes)])
    return {"ident": np.eye(P, dtype=np.float32),
            "mask8": (row[:, None] // HD == np.arange(OCT)[None, :]).astype(np.float32),
            "even_odd": np.stack([(row // HD) % 2 == 0, (row // HD) % 2 == 1], 1).astype(np.float32),
            "sel": sel, "alibi_l": alibi_l, "alibi_r": alibi_r.astype(bf16)}


def kernel(**inputs):
    import concourse.bacc as _bacc
    from concourse.bass_utils import run_bass_kernel_spmd as _run

    nc = _bacc.Bacc("TRN2", target_bir_lowering=False, num_devices=1)
    arrays, aps = {}, {}
    given = {short: np.ascontiguousarray(inputs[name]) for name, short in _INS.items()}
    given.update(shape_constants())
    for short, v in given.items():
        arrays[f"in_{short}"] = v
        aps[short] = nc.dram_tensor(f"in_{short}", v.shape, mybir.dt.from_np(v.dtype), kind="ExternalInput").ap()
    out = nc.dram_tensor("out_0", (B, L, D), F32, kind="ExternalOutput").ap()
    x2_dram = nc.dram_tensor("x2_scratch", (B, L, D), F32, kind="Internal").ap()
    decoder(nc, aps, out, x2_dram)
    r = _run(nc, [arrays], core_ids=[0])
    return r.results[0]["out_0"]
```

```python
from contextlib import ExitStack

import numpy as np
import concourse.bass as bass
from concourse import mybir

F32 = mybir.dt.float32
F32R = mybir.dt.float32r
BF16 = mybir.dt.bfloat16
I16 = mybir.dt.int16
U16 = mybir.dt.uint16
ALU = mybir.AluOpType
ACT = mybir.ActivationFunctionType
AX = mybir.AxisListType

B, L, S, D = 32, 112, 375, 256
H, HD = 16, 16
P = 128
KT = D // P
OCT, QUAD = 8, 4
NC = 3
C = S // NC
SP = S + 1
NU = KT * NC
QW = QUAD * L
BANK = 512
SCALE = HD ** -0.5
EPS = 1e-5
F = 768
FT = F // P
GT = 4 * L
NG = B * L // GT
QBLK = 32
QMAX = 2.0 ** 15 - 1.0
WMAX = 2.0 ** 3 - 1.0
TINY = 1e-12
SIGQ = 65536.0
LOW = 15
HIGH = -16


STAGES = 6
FIRST = 1 - STAGES
LOOP_FROM = 2
LOOP_PAIRS = (B - STAGES - LOOP_FROM) // 2
LOOP_TO = LOOP_FROM + 2 * LOOP_PAIRS

WORK_USES = (
        (("V1", 3), ("K1", 3), ("PT0", 4), ("Ks", 5), ("PT2", 4), ("ctxT1", 4), ("K0", 4), ("Ox", 2)),
        (("x1T", 3), ("Qx", 3), ("xT", 5), ("V2", 3), ("PT1", 4), ("ctxT0", 4), ("AVs0", 4), ("PT3", 4),
     ("AVs1", 4), ("Qs", 5), ("Os", 4), ("x2T", 1), ("V0", 4), ("Vs", 5)),
)
SLOT_USES = (
        (("S1", 4), ("C0", 3), ("C2", 3), ("S0", 5)),
        (("C4", 2), ("C5", 2), ("C1", 3), ("C3", 3)),
)
WORK_OF = {use: bank for bank, uses in enumerate(WORK_USES) for use, _ in uses}
SLOT_OF = {unit: slot for slot, uses in enumerate(SLOT_USES) for unit, _ in uses}


def before(uses, use, batch):
    place = [u for u, _ in uses].index(use)
    i = batch - uses[place][1]
    while i >= FIRST:
        for name, stage in reversed(uses[:place]):
            if 0 <= i + stage < B:
                yield name, i + stage
        place, i = len(uses), i - 1


class Batch:

    def __init__(self, pair, off):
        self.pair, self.off = pair, off
        self.par = off % 2
        self.looped = not isinstance(pair, int)

    def plus(self, d):
        return Batch(self.pair, self.off + d)

    def back(self, d):
        return Batch(self.pair, self.off - d)

    def exists(self):
        return self.looped or 0 <= self.off < B

    def times(self, per, more=0):
        fixed = per * self.off + more
        return self.pair * (2 * per) + fixed if self.looped else fixed

    def loads(self):
        fixed = 16 * (self.off // 2 + 1)
        return self.pair * 16 + fixed if self.looped else fixed

    def first_fills(self, use):
        return sum(1 for _ in before(WORK_USES[WORK_OF[use]], use, self.off))

    def fills(self, use):
        uses = WORK_USES[WORK_OF[use]]
        count = self.first_fills(use)
        if not self.looped:
            return count
        last = sum(1 for _ in before(uses, use, self.off + 2 * (LOOP_PAIRS - 1)))
        assert last == count + 2 * len(uses) * (LOOP_PAIRS - 1)
        return self.pair * (2 * len(uses)) + count


def stages(pair, i):
    batches = [Batch(pair, i + s) for s in range(STAGES)]
    return [n if n.exists() else None for n in batches]


def wait(eng, sem, value):
    if isinstance(value, int) and value <= 0:
        return
    eng.wait_ge(sem, value)


def decoder(nc, a, out, x2_dram):
    with ExitStack() as persist:
        def keep(name, shape, dt=F32):
            return persist.enter_context(nc.sbuf_tensor(name, shape, dt))

        ident = keep("ident", [P, P])
        x2T_all = keep("x2T_all", [P, KT, B * L])
        xmax_all = keep("xmax_all", [P, B])
        wT = {n: [keep(f"{n}T_{p}", [P, KT, F], F32R) for p in ("hi", "lo")] for n in ("w_up", "w_gate")}
        w_down = keep("w_down", [P, KT, F])
        with ExitStack() as scope:
            constants = AttentionConstants(scope, nc, a, x2T_all)
            quantise_weights(nc, a, ident, wT, w_down, constants)
            attention(nc, a, ident, x2T_all, xmax_all, x2_dram, constants)
        feed_forward(nc, out, x2_dram, ident, x2T_all, xmax_all, wT, w_down)


class AttentionConstants:

    def __init__(self, ctx, nc, a, x2T_all):
        def sb(name, shape, dt=F32):
            return ctx.enter_context(nc.sbuf_tensor(name, shape, dt))

        self.a = a
        self.const_ld = ctx.enter_context(nc.semaphore("const_ld"))
        names = ("aWq", "aWk", "aWv", "aWo", "xWq", "xWk", "xWv", "xWo")
        early = {"xWk": 0, "xWv": KT * D}
        w = {n: sb(n, [P, KT, D]) for n in names if n not in early}
        for n, at in early.items():
            w[n] = x2T_all[:, 0, at:at + KT * D].rearrange("p (k n) -> p k n", k=KT)
        split = {n: [sb(f"{n}_{p}", [P, KT, D], F32R) for p in ("hi", "lo")] for n in ("xWk", "xWv")}
        bcol = {n: sb(n, [P, KT]) for n in ("abq", "abk", "abv", "xbq", "xbk")}
        brow = {n: sb(n, [P, D]) for n in ("abo", "xbv", "xbo")}
        mask8 = sb("mask8", [P, OCT])
        even_odd = sb("even_odd", [P, 2])
        sel_raw = x2T_all[:, 1, 0:OCT * L]
        sel = sb("sel", [P, OCT * L], F32R)
        alibi_l = sb("alibi_l", [6, L], BF16)
        alibi_r = sb("alibi_r", [6, H * L], BF16)
        columns = {"abq": "a_bq", "abk": "a_bk", "abv": "a_bv", "xbq": "x_bq", "xbk": "x_bk"}
        rows = {"abo": "a_bo", "xbv": "x_bv", "xbo": "x_bo"}
        N_CONST = len(names) + len(columns) + len(rows) + 5
        self.w, self.split, self.bcol, self.brow, self.early = w, split, bcol, brow, early
        self.mask8, self.even_odd, self.sel_raw, self.sel = mask8, even_odd, sel_raw, sel
        self.alibi_l, self.alibi_r = alibi_l, alibi_r
        self.names, self.columns, self.rows = names, columns, rows
        self.LOADED = 16 * N_CONST

    def load_weights(self, eng, names):
        for n in names:
            eng.dma_start(self.w[n] if n in self.early else self.w[n][:],
                          self.a[n].rearrange("(k p) n -> p k n", p=P)).then_inc(self.const_ld, 16)

    def load_columns(self, eng):
        for n, src in self.columns.items():
            eng.dma_start(self.bcol[n][:], self.a[src].rearrange("(m p) -> p m", p=P),
                          allow_slow_non_contiguous=True).then_inc(self.const_ld, 16)

    def load_rows(self, eng):
        for n, src in self.rows.items():
            eng.dma_start(self.brow[n][:], self.a[src].rearrange("(o n) -> o n", o=1).broadcast_to([P, D]))\
                .then_inc(self.const_ld, 16)
        for dst, src in ((self.mask8, "mask8"), (self.even_odd, "even_odd"), (self.sel_raw, "sel"),
                         (self.alibi_l, "alibi_l"), (self.alibi_r, "alibi_r")):
            eng.dma_start(dst if src == "sel" else dst[:], self.a[src]).then_inc(self.const_ld, 16)


def quantise_weights(nc, a, ident, wT, w_down, constants):
    NB = KT * F // QBLK
    with ExitStack() as ctx:
        def sb(name, shape, dt=F32):
            return ctx.enter_context(nc.sbuf_tensor(name, shape, dt))

        def sem(name):
            return ctx.enter_context(nc.semaphore(name))

        order = ("w_up", "w_gate", "w_down")
        load_order = ("w_up", "w_down", "w_gate")
        raw = {n: sb(f"raw_{n}", [P, NB, QBLK]) for n in order}
        quant = {n: sb(f"quant_{n}", [P, NB, QBLK], I16) for n in order}
        value = {n: sb(f"value_{n}", [P, NB, QBLK]) for n in order[:2]}
        scale = {n: sb(f"scale_{n}", [P, NB]) for n in order}
        inverse = {n: sb(f"inverse_{n}", [P, NB]) for n in order}
        bank = [ctx.enter_context(nc.psum_tensor(f"wbank{p}", [P, BANK], F32)) for p in range(2)]
        HALF = F // 2
        N_FILLS = 2 * KT
        loaded = {n: sem(f"loaded_{n}") for n in order}
        ident_ld, step_done, value_done = sem("ident_ld"), sem("step_done"), sem("value_done")
        turned, hi_done, lo_done = sem("turned"), sem("hi_done"), sem("lo_done")
        block = ctx.enter_context(nc.Block())

        @block.sync
        def _(sp):
            for n in load_order:
                sp.dma_start(raw[n][:].rearrange("p (t b) e -> p t (b e)", t=a[n].shape[0] // P),
                             a[n].rearrange("(t p) i -> p t i", p=P)).then_inc(loaded[n], 16)
            sp.dma_start(ident[:], a["ident"]).then_inc(ident_ld, 16)
            constants.load_weights(sp, constants.names)

        @block.vector
        def _(dve):
            def lo_half(f):
                n, k, h = order[f // N_FILLS], (f // 2) % KT, f % 2
                cols = slice(h * HALF, (h + 1) * HALF)
                dve.wait_ge(hi_done, f + 1)
                dve.tensor_tensor(wT[n][1][:, k, cols], bank[f % 2][:, 0:HALF], wT[n][0][:, k, cols].bitcast(F32),
                                  ALU.subtract).then_inc(lo_done, 1)

            for e, n in enumerate(load_order):
                dve.wait_ge(loaded[n], 16)
                dve.tensor_reduce(scale[n][:], raw[n][:], AX.X, ALU.max, apply_absolute_value=True)\
                    .then_inc(step_done, 1)
                dve.wait_ge(step_done, 4 * e + 1)
                dve.tensor_scalar(scale[n][:], scale[n][:], 1.0 / WMAX, TINY, ALU.mult, ALU.max).then_inc(step_done, 1)
                dve.wait_ge(step_done, 4 * e + 2)
                dve.reciprocal(inverse[n][:], scale[n][:]).then_inc(step_done, 1)
                dve.wait_ge(step_done, 4 * e + 3)
                dve.tensor_tensor(quant[n][:], raw[n][:],
                                  inverse[n][:].rearrange("p (b o) -> p b o", o=1).broadcast_to([P, NB, QBLK]),
                                  ALU.mult).then_inc(step_done, 1)
                dve.wait_ge(step_done, 4 * e + 4)
                dst = value[n][:] if n in value else w_down[:].rearrange("p t (b e) -> p (t b) e", e=QBLK)
                dve.tensor_tensor(dst, quant[n][:],
                                  scale[n][:].rearrange("p (b o) -> p b o", o=1).broadcast_to([P, NB, QBLK]),
                                  ALU.mult).then_inc(value_done, 1)
                if n == "w_down":
                    for f in range(N_FILLS):
                        lo_half(f)
            for f in range(N_FILLS, 2 * N_FILLS):
                lo_half(f)

        @block.scalar
        def _(act):
            constants.load_columns(act)
            constants.load_rows(act)
            for f in range(2 * N_FILLS):
                n, k, h = order[f // N_FILLS], (f // 2) % KT, f % 2
                act.wait_ge(turned, f + 1)
                act.activation(wT[n][0][:, k, h * HALF:(h + 1) * HALF], bank[f % 2][:, 0:HALF], ACT.Copy)\
                    .then_inc(hi_done, 1)

        @block.tensor
        def _(pe):
            pe.wait_ge(ident_ld, 16)
            for f in range(2 * N_FILLS):
                e, k, h = f // N_FILLS, (f // 2) % KT, f % 2
                pe.wait_ge(value_done, (1, 3)[e])
                if f >= 2:
                    pe.wait_ge(lo_done, f - 1)
                rows = value[order[e]][:].rearrange("p (t b) e -> p t (b e)", t=FT)
                for j in range(FT // 2):
                    ins = pe.transpose(bank[f % 2][:, j * P:(j + 1) * P],
                                       rows[:, h * (FT // 2) + j, k * P:(k + 1) * P], ident[:])
                ins.then_inc(turned, 1)


def attention(nc, a, ident, x2T_all, xmax_all, x2_dram, constants):
    with ExitStack() as ctx:
        def sb(name, shape, dt=F32):
            return ctx.enter_context(nc.sbuf_tensor(name, shape, dt))

        def sem(name):
            return ctx.enter_context(nc.semaphore(name))

        w, split, bcol, brow = constants.w, constants.split, constants.bcol, constants.brow
        mask8, even_odd, sel_raw, sel = constants.mask8, constants.even_odd, constants.sel_raw, constants.sel
        alibi_l, alibi_r, const_ld = constants.alibi_l, constants.alibi_r, constants.const_ld
        half = sb("half", [P, 1])
        warm = sb("warm", [P, 2])

        x_in = [sb(f"x_in{p}", [L, D]) for p in range(2)]
        ctx_in = [sb(f"ctx_in{p}", [C, NC, D]) for p in range(2)]
        ctxT = [sb(f"ctxT_{p}", [P, KT, SP], F32R) for p in ("hi", "lo")]
        KxT = [[sb(f"KxT{q}_{p}", [P, KT, S], F32R) for p in ("hi", "lo")] for q in range(2)]
        Vx = [sb(f"Vx{p}", [C, NC, D]) for p in range(2)]
        Qx = [sb(f"Qx_{p}", [P, KT, L], F32R) for p in ("hi", "lo")]
        Qbd = [sb(f"Qbd_{p}", [P, H, L], F32R) for p in ("hi", "lo")]
        Qs = [sb(f"Qs_{p}", [P, KT, L], F32R) for p in ("hi", "lo")]
        Ks = [sb(f"Ks_{p}", [P, KT, L], F32R) for p in ("hi", "lo")]
        Kbd = [sb(f"Kbd_{p}", [P, H, L], F32R) for p in ("hi", "lo")]
        xT = sb("xT", [P, KT, L])
        Vs = sb("Vs", [L, D])
        Ps = sb("Ps", [L, H, L])
        PsT = sb("PsT", [L, H, L])
        nmax_s = sb("nmax_s", [L, H])
        Zs = sb("Zs", [L, H])
        rZs = sb("rZs", [L, H])
        rZrep = sb("rZrep", [L, KT, OCT, HD])
        evenT = sb("evenT", [P, KT, L])
        sumT = sb("sumT", [P, KT, L])
        attnT = sb("attnT", [P, KT, L])
        xb = sb("xb", [L, D])
        r1 = sb("r1", [L, D])
        x1 = sb("x1", [L, D])
        x1T = sb("x1T", [P, KT, L])
        x1b = [sb(f"x1b{p}", [L, D]) for p in range(2)]
        nmax_c = [sb(f"nmax_c{p}", [C, P]) for p in range(2)]
        nmaxT = [sb(f"nmaxT{p}", [P, SP // NC + 1], F32R) for p in range(2)]
        Px = [sb(f"Px{p}", [C, OCT, L]) for p in range(2)]
        Zc = [sb(f"Zc{p}", [C, OCT]) for p in range(2)]
        rZc = [sb(f"rZc{p}", [C, OCT]) for p in range(2)]
        Vn = [sb(f"Vn{p}", [C, OCT, HD]) for p in range(2)]
        evenX = sb("evenX", [P, KT, L])
        OxT = sb("OxT", [P, KT, L])
        r2 = sb("r2", [L, D])
        x2 = sb("x2", [L, D])
        carrier = sb("carrier", [1, 1])
        stats = [sb(f"stats{p}", [L, 6]) for p in range(2)]
        mv = [sb(f"mv{p}", [L, 2]) for p in range(2)]
        vare = [sb(f"vare{p}", [L, 1]) for p in range(2)]
        rstd = [sb(f"rstd{p}", [L, 1]) for p in range(2)]

        score = [ctx.enter_context(nc.psum_tensor(f"score{p}", [P, 2, BANK], F32)) for p in range(2)]
        work = [ctx.enter_context(nc.psum_tensor(f"work{p}", [P, BANK], F32)) for p in range(2)]
        outX = ctx.enter_context(nc.psum_tensor("outX", [P, KT, 2 * L], F32))
        maxT = ctx.enter_context(nc.psum_tensor("maxT", [P, BANK], F32))

        consts = sem("consts")
        bv_spread, bv_product, bo_folded = sem("bv_spread"), sem("bv_product"), sem("bo_folded")
        x_ld = [sem(f"x_ld{p}") for p in range(2)]
        ctx_ld = [sem(f"ctx_ld{p}") for p in range(2)]
        filled = [sem(f"filled{p}") for p in range(2)]
        drained = [sem(f"drained{p}") for p in range(2)]
        ctx_hi, kx_hi, ks_hi, qs_hi, qx_hi = (sem(n) for n in ("ctx_hi", "kx_hi", "ks_hi", "qs_hi", "qx_hi"))
        kbd_done, qbd_done = sem("kbd_done"), sem("qbd_done")
        scores_s, nmax_s_done, exp_s = sem("scores_s"), sem("nmax_s_done"), sem("exp_s")
        rz_s, rzrep_s, even_s, sum_s = sem("rz_s"), sem("rzrep_s"), sem("even_s"), sem("sum_s")
        scores_c, nmax_c_done, nmaxT_done = sem("scores_c"), sem("nmax_c_done"), sem("nmaxT_done")
        nmaxT_copied, shifted, exp_c = sem("nmaxT_copied"), sem("shifted"), sem("exp_c")
        z_c, rz_c, vn_done, av_done = sem("z_c"), sem("rz_c"), sem("vn_done"), sem("av_done")
        even_x, oxT_done, xmax_done = sem("even_x"), sem("oxT_done"), sem("xmax_done")
        xb_done, x1b_done = sem("xb_done"), sem("x1b_done")
        bn_done = [sem(f"bn_done{p}") for p in (1, 2)]
        mv_done = [sem(f"mv_done{p}") for p in (1, 2)]
        var_done = [sem(f"var_done{p}") for p in (1, 2)]
        rstd_done = [sem(f"rstd_done{p}") for p in (1, 2)]
        x1_done, x2_done, x2T_copied, x2_saved = sem("x1_done"), sem("x2_done"), sem("x2T_copied"), sem("x2_saved")

        x_dram, ctx_dram = a["x"], a["ctx"]
        def iterations(eng, step):
            for i in range(FIRST, LOOP_FROM):
                step(*stages(0, i))
            with eng.Fori(0, LOOP_PAIRS) as r:
                step(*stages(r, LOOP_FROM))
                step(*stages(r, LOOP_FROM + 1))
            for i in range(LOOP_TO, B):
                step(*stages(0, i))

        def latest_of_banks(uses):
            latest = {}
            for n, use in uses:
                bank = WORK_OF[use]
                if n.exists() and (bank not in latest or n.first_fills(use) > latest[bank][0].first_fills(latest[bank][1])):
                    latest[bank] = (n, use)
            return latest.items()

        def wait_fill(eng, *uses):
            for bank, (n, use) in latest_of_banks(uses):
                eng.wait_ge(filled[bank], n.fills(use) + 1)

        def wait_drain(eng, *uses):
            for bank, (n, use) in latest_of_banks(uses):
                eng.wait_ge(drained[bank], n.fills(use) + 1)

        block = ctx.enter_context(nc.Block())

        @block.sync
        def _(sp):
            def load_x(n):
                wait(sp, xb_done, n.back(2).times(1, 1))
                sp.dma_start(x_in[n.par][:], x_dram[bass.ds(n.times(1), 1)].rearrange("o l d -> (o l) d"))\
                    .then_inc(x_ld[n.par], 16)

            def load_ctx(n):
                wait_fill(sp, (n.back(2), "ctxT1"))
                sp.dma_start(ctx_in[n.par][:],
                             ctx_dram[bass.ds(n.times(1), 1)].rearrange("o (c s) d -> s (o c) d", c=NC))\
                    .then_inc(ctx_ld[n.par], 16)

            def save_x2(n):
                sp.wait_ge(x2_done, n.times(1, 1))
                sp.dma_start(x2_dram[bass.ds(n.times(1), 1)].rearrange("o l d -> (o l) d"), x2[:])\
                    .then_inc(x2_saved, 16)

            def step(n0, n1, n2, n3, n4, n5):
                if n5:
                    load_x(n5)
                    load_ctx(n5)
                if n1:
                    save_x2(n1)
            iterations(sp, step)
            sp.wait_ge(x2_saved, 16 * B)

        @block.gpsimd
        def _(pool):
            pool.memset(half[:], -0.5).then_inc(consts, 1)
            for h in range(2):
                pool.memset(nmax_c[h][:], 0.0).then_inc(consts, 1)
                pool.memset(ctxT[h][:, :, S:SP].bitcast(F32), 0.0).then_inc(consts, 1)
            pool.memset(xmax_all[:], 0.0).then_inc(consts, 1)
            pool.wait_ge(const_ld, constants.LOADED)
            pool.wait_ge(bo_folded, 1)

            def block_diagonal(dst, src, t, done):
                for h in range(2):
                    ins = pool.tensor_tensor(
                        dst[h][:, OCT * t:OCT * (t + 1), :],
                        src[h][:, t:t + 1, :].bitcast(F32).broadcast_to([P, OCT, L]),
                        mask8[:].rearrange("p (h o) -> p h o", o=1).broadcast_to([P, OCT, L]), ALU.mult)
                ins.then_inc(done, 1)

            def diagonal_keys(n, t):
                if t == 0:
                    wait_drain(pool, (n, "Ks"))
                wait(pool, scores_s, n.back(1).times(KT, t + 1))
                block_diagonal(Kbd, Ks, t, kbd_done)

            def diagonal_queries(n, t):
                if t == 0:
                    wait_drain(pool, (n, "Qx"))
                wait(pool, scores_c, n.back(1).times(NU, NC * (t + 1)))
                block_diagonal(Qbd, Qx, t, qbd_done)

            def inverse_root(n, k):
                pool.wait_ge(var_done[k], n.times(1, 1))
                pool.tensor_tensor(rstd[k][:], vare[k][:], half[0:L, :], ALU.pow).then_inc(rstd_done[k], 1)

            def add_output_bias(n):
                wait_fill(pool, (n, "xT"))
                wait_drain(pool, (n.back(1), "Os"))
                pool.tensor_tensor(xb[:], x_in[n.par][:], brow["abo"][0:L, :], ALU.add).then_inc(xb_done, 1)

            def add_output_bias_2(n):
                pool.wait_ge(x1_done, n.times(1, 1))
                wait_drain(pool, (n.back(2), "Ox"))
                pool.tensor_tensor(x1b[n.par][:], x1[:], brow["xbo"][0:L, :], ALU.add).then_inc(x1b_done, 1)

            def step(n0, n1, n2, n3, n4, n5):
                if n2:
                    diagonal_queries(n2, 1)
                if n4:
                    diagonal_keys(n4, 0)
                if n0:
                    inverse_root(n0, 1)
                if n3:
                    add_output_bias(n3)
                    inverse_root(n3, 0)
                if n4:
                    diagonal_keys(n4, 1)
                if n3:
                    diagonal_queries(n3, 0)
                    add_output_bias_2(n3)
            iterations(pool, step)

        @block.scalar
        def _(act):
            act.wait_ge(const_ld, constants.LOADED)
            act.activation(warm[:, 0:1], mask8[:, 0:1], ACT.Exp)
            for n in ("xWk", "xWv"):
                act.activation(split[n][0][:], w[n], ACT.Copy).then_inc(consts, 1)
            act.activation(sel[:], sel_raw, ACT.Copy).then_inc(consts, 1)

            def exp_self(n, t):
                act.wait_ge(nmax_s_done, n.times(KT, t + 1))
                wait_fill(act, (n.back(1), f"PT{2 * t + 1}"))
                wait(act, rz_s, n.back(1).times(KT, t + 1))
                slot = SLOT_OF[f"S{t}"]
                for h in range(OCT):
                    g = OCT * t + h
                    ins = act.activation(Ps[:, g, :], score[slot][0:L, h // QUAD, (h % QUAD) * L:(h % QUAD + 1) * L],
                                         ACT.Exp, bias=nmax_s[:, g:g + 1], accum_out=Zs[:, g:g + 1])
                ins.then_inc(exp_s, 1)

            def exp_cross(n, u):
                act.wait_ge(shifted, n.times(NU, u + 1))
                wait(act, av_done, n.times(NU, u - 1))
                act.activation(Px[u % 2][:].rearrange("s (q h) l -> s q (h l)", q=2),
                               score[SLOT_OF[f"C{u}"]][0:C, :, 0:QW], ACT.Exp).then_inc(exp_c, 1)

            def copy_max(n, u):
                act.wait_ge(nmaxT_done, n.times(NU, u + 1))
                wait(act, shifted, n.times(NU, u - 1))
                act.activation(nmaxT[u % 2][:, 0:C], maxT[:, 0:C], ACT.Copy).then_inc(nmaxT_copied, 1)

            def hi_with_bias(n, use, dst, bias, done):
                wait_fill(act, (n, use))
                for m in range(KT):
                    ins = act.activation(dst[:, m, :], work[WORK_OF[use]][:, m * L:(m + 1) * L], ACT.Identity,
                                         bias=bias[:, m:m + 1])
                ins.then_inc(done, 1)

            def hi_queries_self(n):
                wait(act, scores_s, n.back(1).times(KT, KT))
                hi_with_bias(n, "Qs", Qs[0], bcol["abq"], qs_hi)

            def hi_keys_self(n):
                wait(act, kbd_done, n.back(1).times(KT, KT))
                hi_with_bias(n, "Ks", Ks[0], bcol["abk"], ks_hi)

            def hi_queries_cross(n):
                wait(act, qbd_done, n.back(1).times(KT, KT))
                hi_with_bias(n, "Qx", Qx[0], bcol["xbq"], qx_hi)

            def drain_copy(n, use, dst, rows_, cols, readers):
                b = WORK_OF[use]
                wait_fill(act, (n, use), *((n.back(1), r) for r in readers))
                act.activation(dst, work[b][0:rows_, 0:cols], ACT.Copy).then_inc(drained[b], 1)

            def copy_xT(n):
                drain_copy(n, "xT", xT[:].rearrange("p k l -> p (k l)"), P, KT * L, ("Ks", "Qs", "Vs"))

            def copy_x1T(n):
                drain_copy(n, "x1T", x1T[:].rearrange("p k l -> p (k l)"), P, KT * L, ("Qx",))

            def copy_x2T(n):
                b = WORK_OF["x2T"]
                wait_fill(act, (n, "x2T"))
                act.activation(x2T_all[:, :, bass.ds(n.times(L), L)],
                               work[b][:, 0:KT * L].rearrange("p (k l) -> p k l", k=KT), ACT.Copy)\
                    .then_inc(drained[b], 1)

            def copy_values_self(n):
                drain_copy(n, "Vs", Vs[:], L, D, ("AVs1",))

            def copy_probs(n, j):
                drain_copy(n, f"PT{j}", PsT[:, QUAD * j:QUAD * (j + 1), :].rearrange("k h q -> k (h q)"), L, QW,
                           (f"AVs{j // 2}",))

            def even_self(n, t):
                use = f"AVs{t}"
                wait_fill(act, (n, use))
                wait(act, sum_s, n.back(1).times(KT, t + 1))
                act.activation(evenT[:, t, :], work[WORK_OF[use]][:, 0:L], ACT.Copy,
                               scale=even_odd[:, 0:1]).then_inc(even_s, 1)

            def even_cross(n):
                act.wait_ge(av_done, n.times(NU, NU))
                wait(act, oxT_done, n.back(1).times(1, 1))
                act.activation(evenX[:], outX[:, :, 0:L], ACT.Copy, scale=even_odd[:, 0:1]).then_inc(even_x, 1)

            def hi_context(n, k):
                use = f"ctxT{k}"
                last = [(n.back(1), u) for u in ("K1", "V2")] if k == 0 else []
                wait_fill(act, (n, use), *last)
                act.activation(ctxT[0][:, k, 0:S], work[WORK_OF[use]][:, 0:S], ACT.Copy).then_inc(ctx_hi, 1)

            def hi_keys_cross(n, m):
                use = f"K{m}"
                wait_fill(act, (n, use))
                wait(act, scores_c, n.back(2).times(NU, NC * (m + 1)))
                act.activation(KxT[n.par][0][:, m, :], work[WORK_OF[use]][:, 0:S], ACT.Identity,
                               bias=bcol["xbk"][:, m:m + 1]).then_inc(kx_hi, 1)

            def step(n0, n1, n2, n3, n4, n5):
                if n1:
                    even_cross(n1)
                if n3:
                    even_self(n3, 1)
                if n2:
                    exp_cross(n2, 1)
                if n4:
                    hi_queries_self(n4)
                if n3:
                    hi_keys_cross(n3, 0)
                if n2:
                    copy_max(n2, 2)
                if n0:
                    copy_x2T(n0)
                if n2:
                    exp_cross(n2, 2)
                    copy_max(n2, 3)
                    exp_cross(n2, 3)
                if n4:
                    copy_values_self(n4)
                if n3:
                    copy_x1T(n3)
                if n4:
                    exp_self(n4, 0)
                if n2:
                    copy_max(n2, 4)
                if n3:
                    hi_keys_cross(n3, 1)
                    hi_queries_cross(n3)
                if n2:
                    exp_cross(n2, 4)
                if n4:
                    copy_probs(n4, 0)
                if n5:
                    copy_xT(n5)
                if n4:
                    exp_self(n4, 1)
                if n5:
                    hi_keys_self(n5)
                if n2:
                    copy_max(n2, 5)
                if n4:
                    copy_probs(n4, 1)
                    hi_context(n4, 0)
                if n2:
                    exp_cross(n2, 5)
                if n3:
                    copy_max(n3, 0)
                if n4:
                    copy_probs(n4, 2)
                    even_self(n4, 0)
                if n3:
                    exp_cross(n3, 0)
                if n4:
                    copy_probs(n4, 3)
                    hi_context(n4, 1)
                if n3:
                    copy_max(n3, 1)
            iterations(act, step)

        @block.vector
        def _(dve):
            dve.wait_ge(const_ld, constants.LOADED)
            for n in ("aWq", "xWq"):
                dve.tensor_scalar(w[n][:], w[n][:], SCALE, None, ALU.mult).then_inc(consts, 1)
            for n in ("abq", "xbq"):
                dve.tensor_scalar(bcol[n][:], bcol[n][:], SCALE, None, ALU.mult).then_inc(consts, 1)
            dve.wait_ge(consts, 13)
            for n in ("xWk", "xWv"):
                dve.tensor_tensor(split[n][1][:], w[n], split[n][0][:].bitcast(F32), ALU.subtract)\
                    .then_inc(consts, 1)

            dve.tensor_copy(x1T[:], bcol["abv"][:].rearrange("p (k o) -> p k o", o=1).broadcast_to([P, KT, L]))\
                .then_inc(bv_spread, 1)
            dve.wait_ge(bv_product, 1)
            dve.tensor_tensor(brow["abo"][0:L, :], work[0][0:L, 0:D], brow["abo"][0:L, :], ALU.add)\
                .then_inc(bo_folded, 1)

            def sum_cross(n, u):
                p = u % 2
                dve.wait_ge(exp_c, n.times(NU, u + 1))
                dve.tensor_reduce(Zc[p][:], Px[p][:], AX.X, ALU.add).then_inc(z_c, 1)

            def reciprocal_cross(n, u):
                dve.wait_ge(z_c, n.times(NU, u + 1))
                dve.reciprocal(rZc[u % 2][:], Zc[u % 2][:]).then_inc(rz_c, 1)

            def normalise_values(n, u):
                t, c = divmod(u, NC)
                p = u % 2
                dve.wait_ge(rz_c, n.times(NU, u + 1))
                dve.tensor_tensor(Vn[p][:], Vx[n.par][:, c, P * t:P * (t + 1)].rearrange("s (h e) -> s h e", h=OCT),
                                  rZc[p][:].rearrange("s (h o) -> s h o", o=1).broadcast_to([C, OCT, HD]), ALU.mult)\
                    .then_inc(vn_done, 1)

            def max_cross(n, u):
                dve.wait_ge(scores_c, n.times(NU, u + 1))
                wait(dve, nmaxT_done, n.times(NU, u - 1))
                dve.tensor_reduce(nmax_c[u % 2][:, 0:OCT].rearrange("s (q h) -> s q h", q=2),
                                  score[SLOT_OF[f"C{u}"]][0:C, :, 0:QW].rearrange("s q (h l) -> s q h l", h=QUAD),
                                  AX.X, ALU.max, negate=True).then_inc(nmax_c_done, 1)

            def max_self(n, t):
                dve.wait_ge(scores_s, n.times(KT, t + 1))
                wait(dve, exp_s, n.back(1).times(KT, t + 1))
                dve.tensor_reduce(nmax_s[:, OCT * t:OCT * (t + 1)].rearrange("s (q h) -> s q h", q=2),
                                  score[SLOT_OF[f"S{t}"]][0:L, :, 0:QW].rearrange("s q (h l) -> s q h l", h=QUAD),
                                  AX.X, ALU.max, negate=True).then_inc(nmax_s_done, 1)

            def lo_with_bias(n, use, dst, hi, bias, hi_sem):
                b = WORK_OF[use]
                dve.wait_ge(hi_sem, n.times(1, 1))
                for m in range(KT):
                    ins = dve.scalar_tensor_tensor(dst[:, m, :], work[b][:, m * L:(m + 1) * L], bias[:, m:m + 1],
                                                   hi[:, m, :].bitcast(F32), ALU.add, ALU.subtract)
                ins.then_inc(drained[b], 1)

            def lo_context(n, k):
                b = WORK_OF[f"ctxT{k}"]
                dve.wait_ge(ctx_hi, n.times(KT, k + 1))
                dve.tensor_tensor(ctxT[1][:, k, 0:S], work[b][:, 0:S], ctxT[0][:, k, 0:S].bitcast(F32),
                                  ALU.subtract).then_inc(drained[b], 1)

            def lo_keys_cross(n, m):
                b = WORK_OF[f"K{m}"]
                dve.wait_ge(kx_hi, n.times(KT, m + 1))
                dve.scalar_tensor_tensor(KxT[n.par][1][:, m, :], work[b][:, 0:S], bcol["xbk"][:, m:m + 1],
                                         KxT[n.par][0][:, m, :].bitcast(F32), ALU.add, ALU.subtract)\
                    .then_inc(drained[b], 1)

            def values_with_bias(n, c):
                use = f"V{c}"
                b = WORK_OF[use]
                wait_fill(dve, (n, use))
                dve.tensor_tensor(Vx[n.par][:, c, :], work[b][0:C, 0:D], brow["xbv"][0:C, :], ALU.add)\
                    .then_inc(drained[b], 1)

            def reciprocal_self(n, t):
                dve.wait_ge(exp_s, n.times(KT, t + 1))
                h = slice(OCT * t, OCT * (t + 1))
                dve.reciprocal(rZs[:, h], Zs[:, h]).then_inc(rz_s, 1)

            def spread_reciprocal(n, t):
                h = slice(OCT * t, OCT * (t + 1))
                dve.wait_ge(rz_s, n.times(KT, t + 1))
                wait_fill(dve, (n.back(1), f"AVs{t}"))
                dve.tensor_copy(rZrep[:, t], rZs[:, h].rearrange("q (h o) -> q h o", o=1).broadcast_to([L, OCT, HD]))\
                    .then_inc(rzrep_s, 1)

            def pick_self(n, t):
                dve.wait_ge(even_s, n.times(KT, t + 1))
                dve.scalar_tensor_tensor(sumT[:, t, :], work[WORK_OF[f"AVs{t}"]][:, L:2 * L], even_odd[:, 1:2],
                                         evenT[:, t, :], ALU.mult, ALU.add).then_inc(sum_s, 1)

            def divide_self(n, t):
                b = WORK_OF[f"AVs{t}"]
                dve.wait_ge(sum_s, n.times(KT, t + 1))
                wait_fill(dve, (n.back(1), "Os"))
                dve.tensor_tensor(attnT[:, t, :], sumT[:, t, :], work[b][:, 2 * L:3 * L], ALU.mult)\
                    .then_inc(drained[b], 1)

            def pick_cross(n):
                dve.wait_ge(even_x, n.times(1, 1))
                wait_fill(dve, (n.back(1), "Ox"))
                dve.scalar_tensor_tensor(OxT[:], outX[:, :, L:2 * L], even_odd[:, 1:2], evenX[:],
                                         ALU.mult, ALU.add).then_inc(oxT_done, 1)

            def residual(n, k):
                use, sum_, add = (("Os", r1, xb), ("Ox", r2, x1b[n.par]))[k]
                b = WORK_OF[use]
                dve.wait_ge((xb_done, x1b_done)[k], n.times(1, 1))
                wait_fill(dve, (n, use))
                dve.tensor_tensor(sum_[:], work[b][0:L, 0:D], add[:], ALU.add).then_inc(drained[b], 1)

            def moments(n, k):
                wait_drain(dve, (n, ("Os", "Ox")[k]))
                dve.bn_stats(stats[k][:], (r1, r2)[k][:]).then_inc(bn_done[k], 1)

            def mean_variance(n, k):
                dve.wait_ge(bn_done[k], n.times(1, 1))
                dve.memset(carrier[:], 0.0)
                dve.bn_aggr(mv[k][:], stats[k][:]).then_inc(mv_done[k], 1)

            def add_eps(n, k):
                dve.wait_ge(mv_done[k], n.times(1, 1))
                dve.tensor_scalar(vare[k][:], mv[k][:, 1:2], EPS, None, ALU.add).then_inc(var_done[k], 1)

            def norm_self(n):
                dve.wait_ge(rstd_done[0], n.times(1, 1))
                wait_fill(dve, (n.back(1), "x1T"))
                wait(dve, x1b_done, n.back(1).times(1, 1))
                dve.tensor_scalar(x1[:], r1[:], mv[0][:, 0:1], rstd[0][:, 0:1], ALU.subtract, ALU.mult)\
                    .then_inc(x1_done, 1)

            def norm_cross(n):
                dve.wait_ge(rstd_done[1], n.times(1, 1))
                wait_fill(dve, (n.back(1), "x2T"))
                wait(dve, x2_saved, n.times(16))
                dve.tensor_scalar(x2[:], r2[:], mv[1][:, 0:1], rstd[1][:, 0:1], ALU.subtract, ALU.mult)\
                    .then_inc(x2_done, 1)

            def largest(n):
                dve.wait_ge(x2_done, n.times(1, 1))
                dve.tensor_reduce(xmax_all[0:L, bass.ds(n.times(1), 1)], x2[:], AX.X, ALU.max,
                                  apply_absolute_value=True).then_inc(xmax_done, 1)

            def step(n0, n1, n2, n3, n4, n5):
                if n4:
                    max_self(n4, 0)
                if n3:
                    norm_self(n3)
                if n2:
                    sum_cross(n2, 3)
                    normalise_values(n2, 2)
                if n3:
                    values_with_bias(n3, 1)
                if n1:
                    moments(n1, 1)
                if n2:
                    max_cross(n2, 4)
                    reciprocal_cross(n2, 3)
                if n3:
                    lo_keys_cross(n3, 1)
                    lo_with_bias(n3, "Qx", Qx[1], Qx[0], bcol["xbq"], qx_hi)
                if n4:
                    reciprocal_self(n4, 0)
                if n2:
                    normalise_values(n2, 3)
                if n4:
                    max_self(n4, 1)
                if n2:
                    sum_cross(n2, 4)
                    max_cross(n2, 5)
                if n3:
                    values_with_bias(n3, 2)
                if n2:
                    reciprocal_cross(n2, 4)
                if n4:
                    spread_reciprocal(n4, 0)
                if n2:
                    normalise_values(n2, 4)
                if n0:
                    largest(n0)
                if n1:
                    mean_variance(n1, 1)
                if n5:
                    lo_with_bias(n5, "Ks", Ks[1], Ks[0], bcol["abk"], ks_hi)
                if n3:
                    max_cross(n3, 0)
                if n4:
                    lo_context(n4, 0)
                    reciprocal_self(n4, 1)
                if n2:
                    sum_cross(n2, 5)
                    reciprocal_cross(n2, 5)
                if n4:
                    pick_self(n4, 0)
                    spread_reciprocal(n4, 1)
                    divide_self(n4, 0)
                if n2:
                    normalise_values(n2, 5)
                if n3:
                    max_cross(n3, 1)
                    sum_cross(n3, 0)
                if n2:
                    pick_cross(n2)
                if n4:
                    pick_self(n4, 1)
                if n3:
                    reciprocal_cross(n3, 0)
                if n4:
                    divide_self(n4, 1)
                    lo_context(n4, 1)
                if n1:
                    add_eps(n1, 1)
                if n3:
                    normalise_values(n3, 0)
                    max_cross(n3, 2)
                if n5:
                    lo_with_bias(n5, "Qs", Qs[1], Qs[0], bcol["abq"], qs_hi)
                if n3:
                    sum_cross(n3, 1)
                if n4:
                    lo_keys_cross(n4, 0)
                if n3:
                    reciprocal_cross(n3, 1)
                if n1:
                    norm_cross(n1)
                if n4:
                    residual(n4, 0)
                if n3:
                    max_cross(n3, 3)
                    normalise_values(n3, 1)
                if n4:
                    moments(n4, 0)
                if n3:
                    sum_cross(n3, 2)
                if n4:
                    mean_variance(n4, 0)
                if n2:
                    residual(n2, 1)
                if n3:
                    reciprocal_cross(n3, 2)
                if n4:
                    values_with_bias(n4, 0)
                    add_eps(n4, 0)
            iterations(dve, step)

        @block.tensor
        def _(pe):
            pe.wait_ge(consts, 15)

            pe.wait_ge(bv_spread, 1)
            for k in range(KT):
                ins = pe.matmul(work[0][0:L, 0:D], x1T[:, k, :], w["aWo"][:, k, :], start=(k == 0), stop=(k == KT - 1))
            ins.then_inc(bv_product, 1)
            pe.wait_ge(bo_folded, 1)

            def fill(n, use, *sources):
                bank = WORK_OF[use]
                wait_drain(pe, *((n, s) for s in sources if WORK_OF[s] != bank))
                wait(pe, drained[bank], n.fills(use))
                return work[bank]

            def wait_slot(n, unit):
                last, batch = next(before(SLOT_USES[SLOT_OF[unit]], unit, n.off), (None, None))
                if last is not None:
                    old = Batch(n.pair, batch)
                    kind, u = last[0], int(last[1:])
                    wait(pe, *((exp_s, old.times(KT, u + 1)) if kind == "S" else (exp_c, old.times(NU, u + 1))))

            def three(dst, lhs, rhs, first, last):
                pe.matmul(dst, lhs[0], rhs[0], start=first, stop=False)
                pe.matmul(dst, lhs[0], rhs[1], start=False, stop=False)
                return pe.matmul(dst, lhs[1], rhs[0], start=False, stop=last)

            def transpose_rows(n, use, src):
                b = fill(n, use)
                for k in range(KT):
                    ins = pe.transpose(b[:, k * L:(k + 1) * L], src[:, k * P:(k + 1) * P], ident[0:L, 0:L])
                ins.then_inc(filled[WORK_OF[use]], 1)

            def transpose_x(n):
                pe.wait_ge(x_ld[n.par], n.loads())
                transpose_rows(n, "xT", x_in[n.par])

            def transpose_x1(n):
                pe.wait_ge(x1_done, n.times(1, 1))
                transpose_rows(n, "x1T", x1)

            def transpose_x2(n):
                pe.wait_ge(x2_done, n.times(1, 1))
                transpose_rows(n, "x2T", x2)

            def project_T(n, use, weight, src, source_use):
                b = fill(n, use, source_use)
                for m in range(KT):
                    for k in range(KT):
                        ins = pe.matmul(b[:, m * L:(m + 1) * L], weight[:, k, m * P:(m + 1) * P], src[:, k, :],
                                        start=(k == 0), stop=(k == KT - 1))
                ins.then_inc(filled[WORK_OF[use]], 1)

            def project(n, use, srcT, weight, *sources):
                b = fill(n, use, *sources)
                for k in range(KT):
                    ins = pe.matmul(b[0:L, 0:D], srcT[:, k, :], weight[:, k, :], start=(k == 0), stop=(k == KT - 1))
                ins.then_inc(filled[WORK_OF[use]], 1)

            def project_values_self(n):
                project(n, "Vs", xT, w["aWv"], "xT")

            def project_out_self(n):
                project(n, "Os", attnT, w["aWo"], "AVs0", "AVs1")

            def project_out_cross(n):
                pe.wait_ge(oxT_done, n.times(1, 1))
                project(n, "Ox", OxT, w["xWo"])

            def self_scores(n, t):
                wait_slot(n, f"S{t}")
                wait_drain(pe, (n, "Qs"))
                pe.wait_ge(kbd_done, n.times(KT, t + 1))
                for q in range(2):
                    j = 2 * t + q
                    dst = score[SLOT_OF[f"S{t}"]][0:L, q, 0:QW]
                    pe.matmul(dst, alibi_l[:], alibi_r[:, j * QW:(j + 1) * QW], start=True, stop=False)
                    rhs = [x[:, QUAD * j:QUAD * (j + 1), :].rearrange("p h k -> p (h k)") for x in Kbd]
                    ins = three(dst, [x[:, t, :] for x in Qs], rhs, False, True)
                ins.then_inc(scores_s, 1)

            def cross_scores(n, u):
                t, c = divmod(u, NC)
                wait_slot(n, f"C{u}")
                if c == 0:
                    wait_drain(pe, (n, f"K{t}"))
                    pe.wait_ge(qbd_done, n.times(KT, t + 1))
                for q in range(2):
                    j = 2 * t + q
                    rhs = [x[:, QUAD * j:QUAD * (j + 1), :].rearrange("p h l -> p (h l)") for x in Qbd]
                    dst = score[SLOT_OF[f"C{u}"]][0:C, q, 0:QW]
                    lhs = [x[:, t, c * C:(c + 1) * C] for x in KxT[n.par]]
                    ins = three(dst, lhs, rhs, True, True)
                ins.then_inc(scores_c, 1)

            def transpose_max(n, u):
                pe.wait_ge(nmax_c_done, n.times(NU, u + 1))
                wait(pe, nmaxT_copied, n.times(NU, u))
                pe.transpose(maxT[:, 0:C], nmax_c[u % 2][:], ident[0:C, 0:C]).then_inc(nmaxT_done, 1)

            def shift(n, u):
                pe.wait_ge(nmaxT_copied, n.times(NU, u + 1))
                for q in range(2):
                    ins = pe.matmul(score[SLOT_OF[f"C{u}"]][0:C, q, 0:QW], nmaxT[u % 2][:, 0:C],
                                    sel[:, q * QW:(q + 1) * QW], start=False, stop=True, skip_group_check=True)
                ins.then_inc(shifted, 1)

            def cross_values(n, u):
                t, c = divmod(u, NC)
                pe.wait_ge(vn_done, n.times(NU, u + 1))
                if u == 0:
                    wait(pe, oxT_done, n.times(1))
                for g in range(4):
                    ins = pe.matmul(outX[32 * g:32 * (g + 1), t, :],
                                    Vn[u % 2][:, 2 * g:2 * g + 2, :].rearrange("s h e -> s (h e)"),
                                    Px[u % 2][:, 2 * g:2 * g + 2, :].rearrange("s h l -> s (h l)"),
                                    start=(c == 0), stop=(c == NC - 1))
                ins.then_inc(av_done, 1)

            def transpose_ctx(n, k):
                use = f"ctxT{k}"
                b = fill(n, use)
                pe.wait_ge(ctx_ld[n.par], n.loads())
                for c in range(NC):
                    ins = pe.transpose(b[:, c * C:(c + 1) * C], ctx_in[n.par][:, c, k * P:(k + 1) * P], ident[0:C, 0:C])
                ins.then_inc(filled[WORK_OF[use]], 1)

            def keys_cross(n, m):
                use = f"K{m}"
                b = fill(n, use, "ctxT0", "ctxT1")
                for k in range(KT):
                    ins = three(b[:, 0:SP], [x[:, k, m * P:(m + 1) * P] for x in split["xWk"]],
                                [x[:, k, :] for x in ctxT], k == 0, k == KT - 1)
                ins.then_inc(filled[WORK_OF[use]], 1)

            def values_cross(n, c):
                use = f"V{c}"
                b = fill(n, use, "ctxT0", "ctxT1")
                for k in range(KT):
                    ins = three(b[0:C, 0:D], [x[:, k, c * C:(c + 1) * C] for x in ctxT],
                                [x[:, k, :] for x in split["xWv"]], k == 0, k == KT - 1)
                ins.then_inc(filled[WORK_OF[use]], 1)

            def transpose_probs(n, j):
                use = f"PT{j}"
                b = fill(n, use)
                pe.wait_ge(exp_s, n.times(KT, j // 2 + 1))
                for h in range(QUAD):
                    ins = pe.transpose(b[0:L, h * L:(h + 1) * L], Ps[:, QUAD * j + h, :], ident[0:L, 0:L])
                ins.then_inc(filled[WORK_OF[use]], 1)

            def self_values(n, t):
                use = f"AVs{t}"
                b = fill(n, use, "Vs", f"PT{2 * t}", f"PT{2 * t + 1}")
                pe.wait_ge(rzrep_s, n.times(KT, t + 1))
                pe.transpose(b[:, 2 * L:3 * L], rZrep[:, t].rearrange("q h e -> q (h e)"), ident[0:L, 0:L])
                for g in range(4):
                    h = OCT * t + 2 * g
                    ins = pe.matmul(b[32 * g:32 * (g + 1), 0:2 * L], Vs[:, h * HD:(h + 2) * HD],
                                    PsT[:, h:h + 2, :].rearrange("k h q -> k (h q)"), start=True, stop=True)
                ins.then_inc(filled[WORK_OF[use]], 1)

            def step(n0, n1, n2, n3, n4, n5):
                if n3:
                    values_cross(n3, 1)
                    transpose_x1(n3)
                if n2:
                    cross_scores(n2, 4)
                    cross_values(n2, 2)
                if n3:
                    keys_cross(n3, 1)
                if n2:
                    transpose_max(n2, 4)
                if n3:
                    project_T(n3, "Qx", w["xWq"], x1T, "x1T")
                if n2:
                    shift(n2, 4)
                if n4:
                    self_scores(n4, 1)
                    transpose_probs(n4, 0)
                if n5:
                    transpose_x(n5)
                if n2:
                    cross_scores(n2, 5)
                if n3:
                    values_cross(n3, 2)
                if n5:
                    project_T(n5, "Ks", w["aWk"], xT, "xT")
                if n2:
                    cross_values(n2, 3)
                    transpose_max(n2, 5)
                if n4:
                    transpose_probs(n4, 1)
                if n3:
                    cross_scores(n3, 0)
                if n4:
                    transpose_ctx(n4, 0)
                if n2:
                    shift(n2, 5)
                if n4:
                    transpose_probs(n4, 2)
                if n2:
                    cross_values(n2, 4)
                if n3:
                    transpose_max(n3, 0)
                if n4:
                    self_values(n4, 0)
                if n3:
                    shift(n3, 0)
                    cross_scores(n3, 1)
                if n4:
                    transpose_probs(n4, 3)
                    transpose_ctx(n4, 1)
                if n2:
                    cross_values(n2, 5)
                if n3:
                    transpose_max(n3, 1)
                if n4:
                    self_values(n4, 1)
                if n3:
                    shift(n3, 1)
                    cross_scores(n3, 2)
                if n5:
                    project_T(n5, "Qs", w["aWq"], xT, "xT")
                if n4:
                    keys_cross(n4, 0)
                if n3:
                    cross_values(n3, 0)
                    transpose_max(n3, 2)
                if n4:
                    project_out_self(n4)
                if n3:
                    shift(n3, 2)
                    cross_scores(n3, 3)
                if n1:
                    transpose_x2(n1)
                if n2:
                    project_out_cross(n2)
                if n4:
                    values_cross(n4, 0)
                if n3:
                    cross_values(n3, 1)
                    transpose_max(n3, 3)
                if n5:
                    self_scores(n5, 0)
                if n3:
                    shift(n3, 3)
                if n5:
                    project_values_self(n5)
            iterations(pe, step)


def feed_forward(nc, out, x2_dram, ident, x2T_all, xmax_all, wT, w_down):
    with ExitStack() as keep:
        U = keep.enter_context(nc.sbuf_tensor("U", [P, NG, FT, GT], F32))
        up_q = keep.enter_context(nc.sbuf_tensor("up_q", [P, NG, FT, GT], I16))
        tiny = {n: keep.enter_context(nc.sbuf_tensor(n, [P, 1], F32)) for n in (
            "x_scale", "x_inv", "up_scale", "up_inv", "gate_scale", "gate_inv",
            "glu_unit", "glu_scale", "glu_inv", "h_unit", "h_scale", "h_inv")}
        ones = keep.enter_context(nc.sbuf_tensor("ones", [P, P], F32))
        up_and_gate(nc, x2T_all, xmax_all, wT, ident, ones, U, up_q, tiny)
        gate_and_down(nc, out, x2_dram, x2T_all, ident, ones, wT, w_down, U, up_q, tiny)


class GlobalMax:

    def __init__(self, ctx, nc, name, ones, ident, bank):
        self.ones, self.ident, self.bank = ones, ident, bank
        self.diag = ctx.enter_context(nc.sbuf_tensor(f"{name}_diag", [P, P], F32))
        self.col = ctx.enter_context(nc.sbuf_tensor(f"{name}_col", [P, 1], F32))
        self.top = ctx.enter_context(nc.sbuf_tensor(f"{name}_top", [P, 1], F32))
        self.col_done = ctx.enter_context(nc.semaphore(f"{name}_col_done"))
        self.diag_done = ctx.enter_context(nc.semaphore(f"{name}_diag_done"))
        self.spread = ctx.enter_context(nc.semaphore(f"{name}_spread"))
        self.top_done = ctx.enter_context(nc.semaphore(f"{name}_top_done"))

    def vector(self, dve, maxima):
        dve.tensor_reduce(self.col[:], maxima, AX.X, ALU.max).then_inc(self.col_done, 1)
        dve.wait_ge(self.col_done, 1)
        dve.tensor_scalar(self.diag[:], self.ident[:], self.col[:, 0:1], None, ALU.mult).then_inc(self.diag_done, 1)
        dve.wait_ge(self.spread, 1)
        dve.tensor_reduce(self.top[:], self.bank, AX.X, ALU.max).then_inc(self.top_done, 1)
        dve.wait_ge(self.top_done, 1)

    def tensor(self, pe):
        pe.wait_ge(self.diag_done, 1)
        pe.matmul(self.bank, self.ones[:], self.diag[:], start=True, stop=True).then_inc(self.spread, 1)


def up_and_gate(nc, x2T_all, xmax_all, wT, ident, ones, U, up_q, tiny):
    with ExitStack() as ctx:
        def sb(name, shape, dt=F32):
            return ctx.enter_context(nc.sbuf_tensor(name, shape, dt))

        def sem(name):
            return ctx.enter_context(nc.semaphore(name))

        xq = sb("xq", [P, KT, GT], I16)
        xh = [[sb(f"xq{q}_{p}", [P, KT, GT], F32R) for p in ("hi", "lo")] for q in range(2)]
        maxima = [sb(f"maxima{p}", [P, NG]) for p in range(2)]
        bank = [ctx.enter_context(nc.psum_tensor(f"ubank{m}", [P, BANK], F32)) for m in range(FT)]
        spread = [ctx.enter_context(nc.psum_tensor(f"spread{p}", [P, BANK], F32)) for p in range(2)]
        ones_done, x_inv_done, steps = sem("ones_done"), sem("x_inv_done"), sem("steps")
        xq_done, xpart_done = sem("xq_done"), sem("xpart_done")
        x_parts = sem("x_parts")
        product = [sem(f"product{m}") for m in range(FT)]
        stored = [sem(f"stored{m}") for m in range(FT)]
        maxed = sem("maxed")
        up_q_done = sem("up_q_done")
        top = [GlobalMax(ctx, nc, n, ones, ident, spread[k % 2][:, 0:P])
               for k, n in enumerate(("x_top", "up_top", "gate_top"))]
        block = ctx.enter_context(nc.Block())

        def xpart(g, part_):
            return x2T_all[:].bitcast(I16)[:, :, bass.ds(g.times(2 * GT, part_ * GT), GT)]

        class Group:
            def __init__(self, which, pair, off):
                self.which, self.pair, self.off, self.par = which, pair, off, off % 2
                self.g = Batch(pair, off)

            def count(self, more=0):
                return self.g.times(1, NG * self.which + more)

        def groups(eng, which, step):
            if which == 0:
                step(Group(0, 0, 0))
                step(Group(0, 0, 1))
                with eng.Fori(0, NG // 2 - 1) as r:
                    step(Group(0, r, 2))
                    step(Group(0, r, 3))
            else:
                with eng.Fori(0, NG // 2) as r:
                    step(Group(1, r, 0))
                    step(Group(1, r, 1))

        @block.gpsimd
        def _(pool):
            pool.memset(ones[:], 1.0).then_inc(ones_done, 1)

        @block.scalar
        def _(act):
            def float_parts(g, par, made, used):
                if made is not None:
                    act.wait_ge(xpart_done, made)
                wait(act, product[FT - 1], used)
                act.activation(xh[par][0][:], xpart(g, 0), ACT.Copy)
                act.activation(xh[par][1][:], xpart(g, 1), ACT.Copy).then_inc(x_parts, 1)

            def step(s, wraps=False, last=False):
                if not last:
                    float_parts(Batch(0, 0) if wraps else s.g.plus(1), 1 - s.par,
                            s.count(2) if s.which == 0 and not wraps else None, s.count())
                if s.which == 1:
                    act.wait_ge(up_q_done, s.g.times(1, 1))
                for m in range(FT):
                    act.wait_ge(product[m], s.count(1))
                    act.activation(U[:, bass.ds(s.g.times(1), 1), m, :].rearrange("p o t -> p (o t)"),
                                   bank[m][:, 0:GT], ACT.Copy).then_inc(stored[m], 1)

            float_parts(Batch(0, 0), 0, 1, 0)
            step(Group(0, 0, 0))
            step(Group(0, 0, 1))
            with act.Fori(0, NG // 2 - 2) as r:
                step(Group(0, r, 2))
                step(Group(0, r, 3))
            step(Group(0, 0, NG - 2))
            step(Group(0, 0, NG - 1), wraps=True)
            with act.Fori(0, NG // 2 - 1) as r:
                step(Group(1, r, 0))
                step(Group(1, r, 1))
            step(Group(1, 0, NG - 2))
            step(Group(1, 0, NG - 1), last=True)

        @block.vector
        def _(dve):
            def quantiser(top_, scale, inv, base):
                dve.tensor_scalar(tiny[scale][:], top_.top[:], 1.0 / QMAX, TINY, ALU.mult, ALU.max).then_inc(steps, 1)
                dve.wait_ge(steps, base + 1)
                dve.reciprocal(tiny[inv][:], tiny[scale][:]).then_inc(steps, 1)
                dve.wait_ge(steps, base + 2)

            def quantise_x(g, count):
                wait(dve, xpart_done, count)
                dve.tensor_scalar(xq[:], x2T_all[:, :, bass.ds(g.times(GT), GT)], tiny["x_inv"][:, 0:1], None,
                                  ALU.mult).then_inc(xq_done, 1)
                dve.wait_ge(xq_done, count + 1)
                dve.tensor_scalar(xpart(g, 0), xq[:], HIGH, None, ALU.bitwise_and)
                dve.tensor_scalar(xpart(g, 1), xq[:], LOW, None, ALU.bitwise_and).then_inc(xpart_done, 1)

            def step(s, ahead=True):
                if s.which == 0 and ahead:
                    quantise_x(s.g.plus(1), s.count(1))
                if s.which == 1:
                    dve.tensor_scalar(up_q[:, bass.ds(s.g.times(1), 1)], U[:, bass.ds(s.g.times(1), 1)],
                                      tiny["up_inv"][:, 0:1], None, ALU.mult).then_inc(up_q_done, 1)
                dve.wait_ge(stored[FT - 1], s.count(1))
                dve.tensor_reduce(maxima[s.which][:, bass.ds(s.g.times(1), 1)], U[:, bass.ds(s.g.times(1), 1)],
                                  AX.XYZ, ALU.max, apply_absolute_value=True).then_inc(maxed, 1)

            top[0].vector(dve, xmax_all[:])
            quantiser(top[0], "x_scale", "x_inv", 0)
            quantise_x(Batch(0, 0), 0)
            step(Group(0, 0, 0))
            step(Group(0, 0, 1))
            with dve.Fori(0, NG // 2 - 2) as r:
                step(Group(0, r, 2))
                step(Group(0, r, 3))
            step(Group(0, 0, NG - 2))
            step(Group(0, 0, NG - 1), ahead=False)
            dve.wait_ge(maxed, NG)
            top[1].vector(dve, maxima[0][:])
            dve.tensor_scalar(tiny["up_scale"][:], top[1].top[:], tiny["x_scale"][:, 0:1], None, ALU.mult)\
                .then_inc(steps, 1)
            dve.wait_ge(steps, 3)
            dve.tensor_scalar(tiny["up_scale"][:], tiny["up_scale"][:], 1.0 / QMAX, TINY, ALU.mult, ALU.max)\
                .then_inc(steps, 1)
            dve.wait_ge(steps, 4)
            dve.reciprocal(tiny["up_inv"][:], tiny["up_scale"][:]).then_inc(steps, 1)
            dve.wait_ge(steps, 5)
            dve.tensor_scalar(tiny["up_inv"][:], tiny["up_inv"][:], tiny["x_scale"][:, 0:1], None, ALU.mult)\
                .then_inc(steps, 1)
            dve.wait_ge(steps, 6)
            groups(dve, 1, step)
            dve.wait_ge(maxed, 2 * NG)
            top[2].vector(dve, maxima[1][:])
            dve.tensor_scalar(tiny["gate_scale"][:], top[2].top[:], tiny["x_scale"][:, 0:1], None, ALU.mult)\
                .then_inc(steps, 1)
            dve.wait_ge(steps, 7)
            dve.tensor_scalar(tiny["gate_scale"][:], tiny["gate_scale"][:], 1.0 / QMAX, TINY, ALU.mult, ALU.max)\
                .then_inc(steps, 1)
            dve.wait_ge(steps, 8)
            dve.reciprocal(tiny["gate_inv"][:], tiny["gate_scale"][:]).then_inc(steps, 1)
            dve.wait_ge(steps, 9)
            dve.tensor_scalar(tiny["gate_inv"][:], tiny["gate_inv"][:], tiny["x_scale"][:, 0:1], None, ALU.mult)\
                .then_inc(steps, 1)

        @block.tensor
        def _(pe):
            def step(s):
                w = wT["w_up" if s.which == 0 else "w_gate"]
                pe.wait_ge(x_parts, s.count(1))
                for m in range(FT):
                    wait(pe, stored[m], s.count())
                    for k in range(KT):
                        lhs = [x[:, k, m * P:(m + 1) * P] for x in w]
                        rhs = [x[:, k, :] for x in xh[s.par]]
                        dst = bank[m][:, 0:GT]
                        pe.matmul(dst, lhs[0], rhs[0], start=(k == 0), stop=False)
                        pe.matmul(dst, lhs[0], rhs[1], start=False, stop=False)
                        ins = pe.matmul(dst, lhs[1], rhs[0], start=False, stop=(k == KT - 1))
                    ins.then_inc(product[m], 1)

            pe.wait_ge(ones_done, 1)
            top[0].tensor(pe)
            groups(pe, 0, step)
            top[1].tensor(pe)
            groups(pe, 1, step)
            top[2].tensor(pe)


def gate_and_down(nc, out, x2_dram, x2T_all, ident, ones, wT, w_down, U, up_q, tiny):
    TG = GT // L
    AHEAD = 3
    with ExitStack() as ctx:
        def sb(name, shape, dt=F32):
            return ctx.enter_context(nc.sbuf_tensor(name, shape, dt))

        def sem(name):
            return ctx.enter_context(nc.semaphore(name))

        HG = FT // 2
        flat = {n: [t[:].rearrange("p k n -> p (k n)") for t in wT[n]] for n in wT}
        wd = [t.rearrange("p (m n) -> p m n", m=FT) for t in flat["w_up"]]
        room = x2T_all[:].rearrange("p k n -> p (k n)")
        spare = w_down[:].rearrange("p k n -> p (k n)")
        sig1 = spare[:, 0:HG * GT].rearrange("p (m t) -> p m t", m=HG)
        sig = [room[:, 0:HG * GT].rearrange("p (m t) -> p m t", m=HG),
               sig1]
        tiles = [room[0:L, HG * GT + k * D:HG * GT + (k + 1) * D] for k in range(TG + 4)]
        x2, r, res = tiles[:TG], tiles[TG:TG + 2], tiles[TG + 2:]
        ints = [room[:, HG * GT + len(tiles) * D + k * (HG * GT // 2):][:, 0:HG * GT // 2] for k in range(4)]
        gate_q = [v.bitcast(I16).rearrange("p (m t) -> p m t", m=HG) for v in ints[:2]]
        sig_q = [v.bitcast(U16).rearrange("p (m t) -> p m t", m=HG) for v in ints[2:]]
        maxima = [sb(f"hmaxima{p}", [P, 2 * NG]) for p in range(2)]
        hq = [sb(f"hq{q}", [P, FT, L], I16) for q in range(2)]
        whole = [spare[:, q * FT * L:(q + 1) * FT * L].rearrange("p (m t) -> p m t", m=FT) for q in range(2)]
        free = flat["w_gate"] + [sb(f"hh{t}", [P, 2 * FT * L], F32R)[:] for t in (2, 3)]
        hh = [[f[:, k * FT * L:(k + 1) * FT * L].rearrange("p (m t) -> p m t", m=FT) for k in range(2)] for f in free]
        carrier = sb("fcarrier", [1, 1])
        stats = [sb(f"fstats{p}", [L, 6]) for p in range(2)]
        mv = [sb(f"fmv{p}", [L, 2]) for p in range(2)]
        vare = [sb(f"fvare{p}", [L, 1]) for p in range(2)]
        rstd = [sb(f"frstd{p}", [L, 1]) for p in range(2)]
        half = sb("fhalf", [L, 1])
        wbank = [ctx.enter_context(nc.psum_tensor(f"dbank{p}", [P, BANK], F32)) for p in range(2)]
        obank = [ctx.enter_context(nc.psum_tensor(f"obank{p}", [P, BANK], F32)) for p in range(4)]
        spread = [ctx.enter_context(nc.psum_tensor(f"dspread{p}", [P, BANK], F32)) for p in range(2)]
        half_done, steps = sem("half_done"), sem("dsteps")
        turned, hi_done, lo_done = sem("dturned"), sem("dhi_done"), sem("dlo_done")
        gate_q_done, sig_done, sig_q_done = sem("gate_q_done"), sem("sig_done"), sem("sig_q_done")
        glu_done, glu_maxed = sem("glu_done"), sem("glu_maxed")
        glu_q_done, h_done, h_maxed = sem("glu_q_done"), sem("h_done"), sem("h_maxed")
        hq_done, whole_done, hi_halves, lo_halves = (sem(n) for n in ("hq_done", "whole_done", "hi_halves", "lo_halves"))
        down_done, resid_done, fbn_done, fmv_done = sem("down_done"), sem("resid_done"), sem("fbn_done"), sem("fmv_done")
        fvar_done, frstd_done, res_done = sem("fvar_done"), sem("frstd_done"), sem("res_done")
        x2_ld = [sem(f"x2_ld{t}") for t in range(TG)]
        out_st = [sem(f"out_st{p}") for p in range(2)]
        top = [GlobalMax(ctx, nc, n, ones, ident, spread[k][:, 0:P]) for k, n in enumerate(("glu_top", "h_top"))]
        glu_q = gate_q
        block = ctx.enter_context(nc.Block())
        NH = 2 * NG

        def part(t, pair, h):
            return t[:, bass.ds(pair, 1), h * HG:(h + 1) * HG, :].rearrange("p o m t -> p (o m) t")

        @block.sync
        def _(sp):
            def load(n, par):
                sp.dma_start(x2[par], x2_dram[bass.ds(n, 1)].rearrange("o l d -> (o l) d")).then_inc(x2_ld[par], 16)

            def store(n, par, count):
                sp.wait_ge(res_done, count)
                sp.dma_start(out[bass.ds(n, 1)].rearrange("o l d -> (o l) d"), res[par]).then_inc(out_st[par], 16)

            for t in range(TG):
                load(t, t)
            with sp.Fori(0, NG - 1) as g:
                for t in range(TG):
                    sp.wait_ge(resid_done, g * TG + (t + 1))
                    load(g * TG + (t + TG), t)
                    store(g * TG + t, t % 2, g * TG + (t + 1))
            for t in range(TG):
                store(B - TG + t, t % 2, B - TG + t + 1)
            for p in range(2):
                sp.wait_ge(out_st[p], 16 * (B // 2))

        @block.gpsimd
        def _(pool):
            pool.memset(half[:], -0.5).then_inc(half_done, 1)
            pool.wait_ge(half_done, 1)

            def root(count, p):
                pool.wait_ge(fvar_done, count)
                pool.tensor_tensor(rstd[p][:], vare[p][:], half[:], ALU.pow).then_inc(frstd_done, 1)

            def lo_half(n, t):
                pool.wait_ge(hi_halves, n + 1)
                pool.tensor_tensor(hh[t][1], whole[t % 2], hh[t][0].bitcast(F32), ALU.subtract).then_inc(lo_halves, 1)

            for t in range(AHEAD):
                lo_half(t, t)
            with pool.Fori(0, NG - 1) as g:
                for t in range(TG):
                    lo_half(g * TG + (t + AHEAD), (t + AHEAD) % TG)
                    root(g * TG + (t + 1), t % 2)
            for t in range(TG):
                if t + AHEAD < TG:
                    lo_half(B - TG + t + AHEAD, t + AHEAD)
                root(B - TG + t + 1, t % 2)

        @block.scalar
        def _(act):
            for f in range(4):
                act.wait_ge(turned, f + 1)
                act.activation(wd[0][:, (f % 2) * HG:(f % 2 + 1) * HG, (f // 2) * P:(f // 2 + 1) * P],
                               wbank[f % 2][:, 0:HG * P].rearrange("p (m n) -> p m n", m=HG), ACT.Copy)\
                    .then_inc(hi_done, 1)

            def sigmoid(q, h, first):
                if not (first or isinstance(q, int)):
                    act.wait_ge(glu_done, q * 2 + (h - 1))
                act.activation(gate_q[h], part(U, q, h), ACT.Copy, scale=tiny["gate_inv"][:, 0:1]).then_inc(gate_q_done, 1)
                act.wait_ge(gate_q_done, q * 2 + (h + 1))
                if not (first or isinstance(q, int)):
                    act.wait_ge(sig_q_done, q * 2 + (h - 1))
                act.activation(sig[h], gate_q[h], ACT.Sigmoid, scale=tiny["gate_scale"][:, 0:1]).then_inc(sig_done, 1)

            sigmoid(0, 0, True)
            sigmoid(0, 1, False)
            with act.Fori(1, NG) as q:
                sigmoid(q, 0, False)
                sigmoid(q, 1, False)

            def glu_ints(q, h, first):
                if not first:
                    act.wait_ge(h_done, q * 2 + (h - 1))
                act.activation(glu_q[h], part(U, q, h), ACT.Copy, scale=tiny["glu_inv"][:, 0:1])\
                    .then_inc(glu_q_done, 1)

            act.wait_ge(steps, 5)
            glu_ints(0, 0, True)
            glu_ints(0, 1, True)
            with act.Fori(1, NG) as q:
                glu_ints(q, 0, False)
                glu_ints(q, 1, False)

            def tile(n, t):
                p = t % 2
                act.wait_ge(hq_done, n + 1)
                wait(act, lo_halves, n - 1)
                act.activation(whole[p], hq[p][:], ACT.Copy).then_inc(whole_done, 1)
                wait(act, down_done, n - (TG - 1))
                act.activation(hh[t][0], hq[p][:], ACT.Copy).then_inc(hi_halves, 1)

            for t in range(TG):
                tile(t, t)
            with act.Fori(1, NG) as g:
                for t in range(TG):
                    tile(g * TG + t, t)

        @block.vector
        def _(dve):
            for f in range(4):
                dst = [w[:, (f % 2) * HG:(f % 2 + 1) * HG, (f // 2) * P:(f // 2 + 1) * P] for w in wd]
                dve.wait_ge(hi_done, f + 1)
                dve.tensor_tensor(dst[1], wbank[f % 2][:, 0:HG * P].rearrange("p (m n) -> p m n", m=HG),
                                  dst[0].bitcast(F32), ALU.subtract).then_inc(lo_done, 1)

            def sigmoid_ints(q, h):
                dve.wait_ge(sig_done, q * 2 + (h + 1))
                dve.tensor_scalar(sig_q[h], sig[h], SIGQ, None, ALU.mult).then_inc(sig_q_done, 1)

            def glu(q, h):
                dve.wait_ge(sig_q_done, q * 2 + (h + 1))
                dve.tensor_tensor(part(U, q, h), gate_q[h], sig_q[h], ALU.mult).then_inc(glu_done, 1)

            def largest(q, h, k, done, maxed_):
                dve.wait_ge(done, q * 2 + (h + 1))
                dve.tensor_reduce(maxima[k][:, bass.ds(q * 2 + h, 1)], part(U, q, h), AX.XY, ALU.max,
                                  apply_absolute_value=True).then_inc(maxed_, 1)

            sigmoid_ints(0, 0)
            glu(0, 0)
            sigmoid_ints(0, 1)
            largest(0, 0, 0, glu_done, glu_maxed)
            glu(0, 1)
            with dve.Fori(1, NG) as q:
                for h in range(2):
                    sigmoid_ints(q, h)
                    largest(q if h else q - 1, 1 - h, 0, glu_done, glu_maxed)
                    glu(q, h)
            largest(NG - 1, 1, 0, glu_done, glu_maxed)
            dve.wait_ge(glu_maxed, NH)
            top[0].vector(dve, maxima[0][:])

            dve.tensor_scalar(tiny["glu_unit"][:], tiny["gate_scale"][:], 1.0 / SIGQ, None, ALU.mult).then_inc(steps, 1)
            dve.wait_ge(steps, 1)
            dve.tensor_scalar(tiny["glu_scale"][:], top[0].top[:], tiny["glu_unit"][:, 0:1], None, ALU.mult)\
                .then_inc(steps, 1)
            dve.wait_ge(steps, 2)
            dve.tensor_scalar(tiny["glu_scale"][:], tiny["glu_scale"][:], 1.0 / QMAX, TINY, ALU.mult, ALU.max)\
                .then_inc(steps, 1)
            dve.wait_ge(steps, 3)
            dve.reciprocal(tiny["glu_inv"][:], tiny["glu_scale"][:]).then_inc(steps, 1)
            dve.wait_ge(steps, 4)
            dve.tensor_scalar(tiny["glu_inv"][:], tiny["glu_inv"][:], tiny["glu_unit"][:, 0:1], None, ALU.mult)\
                .then_inc(steps, 1)

            def hidden(q, h):
                dve.wait_ge(glu_q_done, q * 2 + (h + 1))
                dve.tensor_tensor(part(U, q, h), glu_q[h], part(up_q, q, h), ALU.mult).then_inc(h_done, 1)

            hidden(0, 0)
            hidden(0, 1)
            largest(0, 0, 1, h_done, h_maxed)
            with dve.Fori(1, NG) as q:
                for h in range(2):
                    hidden(q, h)
                    largest(q if h else q - 1, 1 - h, 1, h_done, h_maxed)
            largest(NG - 1, 1, 1, h_done, h_maxed)
            dve.wait_ge(h_maxed, NH)
            top[1].vector(dve, maxima[1][:])
            dve.tensor_scalar(tiny["h_unit"][:], tiny["glu_scale"][:], tiny["up_scale"][:, 0:1], None, ALU.mult)\
                .then_inc(steps, 1)
            dve.wait_ge(steps, 6)
            dve.tensor_scalar(tiny["h_scale"][:], top[1].top[:], tiny["h_unit"][:, 0:1], None, ALU.mult)\
                .then_inc(steps, 1)
            dve.wait_ge(steps, 7)
            dve.tensor_scalar(tiny["h_scale"][:], tiny["h_scale"][:], 1.0 / QMAX, TINY, ALU.mult, ALU.max)\
                .then_inc(steps, 1)
            dve.wait_ge(steps, 8)
            dve.reciprocal(tiny["h_inv"][:], tiny["h_scale"][:]).then_inc(steps, 1)
            dve.wait_ge(steps, 9)
            dve.tensor_scalar(tiny["h_inv"][:], tiny["h_inv"][:], tiny["h_unit"][:, 0:1], None, ALU.mult)\
                .then_inc(steps, 1)
            dve.wait_ge(steps, 10)

            def hidden_ints(g, t, p, made):
                wait(dve, hi_halves, made - 1)
                dve.tensor_scalar(hq[p][:], U[:, bass.ds(g, 1), :, t * L:(t + 1) * L].rearrange("p o m t -> p (o m) t"),
                                  tiny["h_inv"][:, 0:1], None, ALU.mult).then_inc(hq_done, 1)

            def residual(count, loads, t):
                p = t % 2
                dve.wait_ge(down_done, count)
                dve.wait_ge(x2_ld[t], loads)
                wait(dve, res_done, count - 2)
                dve.scalar_tensor_tensor(r[p], obank[t][0:L, 0:D], tiny["h_scale"][:, 0:1][0:L], x2[t],
                                         ALU.mult, ALU.add).then_inc(resid_done, 1)
                dve.wait_ge(resid_done, count)
                dve.bn_stats(stats[p][:], r[p]).then_inc(fbn_done, 1)
                dve.wait_ge(fbn_done, count)
                dve.memset(carrier[:], 0.0)
                dve.bn_aggr(mv[p][:], stats[p][:]).then_inc(fmv_done, 1)
                dve.wait_ge(fmv_done, count)
                dve.tensor_scalar(vare[p][:], mv[p][:, 1:2], EPS, None, ALU.add).then_inc(fvar_done, 1)

            def norm(count, p, stored):
                dve.wait_ge(frstd_done, count)
                wait(dve, out_st[p], stored)
                dve.tensor_scalar(res[p], r[p], mv[p][:, 0:1], rstd[p][:, 0:1], ALU.subtract, ALU.mult)\
                    .then_inc(res_done, 1)

            def integers_ahead(g, t):
                later, u = divmod(t + AHEAD, TG)
                hidden_ints(g + later, u, u % 2, g * TG + (t + AHEAD))

            for t in range(AHEAD):
                hidden_ints(0, t, t % 2, t)
            for t in range(TG):
                integers_ahead(0, t)
                residual(t + 1, 16, t)
                if t:
                    norm(t, (t - 1) % 2, 16 * ((t - 1) // 2))
            with dve.Fori(1, NG - 1) as g:
                for t in range(TG):
                    integers_ahead(g, t)
                    residual(g * TG + (t + 1), g * 16 + 16, t)
                    norm(g * TG + t, (t - 1) % 2, g * (8 * TG) + 16 * ((t - 1) // 2))
            g = NG - 1
            for t in range(TG):
                if t + AHEAD < TG:
                    integers_ahead(g, t)
                residual(g * TG + t + 1, g * 16 + 16, t)
                norm(g * TG + t, (t - 1) % 2, g * (8 * TG) + 16 * ((t - 1) // 2))
            norm(B, 1, 16 * (B // 2 - 1))

        @block.tensor
        def _(pe):
            for f in range(4):
                if f >= 2:
                    pe.wait_ge(lo_done, f - 1)
                for j in range(HG):
                    m = (f % 2) * HG + j
                    ins = pe.transpose(wbank[f % 2][:, j * P:(j + 1) * P], w_down[:, f // 2, m * P:(m + 1) * P], ident[:])
                ins.then_inc(turned, 1)
            pe.wait_ge(lo_done, 4)
            top[0].tensor(pe)
            top[1].tensor(pe)

            def tile(n, t):
                pe.wait_ge(lo_halves, n + 1)
                wait(pe, resid_done, n - (TG - 1))
                for m in range(FT):
                    lhs, rhs = [x[:, m, :] for x in hh[t]], [x[:, m, :] for x in wd]
                    dst = obank[t][0:L, 0:D]
                    pe.matmul(dst, lhs[0], rhs[0], start=(m == 0), stop=False)
                    pe.matmul(dst, lhs[0], rhs[1], start=False, stop=False)
                    ins = pe.matmul(dst, lhs[1], rhs[0], start=False, stop=(m == FT - 1))
                ins.then_inc(down_done, 1)

            for t in range(TG):
                tile(t, t)
            with pe.Fori(1, NG) as g:
                for t in range(TG):
                    tile(g * TG + t, t)


_INS = {"x": "x", "ctx_1024": "ctx",
        "L0_attn_Wq": "aWq", "L0_attn_Wk": "aWk", "L0_attn_Wv": "aWv", "L0_attn_Wo": "aWo",
        "L0_attn_bq": "a_bq", "L0_attn_bk": "a_bk", "L0_attn_bv": "a_bv", "L0_attn_bo": "a_bo",
        "L0_xattn_Wq": "xWq", "L0_xattn_Wk": "xWk", "L0_xattn_Wv": "xWv", "L0_xattn_Wo": "xWo",
        "L0_xattn_bq": "x_bq", "L0_xattn_bk": "x_bk", "L0_xattn_bv": "x_bv", "L0_xattn_bo": "x_bo",
        "L0_ffn_w_gate": "w_gate", "L0_ffn_w_up": "w_up", "L0_ffn_w_down": "w_down"}


def shape_constants():
    bf16 = mybir.dt.np(BF16)

    def pieces(v):
        got, rest = [], v.astype(np.float32)
        for _ in range(3):
            got.append(rest.astype(bf16))
            rest = (rest - got[-1].astype(np.float32)).astype(np.float32)
        return got

    row = np.arange(P)
    slopes = (np.float32(1.0) / np.float32(2.0) ** (np.arange(H, dtype=np.float32) / np.float32(H))).astype(np.float32)
    key = np.arange(L, dtype=np.float32)
    sel = np.zeros((P, OCT * L), np.float32)
    for h in range(OCT):
        sel[h, h * L:(h + 1) * L] = 1.0
    alibi_l = np.stack([np.ones(L)] * 3 + [-key] * 3).astype(bf16)
    alibi_r = np.stack([p.reshape(-1) for p in pieces(slopes[:, None] * key[None, :])]
                       + [np.repeat(p, L) for p in pieces(slopes)])
    return {"ident": np.eye(P, dtype=np.float32),
            "mask8": (row[:, None] // HD == np.arange(OCT)[None, :]).astype(np.float32),
            "even_odd": np.stack([(row // HD) % 2 == 0, (row // HD) % 2 == 1], 1).astype(np.float32),
            "sel": sel, "alibi_l": alibi_l, "alibi_r": alibi_r.astype(bf16)}


def kernel(**inputs):
    import concourse.bacc as _bacc
    from concourse.bass_utils import run_bass_kernel_spmd as _run

    nc = _bacc.Bacc("TRN2", target_bir_lowering=False, num_devices=1)
    arrays, aps = {}, {}
    given = {short: np.ascontiguousarray(inputs[name]) for name, short in _INS.items()}
    given.update(shape_constants())
    for short, v in given.items():
        arrays[f"in_{short}"] = v
        aps[short] = nc.dram_tensor(f"in_{short}", v.shape, mybir.dt.from_np(v.dtype), kind="ExternalInput").ap()
    out = nc.dram_tensor("out_0", (B, L, D), F32, kind="ExternalOutput").ap()
    x2_dram = nc.dram_tensor("x2_scratch", (B, L, D), F32, kind="Internal").ap()
    decoder(nc, aps, out, x2_dram)
    r = _run(nc, [arrays], core_ids=[0])
    return r.results[0]["out_0"]
```

```python
from contextlib import ExitStack

import numpy as np
import concourse.bass as bass
from concourse import mybir

F32 = mybir.dt.float32
F32R = mybir.dt.float32r
BF16 = mybir.dt.bfloat16
I16 = mybir.dt.int16
U16 = mybir.dt.uint16
ALU = mybir.AluOpType
ACT = mybir.ActivationFunctionType
AX = mybir.AxisListType

B, L, S, D = 32, 112, 375, 256
H, HD = 16, 16
P = 128
KT = D // P
OCT, QUAD = 8, 4
NC = 3
C = S // NC
SP = S + 1
NU = KT * NC
QW = QUAD * L
BANK = 512
SCALE = HD ** -0.5
EPS = 1e-5
F = 768
FT = F // P
GT = 4 * L
NG = B * L // GT
QBLK = 32
QMAX = 2.0 ** 15 - 1.0
WMAX = 2.0 ** 3 - 1.0
TINY = 1e-12
SIGQ = 65536.0
LOW = 15
HIGH = -16


STAGES = 7
FIRST = 1 - STAGES
LOOP_FROM = 2
LOOP_PAIRS = (B - STAGES - LOOP_FROM) // 2
LOOP_TO = LOOP_FROM + 2 * LOOP_PAIRS

WORK_USES = (
    (("Ks", 4), ("Qx", 2), ("PT1", 3), ("Qs", 4), ("ctxT0", 3), ("ctxT1", 3), ("AVs1", 3), ("Os", 3),
     ("V1", 3), ("xT", 5)),
    (("Ox", 0), ("x1T", 2), ("PT0", 3), ("V2", 2), ("K1", 2), ("PT2", 3), ("AVs0", 3), ("PT3", 3), ("x2T", 0),
     ("V0", 3), ("K0", 3), ("Vs", 4)),
)
SLOT_USES = (
    (("C4", 1), ("C5", 1), ("C1", 2), ("C2", 2)),
    (("S1", 3), ("C0", 2), ("S0", 4), ("C3", 2)),
)
WORK_OF = {use: bank for bank, uses in enumerate(WORK_USES) for use, _ in uses}
SLOT_OF = {unit: slot for slot, uses in enumerate(SLOT_USES) for unit, _ in uses}


def before(uses, use, batch):
    place = [u for u, _ in uses].index(use)
    i = batch - uses[place][1]
    while i >= FIRST:
        for name, stage in reversed(uses[:place]):
            if 0 <= i + stage < B:
                yield name, i + stage
        place, i = len(uses), i - 1


class Batch:

    def __init__(self, pair, off):
        self.pair, self.off = pair, off
        self.par = off % 2
        self.looped = not isinstance(pair, int)

    def plus(self, d):
        return Batch(self.pair, self.off + d)

    def back(self, d):
        return Batch(self.pair, self.off - d)

    def exists(self):
        return self.looped or 0 <= self.off < B

    def times(self, per, more=0):
        fixed = per * self.off + more
        return self.pair * (2 * per) + fixed if self.looped else fixed

    def loads(self):
        fixed = 16 * (self.off // 2 + 1)
        return self.pair * 16 + fixed if self.looped else fixed

    def first_fills(self, use):
        return sum(1 for _ in before(WORK_USES[WORK_OF[use]], use, self.off))

    def fills(self, use):
        uses = WORK_USES[WORK_OF[use]]
        count = self.first_fills(use)
        if not self.looped:
            return count
        last = sum(1 for _ in before(uses, use, self.off + 2 * (LOOP_PAIRS - 1)))
        assert last == count + 2 * len(uses) * (LOOP_PAIRS - 1)
        return self.pair * (2 * len(uses)) + count


def stages(pair, i):
    batches = [Batch(pair, i + s) for s in range(STAGES)]
    return [n if n.exists() else None for n in batches]


def wait(eng, sem, value):
    if isinstance(value, int) and value <= 0:
        return
    eng.wait_ge(sem, value)


def decoder(nc, a, out, x2_dram):
    with ExitStack() as persist:
        def keep(name, shape, dt=F32):
            return persist.enter_context(nc.sbuf_tensor(name, shape, dt))

        ident = keep("ident", [P, P])
        x2T_all = keep("x2T_all", [P, KT, B * L])
        xmax_all = keep("xmax_all", [P, B])
        wT = {n: [keep(f"{n}T_{p}", [P, KT, F], F32R) for p in ("hi", "lo")] for n in ("w_up", "w_gate")}
        w_down = keep("w_down", [P, KT, F])
        with ExitStack() as scope:
            constants = AttentionConstants(scope, nc, a, x2T_all)
            quantise_weights(nc, a, ident, wT, w_down, constants)
            attention(nc, a, ident, x2T_all, xmax_all, x2_dram, constants)
        feed_forward(nc, out, x2_dram, ident, x2T_all, xmax_all, wT, w_down)


class AttentionConstants:

    def __init__(self, ctx, nc, a, x2T_all):
        def sb(name, shape, dt=F32):
            return ctx.enter_context(nc.sbuf_tensor(name, shape, dt))

        self.a = a
        self.const_ld = ctx.enter_context(nc.semaphore("const_ld"))
        names = ("aWq", "aWk", "aWv", "aWo", "xWq", "xWk", "xWv", "xWo")
        early = {"xWk": 0, "xWv": KT * D}
        w = {n: sb(n, [P, KT, D]) for n in names if n not in early}
        for n, at in early.items():
            w[n] = x2T_all[:, 0, at:at + KT * D].rearrange("p (k n) -> p k n", k=KT)
        split = {n: [sb(f"{n}_{p}", [P, KT, D], F32R) for p in ("hi", "lo")] for n in ("xWk", "xWv")}
        bcol = {n: sb(n, [P, KT]) for n in ("abq", "abk", "abv", "xbq", "xbk")}
        brow = {n: sb(n, [P, D]) for n in ("abo", "xbv", "xbo")}
        mask8 = sb("mask8", [P, OCT])
        even_odd = sb("even_odd", [P, 2])
        sel_raw = x2T_all[:, 1, 0:OCT * L]
        sel = sb("sel", [P, OCT * L], F32R)
        alibi_l = sb("alibi_l", [6, L], BF16)
        alibi_r = sb("alibi_r", [6, H * L], BF16)
        columns = {"abq": "a_bq", "abk": "a_bk", "abv": "a_bv", "xbq": "x_bq", "xbk": "x_bk"}
        rows = {"abo": "a_bo", "xbv": "x_bv", "xbo": "x_bo"}
        N_CONST = len(names) + len(columns) + len(rows) + 5
        self.w, self.split, self.bcol, self.brow, self.early = w, split, bcol, brow, early
        self.mask8, self.even_odd, self.sel_raw, self.sel = mask8, even_odd, sel_raw, sel
        self.alibi_l, self.alibi_r = alibi_l, alibi_r
        self.names, self.columns, self.rows = names, columns, rows
        self.LOADED = 16 * N_CONST

    def load_weights(self, eng, names):
        for n in names:
            eng.dma_start(self.w[n] if n in self.early else self.w[n][:],
                          self.a[n].rearrange("(k p) n -> p k n", p=P)).then_inc(self.const_ld, 16)

    def load_columns(self, eng):
        for n, src in self.columns.items():
            eng.dma_start(self.bcol[n][:], self.a[src].rearrange("(m p) -> p m", p=P),
                          allow_slow_non_contiguous=True).then_inc(self.const_ld, 16)

    def load_rows(self, eng):
        for n, src in self.rows.items():
            eng.dma_start(self.brow[n][:], self.a[src].rearrange("(o n) -> o n", o=1).broadcast_to([P, D]))\
                .then_inc(self.const_ld, 16)
        for dst, src in ((self.mask8, "mask8"), (self.even_odd, "even_odd"), (self.sel_raw, "sel"),
                         (self.alibi_l, "alibi_l"), (self.alibi_r, "alibi_r")):
            eng.dma_start(dst if src == "sel" else dst[:], self.a[src]).then_inc(self.const_ld, 16)


def quantise_weights(nc, a, ident, wT, w_down, constants):
    NB = KT * F // QBLK
    with ExitStack() as ctx:
        def sb(name, shape, dt=F32):
            return ctx.enter_context(nc.sbuf_tensor(name, shape, dt))

        def sem(name):
            return ctx.enter_context(nc.semaphore(name))

        order = ("w_up", "w_gate", "w_down")
        load_order = ("w_up", "w_down", "w_gate")
        raw = {n: sb(f"raw_{n}", [P, NB, QBLK]) for n in order}
        quant = {n: sb(f"quant_{n}", [P, NB, QBLK], I16) for n in order}
        value = {n: sb(f"value_{n}", [P, NB, QBLK]) for n in order[:2]}
        scale = {n: sb(f"scale_{n}", [P, NB]) for n in order}
        inverse = {n: sb(f"inverse_{n}", [P, NB]) for n in order}
        bank = [ctx.enter_context(nc.psum_tensor(f"wbank{p}", [P, BANK], F32)) for p in range(2)]
        HALF = F // 2
        N_FILLS = 2 * KT
        loaded = {n: sem(f"loaded_{n}") for n in order}
        ident_ld, step_done, value_done = sem("ident_ld"), sem("step_done"), sem("value_done")
        turned, hi_done, lo_done = sem("turned"), sem("hi_done"), sem("lo_done")
        block = ctx.enter_context(nc.Block())

        @block.sync
        def _(sp):
            for n in load_order:
                sp.dma_start(raw[n][:].rearrange("p (t b) e -> p t (b e)", t=a[n].shape[0] // P),
                             a[n].rearrange("(t p) i -> p t i", p=P)).then_inc(loaded[n], 16)
            sp.dma_start(ident[:], a["ident"]).then_inc(ident_ld, 16)
            constants.load_weights(sp, constants.names)

        @block.vector
        def _(dve):
            def lo_half(f):
                n, k, h = order[f // N_FILLS], (f // 2) % KT, f % 2
                cols = slice(h * HALF, (h + 1) * HALF)
                dve.wait_ge(hi_done, f + 1)
                dve.tensor_tensor(wT[n][1][:, k, cols], bank[f % 2][:, 0:HALF], wT[n][0][:, k, cols].bitcast(F32),
                                  ALU.subtract).then_inc(lo_done, 1)

            for e, n in enumerate(load_order):
                dve.wait_ge(loaded[n], 16)
                dve.tensor_reduce(scale[n][:], raw[n][:], AX.X, ALU.max, apply_absolute_value=True)\
                    .then_inc(step_done, 1)
                dve.wait_ge(step_done, 4 * e + 1)
                dve.tensor_scalar(scale[n][:], scale[n][:], 1.0 / WMAX, TINY, ALU.mult, ALU.max).then_inc(step_done, 1)
                dve.wait_ge(step_done, 4 * e + 2)
                dve.reciprocal(inverse[n][:], scale[n][:]).then_inc(step_done, 1)
                dve.wait_ge(step_done, 4 * e + 3)
                dve.tensor_tensor(quant[n][:], raw[n][:],
                                  inverse[n][:].rearrange("p (b o) -> p b o", o=1).broadcast_to([P, NB, QBLK]),
                                  ALU.mult).then_inc(step_done, 1)
                dve.wait_ge(step_done, 4 * e + 4)
                dst = value[n][:] if n in value else w_down[:].rearrange("p t (b e) -> p (t b) e", e=QBLK)
                dve.tensor_tensor(dst, quant[n][:],
                                  scale[n][:].rearrange("p (b o) -> p b o", o=1).broadcast_to([P, NB, QBLK]),
                                  ALU.mult).then_inc(value_done, 1)
                if n == "w_down":
                    for f in range(N_FILLS):
                        lo_half(f)
            for f in range(N_FILLS, 2 * N_FILLS):
                lo_half(f)

        @block.scalar
        def _(act):
            constants.load_columns(act)
            constants.load_rows(act)
            for f in range(2 * N_FILLS):
                n, k, h = order[f // N_FILLS], (f // 2) % KT, f % 2
                act.wait_ge(turned, f + 1)
                act.activation(wT[n][0][:, k, h * HALF:(h + 1) * HALF], bank[f % 2][:, 0:HALF], ACT.Copy)\
                    .then_inc(hi_done, 1)

        @block.tensor
        def _(pe):
            pe.wait_ge(ident_ld, 16)
            for f in range(2 * N_FILLS):
                e, k, h = f // N_FILLS, (f // 2) % KT, f % 2
                pe.wait_ge(value_done, (1, 3)[e])
                if f >= 2:
                    pe.wait_ge(lo_done, f - 1)
                rows = value[order[e]][:].rearrange("p (t b) e -> p t (b e)", t=FT)
                for j in range(FT // 2):
                    ins = pe.transpose(bank[f % 2][:, j * P:(j + 1) * P],
                                       rows[:, h * (FT // 2) + j, k * P:(k + 1) * P], ident[:])
                ins.then_inc(turned, 1)


def attention(nc, a, ident, x2T_all, xmax_all, x2_dram, constants):
    with ExitStack() as ctx:
        def sb(name, shape, dt=F32):
            return ctx.enter_context(nc.sbuf_tensor(name, shape, dt))

        def sem(name):
            return ctx.enter_context(nc.semaphore(name))

        w, split, bcol, brow = constants.w, constants.split, constants.bcol, constants.brow
        mask8, even_odd, sel_raw, sel = constants.mask8, constants.even_odd, constants.sel_raw, constants.sel
        alibi_l, alibi_r, const_ld = constants.alibi_l, constants.alibi_r, constants.const_ld
        half = sb("half", [P, 1])
        warm = sb("warm", [P, 2])

        x_in = [sb(f"x_in{p}", [L, D]) for p in range(2)]
        ctx_in = [sb(f"ctx_in{p}", [C, NC, D]) for p in range(2)]
        ctxT = [sb(f"ctxT_{p}", [P, KT, SP], F32R) for p in ("hi", "lo")]
        KxT = [[sb(f"KxT{q}_{p}", [P, KT, S], F32R) for p in ("hi", "lo")] for q in range(2)]
        Vx = [sb(f"Vx{p}", [C, NC, D]) for p in range(2)]
        Qx = [sb(f"Qx_{p}", [P, KT, L], F32R) for p in ("hi", "lo")]
        Qbd = [sb(f"Qbd_{p}", [P, H, L], F32R) for p in ("hi", "lo")]
        Qs = [sb(f"Qs_{p}", [P, KT, L], F32R) for p in ("hi", "lo")]
        Ks = [sb(f"Ks_{p}", [P, KT, L], F32R) for p in ("hi", "lo")]
        Kbd = [sb(f"Kbd_{p}", [P, H, L], F32R) for p in ("hi", "lo")]
        xT = sb("xT", [P, KT, L])
        Vs = sb("Vs", [L, D])
        Ps = sb("Ps", [L, H, L])
        PsT = sb("PsT", [L, H, L])
        nmax_s = sb("nmax_s", [L, H])
        Zs = sb("Zs", [L, H])
        rZs = sb("rZs", [L, H])
        rZrep = sb("rZrep", [L, KT, OCT, HD])
        evenT = sb("evenT", [P, KT, L])
        sumT = sb("sumT", [P, KT, L])
        attnT = sb("attnT", [P, KT, L])
        xb = sb("xb", [L, D])
        r1 = sb("r1", [L, D])
        x1 = sb("x1", [L, D])
        x1T = sb("x1T", [P, KT, L])
        x1b = [sb(f"x1b{p}", [L, D]) for p in range(2)]
        nmax_c = [sb(f"nmax_c{p}", [C, P]) for p in range(2)]
        nmaxT = [sb(f"nmaxT{p}", [P, SP // NC + 1], F32R) for p in range(2)]
        Px = [sb(f"Px{p}", [C, OCT, L]) for p in range(2)]
        Zc = [sb(f"Zc{p}", [C, OCT]) for p in range(2)]
        rZc = [sb(f"rZc{p}", [C, OCT]) for p in range(2)]
        Vn = [sb(f"Vn{p}", [C, OCT, HD]) for p in range(2)]
        evenX = sb("evenX", [P, KT, L])
        OxT = sb("OxT", [P, KT, L])
        r2 = sb("r2", [L, D])
        x2 = sb("x2", [L, D])
        carrier = sb("carrier", [1, 1])
        stats = [sb(f"stats{p}", [L, 6]) for p in range(2)]
        mv = [sb(f"mv{p}", [L, 2]) for p in range(2)]
        vare = [sb(f"vare{p}", [L, 1]) for p in range(2)]
        rstd = [sb(f"rstd{p}", [L, 1]) for p in range(2)]

        score = [ctx.enter_context(nc.psum_tensor(f"score{p}", [P, 2, BANK], F32)) for p in range(2)]
        work = [ctx.enter_context(nc.psum_tensor(f"work{p}", [P, BANK], F32)) for p in range(2)]
        outX = ctx.enter_context(nc.psum_tensor("outX", [P, KT, 2 * L], F32))
        maxT = ctx.enter_context(nc.psum_tensor("maxT", [P, BANK], F32))

        consts = sem("consts")
        bv_spread, bv_product, bo_folded = sem("bv_spread"), sem("bv_product"), sem("bo_folded")
        x_ld = [sem(f"x_ld{p}") for p in range(2)]
        ctx_ld = [sem(f"ctx_ld{p}") for p in range(2)]
        filled = [sem(f"filled{p}") for p in range(2)]
        drained = [sem(f"drained{p}") for p in range(2)]
        ctx_hi, kx_hi, ks_hi, qs_hi, qx_hi = (sem(n) for n in ("ctx_hi", "kx_hi", "ks_hi", "qs_hi", "qx_hi"))
        kbd_done, qbd_done = sem("kbd_done"), sem("qbd_done")
        scores_s, nmax_s_done, exp_s = sem("scores_s"), sem("nmax_s_done"), sem("exp_s")
        rz_s, rzrep_s, even_s, sum_s = sem("rz_s"), sem("rzrep_s"), sem("even_s"), sem("sum_s")
        scores_c, nmax_c_done, nmaxT_done = sem("scores_c"), sem("nmax_c_done"), sem("nmaxT_done")
        nmaxT_copied, shifted, exp_c = sem("nmaxT_copied"), sem("shifted"), sem("exp_c")
        z_c, rz_c, vn_done, av_done = sem("z_c"), sem("rz_c"), sem("vn_done"), sem("av_done")
        even_x, oxT_done, xmax_done = sem("even_x"), sem("oxT_done"), sem("xmax_done")
        xb_done, x1b_done = sem("xb_done"), sem("x1b_done")
        bn_done = [sem(f"bn_done{p}") for p in (1, 2)]
        mv_done = [sem(f"mv_done{p}") for p in (1, 2)]
        var_done = [sem(f"var_done{p}") for p in (1, 2)]
        rstd_done = [sem(f"rstd_done{p}") for p in (1, 2)]
        x1_done, x2_done, x2T_copied, x2_saved = sem("x1_done"), sem("x2_done"), sem("x2T_copied"), sem("x2_saved")

        x_dram, ctx_dram = a["x"], a["ctx"]
        def iterations(eng, step):
            for i in range(FIRST, LOOP_FROM):
                step(*stages(0, i))
            with eng.Fori(0, LOOP_PAIRS) as r:
                step(*stages(r, LOOP_FROM))
                step(*stages(r, LOOP_FROM + 1))
            for i in range(LOOP_TO, B):
                step(*stages(0, i))

        def latest_of_banks(uses):
            latest = {}
            for n, use in uses:
                bank = WORK_OF[use]
                if n.exists() and (bank not in latest or n.first_fills(use) > latest[bank][0].first_fills(latest[bank][1])):
                    latest[bank] = (n, use)
            return latest.items()

        def wait_fill(eng, *uses):
            for bank, (n, use) in latest_of_banks(uses):
                eng.wait_ge(filled[bank], n.fills(use) + 1)

        def wait_drain(eng, *uses):
            for bank, (n, use) in latest_of_banks(uses):
                eng.wait_ge(drained[bank], n.fills(use) + 1)

        block = ctx.enter_context(nc.Block())

        @block.sync
        def _(sp):
            def load_x(n):
                wait(sp, xb_done, n.back(2).times(1, 1))
                sp.dma_start(x_in[n.par][:], x_dram[bass.ds(n.times(1), 1)].rearrange("o l d -> (o l) d"))\
                    .then_inc(x_ld[n.par], 16)

            def load_ctx(n):
                wait_fill(sp, (n.back(2), "ctxT1"))
                sp.dma_start(ctx_in[n.par][:],
                             ctx_dram[bass.ds(n.times(1), 1)].rearrange("o (c s) d -> s (o c) d", c=NC))\
                    .then_inc(ctx_ld[n.par], 16)

            def save_x2(n):
                sp.wait_ge(x2_done, n.times(1, 1))
                sp.dma_start(x2_dram[bass.ds(n.times(1), 1)].rearrange("o l d -> (o l) d"), x2[:])\
                    .then_inc(x2_saved, 16)

            def step(n0, n1, n2, n3, n4, n5, n6):
                if n5:
                    load_x(n5)
                    load_ctx(n5)
                if n0:
                    save_x2(n0)
            iterations(sp, step)
            sp.wait_ge(x2_saved, 16 * B)

        @block.gpsimd
        def _(pool):
            pool.memset(half[:], -0.5).then_inc(consts, 1)
            for h in range(2):
                pool.memset(nmax_c[h][:], 0.0).then_inc(consts, 1)
                pool.memset(ctxT[h][:, :, S:SP].bitcast(F32), 0.0).then_inc(consts, 1)
            pool.memset(xmax_all[:], 0.0).then_inc(consts, 1)
            pool.wait_ge(const_ld, constants.LOADED)
            pool.wait_ge(bo_folded, 1)

            def block_diagonal(dst, src, t, done):
                for h in range(2):
                    ins = pool.tensor_tensor(
                        dst[h][:, OCT * t:OCT * (t + 1), :],
                        src[h][:, t:t + 1, :].bitcast(F32).broadcast_to([P, OCT, L]),
                        mask8[:].rearrange("p (h o) -> p h o", o=1).broadcast_to([P, OCT, L]), ALU.mult)
                ins.then_inc(done, 1)

            def diagonal_keys(n, t):
                if t == 0:
                    wait_drain(pool, (n, "Ks"))
                wait(pool, scores_s, n.back(1).times(KT, t + 1))
                block_diagonal(Kbd, Ks, t, kbd_done)

            def diagonal_queries(n, t):
                if t == 0:
                    wait_drain(pool, (n, "Qx"))
                wait(pool, scores_c, n.back(1).times(NU, NC * (t + 1)))
                block_diagonal(Qbd, Qx, t, qbd_done)

            def inverse_root(n, k):
                pool.wait_ge(var_done[k], n.times(1, 1))
                pool.tensor_tensor(rstd[k][:], vare[k][:], half[0:L, :], ALU.pow).then_inc(rstd_done[k], 1)

            def add_output_bias(n):
                wait_fill(pool, (n, "xT"))
                wait_drain(pool, (n.back(1), "Os"))
                pool.tensor_tensor(xb[:], x_in[n.par][:], brow["abo"][0:L, :], ALU.add).then_inc(xb_done, 1)

            def add_output_bias_2(n):
                pool.wait_ge(x1_done, n.times(1, 1))
                wait_drain(pool, (n.back(2), "Ox"))
                pool.tensor_tensor(x1b[n.par][:], x1[:], brow["xbo"][0:L, :], ALU.add).then_inc(x1b_done, 1)

            def step(n0, n1, n2, n3, n4, n5, n6):
                if n5:
                    add_output_bias(n5)
                if n4:
                    diagonal_queries(n4, 0)
                if n2:
                    inverse_root(n2, 1)
                if n6:
                    diagonal_keys(n6, 0)
                    diagonal_keys(n6, 1)
                if n4:
                    diagonal_queries(n4, 1)
                if n5:
                    inverse_root(n5, 0)
                    add_output_bias_2(n5)
            iterations(pool, step)

        @block.scalar
        def _(act):
            act.wait_ge(const_ld, constants.LOADED)
            act.activation(warm[:, 0:1], mask8[:, 0:1], ACT.Exp)
            for n in ("xWk", "xWv"):
                act.activation(split[n][0][:], w[n], ACT.Copy).then_inc(consts, 1)
            act.activation(sel[:], sel_raw, ACT.Copy).then_inc(consts, 1)

            def exp_self(n, t):
                act.wait_ge(nmax_s_done, n.times(KT, t + 1))
                wait_fill(act, (n.back(1), f"PT{2 * t + 1}"))
                wait(act, rz_s, n.back(1).times(KT, t + 1))
                slot = SLOT_OF[f"S{t}"]
                for h in range(OCT):
                    g = OCT * t + h
                    ins = act.activation(Ps[:, g, :], score[slot][0:L, h // QUAD, (h % QUAD) * L:(h % QUAD + 1) * L],
                                         ACT.Exp, bias=nmax_s[:, g:g + 1], accum_out=Zs[:, g:g + 1])
                ins.then_inc(exp_s, 1)

            def exp_cross(n, u):
                act.wait_ge(shifted, n.times(NU, u + 1))
                wait(act, av_done, n.times(NU, u - 1))
                act.activation(Px[u % 2][:].rearrange("s (q h) l -> s q (h l)", q=2),
                               score[SLOT_OF[f"C{u}"]][0:C, :, 0:QW], ACT.Exp).then_inc(exp_c, 1)

            def copy_max(n, u):
                act.wait_ge(nmaxT_done, n.times(NU, u + 1))
                wait(act, shifted, n.times(NU, u - 1))
                act.activation(nmaxT[u % 2][:, 0:C], maxT[:, 0:C], ACT.Copy).then_inc(nmaxT_copied, 1)

            def hi_with_bias(n, use, dst, bias, done):
                wait_fill(act, (n, use))
                for m in range(KT):
                    ins = act.activation(dst[:, m, :], work[WORK_OF[use]][:, m * L:(m + 1) * L], ACT.Identity,
                                         bias=bias[:, m:m + 1])
                ins.then_inc(done, 1)

            def hi_queries_self(n):
                wait(act, scores_s, n.back(1).times(KT, KT))
                hi_with_bias(n, "Qs", Qs[0], bcol["abq"], qs_hi)

            def hi_keys_self(n):
                wait(act, kbd_done, n.back(1).times(KT, KT))
                hi_with_bias(n, "Ks", Ks[0], bcol["abk"], ks_hi)

            def hi_queries_cross(n):
                wait(act, qbd_done, n.back(1).times(KT, KT))
                hi_with_bias(n, "Qx", Qx[0], bcol["xbq"], qx_hi)

            def drain_copy(n, use, dst, rows_, cols, readers):
                b = WORK_OF[use]
                wait_fill(act, (n, use), *((n.back(1), r) for r in readers))
                act.activation(dst, work[b][0:rows_, 0:cols], ACT.Copy).then_inc(drained[b], 1)

            def copy_xT(n):
                drain_copy(n, "xT", xT[:].rearrange("p k l -> p (k l)"), P, KT * L, ("Ks", "Qs", "Vs"))

            def copy_x1T(n):
                drain_copy(n, "x1T", x1T[:].rearrange("p k l -> p (k l)"), P, KT * L, ("Qx",))

            def copy_x2T(n):
                b = WORK_OF["x2T"]
                wait_fill(act, (n, "x2T"))
                act.activation(x2T_all[:, :, bass.ds(n.times(L), L)],
                               work[b][:, 0:KT * L].rearrange("p (k l) -> p k l", k=KT), ACT.Copy)\
                    .then_inc(drained[b], 1)

            def copy_values_self(n):
                drain_copy(n, "Vs", Vs[:], L, D, ("AVs1",))

            def copy_probs(n, j):
                drain_copy(n, f"PT{j}", PsT[:, QUAD * j:QUAD * (j + 1), :].rearrange("k h q -> k (h q)"), L, QW,
                           (f"AVs{j // 2}",))

            def even_self(n, t):
                use = f"AVs{t}"
                wait_fill(act, (n, use))
                wait(act, sum_s, n.back(1).times(KT, t + 1))
                act.activation(evenT[:, t, :], work[WORK_OF[use]][:, 0:L], ACT.Copy,
                               scale=even_odd[:, 0:1]).then_inc(even_s, 1)

            def even_cross(n):
                act.wait_ge(av_done, n.times(NU, NU))
                wait(act, oxT_done, n.back(1).times(1, 1))
                act.activation(evenX[:], outX[:, :, 0:L], ACT.Copy, scale=even_odd[:, 0:1]).then_inc(even_x, 1)

            def hi_context(n, k):
                use = f"ctxT{k}"
                last = [(n.back(1), u) for u in ("K1", "V2")] if k == 0 else []
                wait_fill(act, (n, use), *last)
                act.activation(ctxT[0][:, k, 0:S], work[WORK_OF[use]][:, 0:S], ACT.Copy).then_inc(ctx_hi, 1)

            def hi_keys_cross(n, m):
                use = f"K{m}"
                wait_fill(act, (n, use))
                wait(act, scores_c, n.back(2).times(NU, NC * (m + 1)))
                act.activation(KxT[n.par][0][:, m, :], work[WORK_OF[use]][:, 0:S], ACT.Identity,
                               bias=bcol["xbk"][:, m:m + 1]).then_inc(kx_hi, 1)

            def step(n0, n1, n2, n3, n4, n5, n6):
                if n4:
                    copy_probs(n4, 0)
                if n2:
                    copy_max(n2, 4)
                    exp_cross(n2, 4)
                if n4:
                    copy_probs(n4, 1)
                    exp_self(n4, 1)
                if n3:
                    hi_keys_cross(n3, 1)
                if n5:
                    hi_queries_self(n5)
                if n2:
                    copy_max(n2, 5)
                if n4:
                    copy_probs(n4, 2)
                    hi_context(n4, 0)
                if n2:
                    exp_cross(n2, 5)
                if n3:
                    copy_max(n3, 0)
                if n4:
                    even_self(n4, 0)
                if n3:
                    exp_cross(n3, 0)
                if n4:
                    hi_context(n4, 1)
                    copy_probs(n4, 3)
                if n3:
                    copy_max(n3, 1)
                if n1:
                    copy_x2T(n1)
                if n2:
                    even_cross(n2)
                if n3:
                    exp_cross(n3, 1)
                if n4:
                    even_self(n4, 1)
                if n5:
                    exp_self(n5, 0)
                if n3:
                    copy_max(n3, 2)
                if n4:
                    hi_keys_cross(n4, 0)
                if n3:
                    exp_cross(n3, 2)
                if n5:
                    copy_values_self(n5)
                if n6:
                    copy_xT(n6)
                if n3:
                    copy_max(n3, 3)
                if n6:
                    hi_keys_self(n6)
                if n4:
                    copy_x1T(n4)
                if n3:
                    exp_cross(n3, 3)
                if n4:
                    hi_queries_cross(n4)
            iterations(act, step)

        @block.vector
        def _(dve):
            dve.wait_ge(const_ld, constants.LOADED)
            for n in ("aWq", "xWq"):
                dve.tensor_scalar(w[n][:], w[n][:], SCALE, None, ALU.mult).then_inc(consts, 1)
            for n in ("abq", "xbq"):
                dve.tensor_scalar(bcol[n][:], bcol[n][:], SCALE, None, ALU.mult).then_inc(consts, 1)
            dve.wait_ge(consts, 13)
            for n in ("xWk", "xWv"):
                dve.tensor_tensor(split[n][1][:], w[n], split[n][0][:].bitcast(F32), ALU.subtract)\
                    .then_inc(consts, 1)

            dve.tensor_copy(x1T[:], bcol["abv"][:].rearrange("p (k o) -> p k o", o=1).broadcast_to([P, KT, L]))\
                .then_inc(bv_spread, 1)
            dve.wait_ge(bv_product, 1)
            dve.tensor_tensor(brow["abo"][0:L, :], work[0][0:L, 0:D], brow["abo"][0:L, :], ALU.add)\
                .then_inc(bo_folded, 1)

            def sum_cross(n, u):
                p = u % 2
                dve.wait_ge(exp_c, n.times(NU, u + 1))
                dve.tensor_reduce(Zc[p][:], Px[p][:], AX.X, ALU.add).then_inc(z_c, 1)

            def reciprocal_cross(n, u):
                dve.wait_ge(z_c, n.times(NU, u + 1))
                dve.reciprocal(rZc[u % 2][:], Zc[u % 2][:]).then_inc(rz_c, 1)

            def normalise_values(n, u):
                t, c = divmod(u, NC)
                p = u % 2
                dve.wait_ge(rz_c, n.times(NU, u + 1))
                dve.tensor_tensor(Vn[p][:], Vx[n.par][:, c, P * t:P * (t + 1)].rearrange("s (h e) -> s h e", h=OCT),
                                  rZc[p][:].rearrange("s (h o) -> s h o", o=1).broadcast_to([C, OCT, HD]), ALU.mult)\
                    .then_inc(vn_done, 1)

            def max_cross(n, u):
                dve.wait_ge(scores_c, n.times(NU, u + 1))
                wait(dve, nmaxT_done, n.times(NU, u - 1))
                dve.tensor_reduce(nmax_c[u % 2][:, 0:OCT].rearrange("s (q h) -> s q h", q=2),
                                  score[SLOT_OF[f"C{u}"]][0:C, :, 0:QW].rearrange("s q (h l) -> s q h l", h=QUAD),
                                  AX.X, ALU.max, negate=True).then_inc(nmax_c_done, 1)

            def max_self(n, t):
                dve.wait_ge(scores_s, n.times(KT, t + 1))
                wait(dve, exp_s, n.back(1).times(KT, t + 1))
                dve.tensor_reduce(nmax_s[:, OCT * t:OCT * (t + 1)].rearrange("s (q h) -> s q h", q=2),
                                  score[SLOT_OF[f"S{t}"]][0:L, :, 0:QW].rearrange("s q (h l) -> s q h l", h=QUAD),
                                  AX.X, ALU.max, negate=True).then_inc(nmax_s_done, 1)

            def lo_with_bias(n, use, dst, hi, bias, hi_sem):
                b = WORK_OF[use]
                dve.wait_ge(hi_sem, n.times(1, 1))
                for m in range(KT):
                    ins = dve.scalar_tensor_tensor(dst[:, m, :], work[b][:, m * L:(m + 1) * L], bias[:, m:m + 1],
                                                   hi[:, m, :].bitcast(F32), ALU.add, ALU.subtract)
                ins.then_inc(drained[b], 1)

            def lo_context(n, k):
                b = WORK_OF[f"ctxT{k}"]
                dve.wait_ge(ctx_hi, n.times(KT, k + 1))
                dve.tensor_tensor(ctxT[1][:, k, 0:S], work[b][:, 0:S], ctxT[0][:, k, 0:S].bitcast(F32),
                                  ALU.subtract).then_inc(drained[b], 1)

            def lo_keys_cross(n, m):
                b = WORK_OF[f"K{m}"]
                dve.wait_ge(kx_hi, n.times(KT, m + 1))
                dve.scalar_tensor_tensor(KxT[n.par][1][:, m, :], work[b][:, 0:S], bcol["xbk"][:, m:m + 1],
                                         KxT[n.par][0][:, m, :].bitcast(F32), ALU.add, ALU.subtract)\
                    .then_inc(drained[b], 1)

            def values_with_bias(n, c):
                use = f"V{c}"
                b = WORK_OF[use]
                wait_fill(dve, (n, use))
                dve.tensor_tensor(Vx[n.par][:, c, :], work[b][0:C, 0:D], brow["xbv"][0:C, :], ALU.add)\
                    .then_inc(drained[b], 1)

            def reciprocal_self(n, t):
                dve.wait_ge(exp_s, n.times(KT, t + 1))
                h = slice(OCT * t, OCT * (t + 1))
                dve.reciprocal(rZs[:, h], Zs[:, h]).then_inc(rz_s, 1)

            def spread_reciprocal(n, t):
                h = slice(OCT * t, OCT * (t + 1))
                dve.wait_ge(rz_s, n.times(KT, t + 1))
                wait_fill(dve, (n.back(1), f"AVs{t}"))
                dve.tensor_copy(rZrep[:, t], rZs[:, h].rearrange("q (h o) -> q h o", o=1).broadcast_to([L, OCT, HD]))\
                    .then_inc(rzrep_s, 1)

            def pick_self(n, t):
                dve.wait_ge(even_s, n.times(KT, t + 1))
                dve.scalar_tensor_tensor(sumT[:, t, :], work[WORK_OF[f"AVs{t}"]][:, L:2 * L], even_odd[:, 1:2],
                                         evenT[:, t, :], ALU.mult, ALU.add).then_inc(sum_s, 1)

            def divide_self(n, t):
                b = WORK_OF[f"AVs{t}"]
                dve.wait_ge(sum_s, n.times(KT, t + 1))
                wait_fill(dve, (n.back(1), "Os"))
                dve.tensor_tensor(attnT[:, t, :], sumT[:, t, :], work[b][:, 2 * L:3 * L], ALU.mult)\
                    .then_inc(drained[b], 1)

            def pick_cross(n):
                dve.wait_ge(even_x, n.times(1, 1))
                wait_fill(dve, (n.back(1), "Ox"))
                dve.scalar_tensor_tensor(OxT[:], outX[:, :, L:2 * L], even_odd[:, 1:2], evenX[:],
                                         ALU.mult, ALU.add).then_inc(oxT_done, 1)

            def residual(n, k):
                use, sum_, add = (("Os", r1, xb), ("Ox", r2, x1b[n.par]))[k]
                b = WORK_OF[use]
                dve.wait_ge((xb_done, x1b_done)[k], n.times(1, 1))
                wait_fill(dve, (n, use))
                dve.tensor_tensor(sum_[:], work[b][0:L, 0:D], add[:], ALU.add).then_inc(drained[b], 1)

            def moments(n, k):
                wait_drain(dve, (n, ("Os", "Ox")[k]))
                dve.bn_stats(stats[k][:], (r1, r2)[k][:]).then_inc(bn_done[k], 1)

            def mean_variance(n, k):
                dve.wait_ge(bn_done[k], n.times(1, 1))
                dve.memset(carrier[:], 0.0)
                dve.bn_aggr(mv[k][:], stats[k][:]).then_inc(mv_done[k], 1)

            def add_eps(n, k):
                dve.wait_ge(mv_done[k], n.times(1, 1))
                dve.tensor_scalar(vare[k][:], mv[k][:, 1:2], EPS, None, ALU.add).then_inc(var_done[k], 1)

            def norm_self(n):
                dve.wait_ge(rstd_done[0], n.times(1, 1))
                wait_fill(dve, (n.back(1), "x1T"))
                wait(dve, x1b_done, n.back(1).times(1, 1))
                dve.tensor_scalar(x1[:], r1[:], mv[0][:, 0:1], rstd[0][:, 0:1], ALU.subtract, ALU.mult)\
                    .then_inc(x1_done, 1)

            def norm_cross(n):
                dve.wait_ge(rstd_done[1], n.times(1, 1))
                wait_fill(dve, (n.back(1), "x2T"))
                wait(dve, x2_saved, n.times(16))
                dve.tensor_scalar(x2[:], r2[:], mv[1][:, 0:1], rstd[1][:, 0:1], ALU.subtract, ALU.mult)\
                    .then_inc(x2_done, 1)

            def largest(n):
                dve.wait_ge(x2_done, n.times(1, 1))
                dve.tensor_reduce(xmax_all[0:L, bass.ds(n.times(1), 1)], x2[:], AX.X, ALU.max,
                                  apply_absolute_value=True).then_inc(xmax_done, 1)

            def step(n0, n1, n2, n3, n4, n5, n6):
                if n2:
                    residual(n2, 1)
                if n3:
                    reciprocal_cross(n3, 2)
                if n2:
                    moments(n2, 1)
                    mean_variance(n2, 1)
                if n6:
                    lo_with_bias(n6, "Ks", Ks[1], Ks[0], bcol["abk"], ks_hi)
                if n3:
                    normalise_values(n3, 2)
                    max_cross(n3, 4)
                    sum_cross(n3, 3)
                if n5:
                    reciprocal_self(n5, 0)
                if n4:
                    lo_with_bias(n4, "Qx", Qx[1], Qx[0], bcol["xbq"], qx_hi)
                if n5:
                    spread_reciprocal(n5, 0)
                if n3:
                    reciprocal_cross(n3, 3)
                    normalise_values(n3, 3)
                if n5:
                    max_self(n5, 1)
                if n2:
                    add_eps(n2, 1)
                if n4:
                    values_with_bias(n4, 2)
                if n3:
                    sum_cross(n3, 4)
                    reciprocal_cross(n3, 4)
                    max_cross(n3, 5)
                if n5:
                    reciprocal_self(n5, 1)
                if n4:
                    lo_keys_cross(n4, 1)
                if n6:
                    lo_with_bias(n6, "Qs", Qs[1], Qs[0], bcol["abq"], qs_hi)
                if n3:
                    normalise_values(n3, 4)
                if n4:
                    max_cross(n4, 0)
                if n2:
                    norm_cross(n2)
                if n5:
                    lo_context(n5, 0)
                if n3:
                    sum_cross(n3, 5)
                if n5:
                    pick_self(n5, 0)
                if n3:
                    reciprocal_cross(n3, 5)
                if n5:
                    divide_self(n5, 0)
                if n3:
                    normalise_values(n3, 5)
                if n5:
                    spread_reciprocal(n5, 1)
                if n4:
                    max_cross(n4, 1)
                if n2:
                    largest(n2)
                if n5:
                    lo_context(n5, 1)
                if n6:
                    max_self(n6, 0)
                if n4:
                    sum_cross(n4, 0)
                if n3:
                    pick_cross(n3)
                if n5:
                    pick_self(n5, 1)
                if n4:
                    reciprocal_cross(n4, 0)
                if n5:
                    divide_self(n5, 1)
                    values_with_bias(n5, 0)
                if n4:
                    normalise_values(n4, 0)
                    max_cross(n4, 2)
                if n5:
                    residual(n5, 0)
                if n4:
                    sum_cross(n4, 1)
                if n5:
                    moments(n5, 0)
                if n4:
                    reciprocal_cross(n4, 1)
                if n5:
                    lo_keys_cross(n5, 0)
                if n4:
                    normalise_values(n4, 1)
                if n5:
                    mean_variance(n5, 0)
                    values_with_bias(n5, 1)
                    add_eps(n5, 0)
                if n4:
                    max_cross(n4, 3)
                if n5:
                    norm_self(n5)
                if n4:
                    sum_cross(n4, 2)
            iterations(dve, step)

        @block.tensor
        def _(pe):
            pe.wait_ge(consts, 15)

            pe.wait_ge(bv_spread, 1)
            for k in range(KT):
                ins = pe.matmul(work[0][0:L, 0:D], x1T[:, k, :], w["aWo"][:, k, :], start=(k == 0), stop=(k == KT - 1))
            ins.then_inc(bv_product, 1)
            pe.wait_ge(bo_folded, 1)

            def fill(n, use, *sources):
                bank = WORK_OF[use]
                wait_drain(pe, *((n, s) for s in sources if WORK_OF[s] != bank))
                wait(pe, drained[bank], n.fills(use))
                return work[bank]

            def wait_slot(n, unit):
                last, batch = next(before(SLOT_USES[SLOT_OF[unit]], unit, n.off), (None, None))
                if last is not None:
                    old = Batch(n.pair, batch)
                    kind, u = last[0], int(last[1:])
                    wait(pe, *((exp_s, old.times(KT, u + 1)) if kind == "S" else (exp_c, old.times(NU, u + 1))))

            def three(dst, lhs, rhs, first, last):
                pe.matmul(dst, lhs[0], rhs[0], start=first, stop=False)
                pe.matmul(dst, lhs[0], rhs[1], start=False, stop=False)
                return pe.matmul(dst, lhs[1], rhs[0], start=False, stop=last)

            def transpose_rows(n, use, src):
                b = fill(n, use)
                for k in range(KT):
                    ins = pe.transpose(b[:, k * L:(k + 1) * L], src[:, k * P:(k + 1) * P], ident[0:L, 0:L])
                ins.then_inc(filled[WORK_OF[use]], 1)

            def transpose_x(n):
                pe.wait_ge(x_ld[n.par], n.loads())
                transpose_rows(n, "xT", x_in[n.par])

            def transpose_x1(n):
                pe.wait_ge(x1_done, n.times(1, 1))
                transpose_rows(n, "x1T", x1)

            def transpose_x2(n):
                pe.wait_ge(x2_done, n.times(1, 1))
                transpose_rows(n, "x2T", x2)

            def project_T(n, use, weight, src, source_use):
                b = fill(n, use, source_use)
                for m in range(KT):
                    for k in range(KT):
                        ins = pe.matmul(b[:, m * L:(m + 1) * L], weight[:, k, m * P:(m + 1) * P], src[:, k, :],
                                        start=(k == 0), stop=(k == KT - 1))
                ins.then_inc(filled[WORK_OF[use]], 1)

            def project(n, use, srcT, weight, *sources):
                b = fill(n, use, *sources)
                for k in range(KT):
                    ins = pe.matmul(b[0:L, 0:D], srcT[:, k, :], weight[:, k, :], start=(k == 0), stop=(k == KT - 1))
                ins.then_inc(filled[WORK_OF[use]], 1)

            def project_values_self(n):
                project(n, "Vs", xT, w["aWv"], "xT")

            def project_out_self(n):
                project(n, "Os", attnT, w["aWo"], "AVs0", "AVs1")

            def project_out_cross(n):
                pe.wait_ge(oxT_done, n.times(1, 1))
                project(n, "Ox", OxT, w["xWo"])

            def self_scores(n, t):
                wait_slot(n, f"S{t}")
                wait_drain(pe, (n, "Qs"))
                pe.wait_ge(kbd_done, n.times(KT, t + 1))
                for q in range(2):
                    j = 2 * t + q
                    dst = score[SLOT_OF[f"S{t}"]][0:L, q, 0:QW]
                    pe.matmul(dst, alibi_l[:], alibi_r[:, j * QW:(j + 1) * QW], start=True, stop=False)
                    rhs = [x[:, QUAD * j:QUAD * (j + 1), :].rearrange("p h k -> p (h k)") for x in Kbd]
                    ins = three(dst, [x[:, t, :] for x in Qs], rhs, False, True)
                ins.then_inc(scores_s, 1)

            def cross_scores(n, u):
                t, c = divmod(u, NC)
                wait_slot(n, f"C{u}")
                if c == 0:
                    wait_drain(pe, (n, f"K{t}"))
                    pe.wait_ge(qbd_done, n.times(KT, t + 1))
                for q in range(2):
                    j = 2 * t + q
                    rhs = [x[:, QUAD * j:QUAD * (j + 1), :].rearrange("p h l -> p (h l)") for x in Qbd]
                    dst = score[SLOT_OF[f"C{u}"]][0:C, q, 0:QW]
                    lhs = [x[:, t, c * C:(c + 1) * C] for x in KxT[n.par]]
                    ins = three(dst, lhs, rhs, True, True)
                ins.then_inc(scores_c, 1)

            def transpose_max(n, u):
                pe.wait_ge(nmax_c_done, n.times(NU, u + 1))
                wait(pe, nmaxT_copied, n.times(NU, u))
                pe.transpose(maxT[:, 0:C], nmax_c[u % 2][:], ident[0:C, 0:C]).then_inc(nmaxT_done, 1)

            def shift(n, u):
                pe.wait_ge(nmaxT_copied, n.times(NU, u + 1))
                for q in range(2):
                    ins = pe.matmul(score[SLOT_OF[f"C{u}"]][0:C, q, 0:QW], nmaxT[u % 2][:, 0:C],
                                    sel[:, q * QW:(q + 1) * QW], start=False, stop=True, skip_group_check=True)
                ins.then_inc(shifted, 1)

            def cross_values(n, u):
                t, c = divmod(u, NC)
                pe.wait_ge(vn_done, n.times(NU, u + 1))
                if u == 0:
                    wait(pe, oxT_done, n.times(1))
                for g in range(4):
                    ins = pe.matmul(outX[32 * g:32 * (g + 1), t, :],
                                    Vn[u % 2][:, 2 * g:2 * g + 2, :].rearrange("s h e -> s (h e)"),
                                    Px[u % 2][:, 2 * g:2 * g + 2, :].rearrange("s h l -> s (h l)"),
                                    start=(c == 0), stop=(c == NC - 1))
                ins.then_inc(av_done, 1)

            def transpose_ctx(n, k):
                use = f"ctxT{k}"
                b = fill(n, use)
                pe.wait_ge(ctx_ld[n.par], n.loads())
                for c in range(NC):
                    ins = pe.transpose(b[:, c * C:(c + 1) * C], ctx_in[n.par][:, c, k * P:(k + 1) * P], ident[0:C, 0:C])
                ins.then_inc(filled[WORK_OF[use]], 1)

            def keys_cross(n, m):
                use = f"K{m}"
                b = fill(n, use, "ctxT0", "ctxT1")
                for k in range(KT):
                    ins = three(b[:, 0:SP], [x[:, k, m * P:(m + 1) * P] for x in split["xWk"]],
                                [x[:, k, :] for x in ctxT], k == 0, k == KT - 1)
                ins.then_inc(filled[WORK_OF[use]], 1)

            def values_cross(n, c):
                use = f"V{c}"
                b = fill(n, use, "ctxT0", "ctxT1")
                for k in range(KT):
                    ins = three(b[0:C, 0:D], [x[:, k, c * C:(c + 1) * C] for x in ctxT],
                                [x[:, k, :] for x in split["xWv"]], k == 0, k == KT - 1)
                ins.then_inc(filled[WORK_OF[use]], 1)

            def transpose_probs(n, j):
                use = f"PT{j}"
                b = fill(n, use)
                pe.wait_ge(exp_s, n.times(KT, j // 2 + 1))
                for h in range(QUAD):
                    ins = pe.transpose(b[0:L, h * L:(h + 1) * L], Ps[:, QUAD * j + h, :], ident[0:L, 0:L])
                ins.then_inc(filled[WORK_OF[use]], 1)

            def self_values(n, t):
                use = f"AVs{t}"
                b = fill(n, use, "Vs", f"PT{2 * t}", f"PT{2 * t + 1}")
                pe.wait_ge(rzrep_s, n.times(KT, t + 1))
                pe.transpose(b[:, 2 * L:3 * L], rZrep[:, t].rearrange("q h e -> q (h e)"), ident[0:L, 0:L])
                for g in range(4):
                    h = OCT * t + 2 * g
                    ins = pe.matmul(b[32 * g:32 * (g + 1), 0:2 * L], Vs[:, h * HD:(h + 2) * HD],
                                    PsT[:, h:h + 2, :].rearrange("k h q -> k (h q)"), start=True, stop=True)
                ins.then_inc(filled[WORK_OF[use]], 1)

            def step(n0, n1, n2, n3, n4, n5, n6):
                if n0:
                    project_out_cross(n0)
                if n4:
                    project_T(n4, "Ks", w["aWk"], xT, "xT")
                if n1:
                    shift(n1, 3)
                if n2:
                    transpose_x1(n2)
                if n1:
                    cross_scores(n1, 4)
                if n3:
                    transpose_probs(n3, 0)
                if n2:
                    project_T(n2, "Qx", w["xWq"], x1T, "x1T")
                if n1:
                    cross_values(n1, 2)
                    transpose_max(n1, 4)
                if n3:
                    self_scores(n3, 1)
                if n1:
                    shift(n1, 4)
                if n3:
                    transpose_probs(n3, 1)
                if n2:
                    values_cross(n2, 2)
                if n1:
                    cross_values(n1, 3)
                    cross_scores(n1, 5)
                if n2:
                    keys_cross(n2, 1)
                if n4:
                    project_T(n4, "Qs", w["aWq"], xT, "xT")
                if n1:
                    transpose_max(n1, 5)
                if n2:
                    cross_scores(n2, 0)
                if n3:
                    transpose_probs(n3, 2)
                    transpose_ctx(n3, 0)
                if n1:
                    shift(n1, 5)
                if n3:
                    self_values(n3, 0)
                if n2:
                    transpose_max(n2, 0)
                if n1:
                    cross_values(n1, 4)
                if n3:
                    transpose_ctx(n3, 1)
                if n2:
                    shift(n2, 0)
                    cross_scores(n2, 1)
                if n3:
                    transpose_probs(n3, 3)
                if n4:
                    self_scores(n4, 0)
                if n2:
                    transpose_max(n2, 1)
                if n0:
                    transpose_x2(n0)
                if n1:
                    cross_values(n1, 5)
                if n2:
                    shift(n2, 1)
                if n3:
                    self_values(n3, 1)
                    values_cross(n3, 0)
                if n2:
                    cross_scores(n2, 2)
                if n3:
                    project_out_self(n3)
                    keys_cross(n3, 0)
                if n2:
                    transpose_max(n2, 2)
                if n3:
                    values_cross(n3, 1)
                if n2:
                    shift(n2, 2)
                    cross_scores(n2, 3)
                    cross_values(n2, 0)
                if n4:
                    project_values_self(n4)
                if n5:
                    transpose_x(n5)
                if n2:
                    cross_values(n2, 1)
                    transpose_max(n2, 3)
            iterations(pe, step)


def feed_forward(nc, out, x2_dram, ident, x2T_all, xmax_all, wT, w_down):
    with ExitStack() as keep:
        def sb(name, shape, dt=F32):
            return keep.enter_context(nc.sbuf_tensor(name, shape, dt))

        U = sb("U", [P, NG, FT, GT])
        up_q = sb("up_q", [P, NG, FT, GT], I16)
        tiny = {n: sb(n, [P, 1]) for n in (
            "x_scale", "x_inv", "up_scale", "up_inv", "gate_scale", "gate_inv",
            "glu_unit", "glu_scale", "glu_inv", "h_unit", "h_scale", "h_inv")}
        ones = sb("ones", [P, P])
        wd = [t[:].rearrange("p k n -> p (k n)").rearrange("p (m n) -> p m n", m=FT) for t in wT["w_gate"]]
        with ExitStack() as parts:
            xh = [[parts.enter_context(nc.sbuf_tensor(f"xq{q}_{p}", [P, KT, GT], F32R)) for p in ("hi", "lo")]
                  for q in range(2)]
            gate_product(nc, x2T_all, xmax_all, wT["w_gate"], ident, ones, U, xh, tiny)
            gated(nc, x2T_all, wT["w_up"], w_down, wd, ident, ones, U, up_q, xh, tiny)
            hidden_values(nc, x2T_all, wT["w_up"], w_down, ident, ones, U, up_q, xh, tiny)
        down(nc, out, x2_dram, x2T_all, wT["w_up"], w_down, wd, U, tiny)


class GlobalMax:

    def __init__(self, ctx, nc, name, ones, ident, bank):
        self.ones, self.ident, self.bank = ones, ident, bank
        self.diag = ctx.enter_context(nc.sbuf_tensor(f"{name}_diag", [P, P], F32))
        self.col = ctx.enter_context(nc.sbuf_tensor(f"{name}_col", [P, 1], F32))
        self.top = ctx.enter_context(nc.sbuf_tensor(f"{name}_top", [P, 1], F32))
        self.col_done = ctx.enter_context(nc.semaphore(f"{name}_col_done"))
        self.diag_done = ctx.enter_context(nc.semaphore(f"{name}_diag_done"))
        self.spread = ctx.enter_context(nc.semaphore(f"{name}_spread"))
        self.top_done = ctx.enter_context(nc.semaphore(f"{name}_top_done"))

    def vector(self, dve, maxima):
        self.spread_out(dve, maxima)
        self.gather(dve)

    def spread_out(self, dve, maxima):
        dve.tensor_reduce(self.col[:], maxima, AX.X, ALU.max).then_inc(self.col_done, 1)
        dve.wait_ge(self.col_done, 1)
        dve.tensor_scalar(self.diag[:], self.ident[:], self.col[:, 0:1], None, ALU.mult).then_inc(self.diag_done, 1)

    def gather(self, dve):
        dve.wait_ge(self.spread, 1)
        dve.tensor_reduce(self.top[:], self.bank, AX.X, ALU.max).then_inc(self.top_done, 1)
        dve.wait_ge(self.top_done, 1)

    def tensor(self, pe):
        pe.wait_ge(self.diag_done, 1)
        pe.matmul(self.bank, self.ones[:], self.diag[:], start=True, stop=True).then_inc(self.spread, 1)


HG = FT // 2
NH = 2 * NG


def xpart(x2T_all, g, part_):
    return x2T_all[:].bitcast(I16)[:, :, bass.ds(g * (2 * GT) + part_ * GT, GT)]


def half_of(t, g, h):
    return t[:, bass.ds(g, 1), h * HG:(h + 1) * HG, :].rearrange("p o m t -> p (o m) t")


def over_groups(eng, step):
    for g in range(2):
        step(g, g, False)
    with eng.Fori(1, NG // 2 - 1) as r:
        for p in range(2):
            step(r * 2 + p, p, False)
    for g in (NG - 2, NG - 1):
        step(g, g % 2, g == NG - 1)


def float_parts(act, x2T_all, xh, g, p, product, x_parts):
    wait(act, product, g * 2 - 2)
    act.activation(xh[p][0][:], xpart(x2T_all, g, 0), ACT.Copy)
    act.activation(xh[p][1][:], xpart(x2T_all, g, 1), ACT.Copy).then_inc(x_parts, 1)


def products(pe, w, xh, bank, g, p, x_parts, product, freed):
    pe.wait_ge(x_parts, g + 1)
    for h in range(2):
        wait(pe, freed, g * 2 + (h - 1))
        for m in range(h * HG, (h + 1) * HG):
            for k in range(KT):
                lhs = [x[:, k, m * P:(m + 1) * P] for x in w]
                rhs = [x[:, k, :] for x in xh[p]]
                dst = bank[h][:, m % HG, 0:GT]
                pe.matmul(dst, lhs[0], rhs[0], start=(k == 0), stop=False)
                pe.matmul(dst, lhs[0], rhs[1], start=False, stop=False)
                ins = pe.matmul(dst, lhs[1], rhs[0], start=False, stop=(k == KT - 1))
        ins.then_inc(product, 1)


class Steps:

    def __init__(self, dve, sem):
        self.dve, self.sem, self.count = dve, sem, 0

    def done(self, ins):
        self.count += 1
        ins.then_inc(self.sem, 1)
        self.dve.wait_ge(self.sem, self.count)

    def quantiser(self, top, unit, scale, inv):
        self.done(self.dve.tensor_scalar(scale[:], top[:], unit[:, 0:1], None, ALU.mult))
        self.done(self.dve.tensor_scalar(scale[:], scale[:], 1.0 / QMAX, TINY, ALU.mult, ALU.max))
        self.done(self.dve.reciprocal(inv[:], scale[:]))
        self.done(self.dve.tensor_scalar(inv[:], inv[:], unit[:, 0:1], None, ALU.mult))


def gate_product(nc, x2T_all, xmax_all, w_gate, ident, ones, U, xh, tiny):
    with ExitStack() as ctx:
        def sem(name):
            return ctx.enter_context(nc.semaphore(name))

        xq = ctx.enter_context(nc.sbuf_tensor("xq", [P, KT, GT], I16))
        maxima = ctx.enter_context(nc.sbuf_tensor("gate_maxima", [P, NG], F32))
        bank = [ctx.enter_context(nc.psum_tensor(f"gbank{h}", [P, HG, BANK], F32)) for h in range(2)]
        spread = [ctx.enter_context(nc.psum_tensor(f"gspread{p}", [P, BANK], F32)) for p in range(2)]
        ones_done, steps, xq_done, xpart_done = (sem(f"g{n}") for n in ("ones_done", "steps", "xq_done", "xpart_done"))
        x_parts, product, stored, maxed = (sem(f"g{n}") for n in ("x_parts", "product", "stored", "maxed"))
        top = [GlobalMax(ctx, nc, n, ones, ident, spread[k][:, 0:P]) for k, n in enumerate(("x_top", "gate_top"))]
        block = ctx.enter_context(nc.Block())

        @block.gpsimd
        def _(pool):
            pool.memset(ones[:], 1.0).then_inc(ones_done, 1)

        @block.scalar
        def _(act):
            def parts(g, p):
                act.wait_ge(xpart_done, g + 1)
                float_parts(act, x2T_all, xh, g, p, product, x_parts)

            def step(g, p, last):
                if not last:
                    parts(g + 1, 1 - p)
                for h in range(2):
                    act.wait_ge(product, g * 2 + (h + 1))
                    act.activation(half_of(U, g, h), bank[h][:, :, 0:GT], ACT.Copy).then_inc(stored, 1)

            parts(0, 0)
            over_groups(act, step)

        @block.vector
        def _(dve):
            def quantise_x(g):
                wait(dve, xpart_done, g)
                dve.tensor_scalar(xq[:], x2T_all[:, :, bass.ds(g * GT, GT)], tiny["x_inv"][:, 0:1], None,
                                  ALU.mult).then_inc(xq_done, 1)
                dve.wait_ge(xq_done, g + 1)
                dve.tensor_scalar(xpart(x2T_all, g, 0), xq[:], HIGH, None, ALU.bitwise_and)
                dve.tensor_scalar(xpart(x2T_all, g, 1), xq[:], LOW, None, ALU.bitwise_and).then_inc(xpart_done, 1)

            def step(g, p, last):
                if not last:
                    quantise_x(g + 1)
                dve.wait_ge(stored, g * 2 + 2)
                dve.tensor_reduce(maxima[:, bass.ds(g, 1)], U[:, bass.ds(g, 1)], AX.XYZ, ALU.max,
                                  apply_absolute_value=True).then_inc(maxed, 1)

            top[0].vector(dve, xmax_all[:])
            small = Steps(dve, steps)
            small.done(dve.tensor_scalar(tiny["x_scale"][:], top[0].top[:], 1.0 / QMAX, TINY, ALU.mult, ALU.max))
            small.done(dve.reciprocal(tiny["x_inv"][:], tiny["x_scale"][:]))
            quantise_x(0)
            over_groups(dve, step)
            dve.wait_ge(maxed, NG)
            top[1].vector(dve, maxima[:])
            small.quantiser(top[1].top, tiny["x_scale"], tiny["gate_scale"], tiny["gate_inv"])

        @block.tensor
        def _(pe):
            pe.wait_ge(ones_done, 1)
            top[0].tensor(pe)
            over_groups(pe, lambda g, p, last: products(pe, w_gate, xh, bank, g, p, x_parts, product, stored))
            top[1].tensor(pe)


def gated(nc, x2T_all, w_up, w_down, wd, ident, ones, U, up_q, xh, tiny):
    with ExitStack() as ctx:
        def sem(name):
            return ctx.enter_context(nc.semaphore(name))

        room = up_q[:].rearrange("p g m t -> p (g m t)")
        N = HG * GT
        sig = [room[:, 2 * k * N:2 * (k + 1) * N].bitcast(F32).rearrange("p (m t) -> p m t", m=HG) for k in range(2)]
        gate_q = [room[:, (4 + k) * N:(5 + k) * N].rearrange("p (m t) -> p m t", m=HG) for k in range(2)]
        sig_q = [room[:, (6 + k) * N:(7 + k) * N].bitcast(U16).rearrange("p (m t) -> p m t", m=HG) for k in range(2)]
        maxima = {n: ctx.enter_context(nc.sbuf_tensor(f"{n}_maxima", [P, NH], F32)) for n in ("up", "glu")}
        bank = [ctx.enter_context(nc.psum_tensor(f"ubank{h}", [P, HG, BANK], F32)) for h in range(2)]
        spare = [ctx.enter_context(nc.psum_tensor(f"uspare{p}", [P, BANK], F32)) for p in range(2)]
        turned, hi_done, lo_done, steps = (sem(f"u{n}") for n in ("turned", "hi_done", "lo_done", "steps"))
        x_parts, product, up_maxed = (sem(f"u{n}") for n in ("x_parts", "product", "maxed"))
        gate_q_done, sig_done, sig_q_done = sem("gate_q_done"), sem("sig_done"), sem("sig_q_done")
        glu_done, glu_maxed = sem("glu_done"), sem("glu_maxed")
        top = {n: GlobalMax(ctx, nc, f"{n}_top", ones, ident, spare[k][:, 0:P]) for k, n in enumerate(("up", "glu"))}
        N_FILLS = 2 * KT
        block = ctx.enter_context(nc.Block())

        def down_part(half, f):
            return wd[half][:, (f % 2) * HG:(f % 2 + 1) * HG, (f // 2) * P:(f // 2 + 1) * P]

        @block.scalar
        def _(act):
            for f in range(N_FILLS):
                act.wait_ge(turned, f + 1)
                act.activation(down_part(0, f), spare[f % 2][:, 0:HG * P].rearrange("p (m n) -> p m n", m=HG),
                               ACT.Copy).then_inc(hi_done, 1)

            def sigmoid(g, h):
                wait(act, glu_done, g * 2 + (h - 1))
                act.activation(gate_q[h], half_of(U, g, h), ACT.Copy, scale=tiny["gate_inv"][:, 0:1])\
                    .then_inc(gate_q_done, 1)
                act.wait_ge(gate_q_done, g * 2 + (h + 1))
                act.activation(sig[h], gate_q[h], ACT.Sigmoid, scale=tiny["gate_scale"][:, 0:1]).then_inc(sig_done, 1)
                act.wait_ge(sig_done, g * 2 + (h + 1))
                act.activation(sig_q[h], sig[h], ACT.Copy, scale=SIGQ).then_inc(sig_q_done, 1)

            def step(g, p, last):
                if not last:
                    float_parts(act, x2T_all, xh, g + 1, 1 - p, product, x_parts)
                sigmoid(g, 0)
                sigmoid(g, 1)

            float_parts(act, x2T_all, xh, 0, 0, product, x_parts)
            over_groups(act, step)

        @block.vector
        def _(dve):
            for f in range(N_FILLS):
                dve.wait_ge(hi_done, f + 1)
                dve.tensor_tensor(down_part(1, f), spare[f % 2][:, 0:HG * P].rearrange("p (m n) -> p m n", m=HG),
                                  down_part(0, f).bitcast(F32), ALU.subtract).then_inc(lo_done, 1)

            def largest_up(g, h):
                dve.wait_ge(product, g * 2 + (h + 1))
                dve.tensor_reduce(maxima["up"][:, bass.ds(g * 2 + h, 1)], bank[h][:, :, 0:GT], AX.XY, ALU.max,
                                  apply_absolute_value=True).then_inc(up_maxed, 1)

            def glu(g, h):
                dve.wait_ge(sig_q_done, g * 2 + (h + 1))
                dve.tensor_tensor(half_of(U, g, h), gate_q[h], sig_q[h], ALU.mult).then_inc(glu_done, 1)

            def largest_glu(g, h):
                dve.wait_ge(glu_done, g * 2 + (h + 1))
                dve.tensor_reduce(maxima["glu"][:, bass.ds(g * 2 + h, 1)], half_of(U, g, h), AX.XY, ALU.max,
                                  apply_absolute_value=True).then_inc(glu_maxed, 1)

            def step(g, p, last):
                for h in range(2):
                    largest_up(g, h)
                    glu(g, h)
                    if h:
                        largest_glu(g, 0)
                    elif not isinstance(g, int) or g > 0:
                        largest_glu(g - 1, 1)

            over_groups(dve, step)
            dve.wait_ge(up_maxed, NH)
            top["up"].spread_out(dve, maxima["up"][:])
            largest_glu(NG - 1, 1)
            dve.wait_ge(glu_maxed, NH)
            top["glu"].spread_out(dve, maxima["glu"][:])
            top["up"].gather(dve)
            small = Steps(dve, steps)
            small.quantiser(top["up"].top, tiny["x_scale"], tiny["up_scale"], tiny["up_inv"])
            top["glu"].gather(dve)
            small.done(dve.tensor_scalar(tiny["glu_unit"][:], tiny["gate_scale"][:], 1.0 / SIGQ, None, ALU.mult))
            small.quantiser(top["glu"].top, tiny["glu_unit"], tiny["glu_scale"], tiny["glu_inv"])

        @block.tensor
        def _(pe):
            for f in range(N_FILLS):
                if f >= 2:
                    pe.wait_ge(lo_done, f - 1)
                for j in range(HG):
                    m = (f % 2) * HG + j
                    ins = pe.transpose(spare[f % 2][:, j * P:(j + 1) * P], w_down[:, f // 2, m * P:(m + 1) * P], ident[:])
                ins.then_inc(turned, 1)
            over_groups(pe, lambda g, p, last: products(pe, w_up, xh, bank, g, p, x_parts, product, up_maxed))
            pe.wait_ge(lo_done, N_FILLS)
            top["up"].tensor(pe)
            top["glu"].tensor(pe)


def hidden_values(nc, x2T_all, w_up, w_down, ident, ones, U, up_q, xh, tiny):
    with ExitStack() as ctx:
        def sem(name):
            return ctx.enter_context(nc.semaphore(name))

        ints = w_down[:].rearrange("p k n -> p (k n)").bitcast(I16)
        glu_q = [ints[:, h * HG * GT:(h + 1) * HG * GT].rearrange("p (m t) -> p m t", m=HG) for h in range(2)]
        maxima = ctx.enter_context(nc.sbuf_tensor("h_maxima", [P, NH], F32))
        bank = [ctx.enter_context(nc.psum_tensor(f"hbank{h}", [P, HG, BANK], F32)) for h in range(2)]
        spread = ctx.enter_context(nc.psum_tensor("hspread", [P, BANK], F32))
        x_parts, product, steps = (sem(f"h{n}") for n in ("x_parts", "product", "steps"))
        glu_q_done, up_q_done, h_done, h_maxed = sem("glu_q_done"), sem("up_q_done"), sem("h_done"), sem("h_maxed")
        top = GlobalMax(ctx, nc, "h_top", ones, ident, spread[:, 0:P])
        block = ctx.enter_context(nc.Block())

        @block.scalar
        def _(act):
            def step(g, p, last):
                if not last:
                    float_parts(act, x2T_all, xh, g + 1, 1 - p, product, x_parts)
                for h in range(2):
                    wait(act, h_done, g * 2 + (h - 1))
                    act.activation(glu_q[h], half_of(U, g, h), ACT.Copy, scale=tiny["glu_inv"][:, 0:1])\
                        .then_inc(glu_q_done, 1)
                    act.wait_ge(product, g * 2 + (h + 1))
                    act.activation(half_of(up_q, g, h), bank[h][:, :, 0:GT], ACT.Copy, scale=tiny["up_inv"][:, 0:1])\
                        .then_inc(up_q_done, 1)

            float_parts(act, x2T_all, xh, 0, 0, product, x_parts)
            over_groups(act, step)

        @block.vector
        def _(dve):
            def hidden(g, h):
                dve.wait_ge(glu_q_done, g * 2 + (h + 1))
                dve.wait_ge(up_q_done, g * 2 + (h + 1))
                dve.tensor_tensor(half_of(U, g, h), glu_q[h], half_of(up_q, g, h), ALU.mult).then_inc(h_done, 1)

            def largest(g, h):
                dve.wait_ge(h_done, g * 2 + (h + 1))
                dve.tensor_reduce(maxima[:, bass.ds(g * 2 + h, 1)], half_of(U, g, h), AX.XY, ALU.max,
                                  apply_absolute_value=True).then_inc(h_maxed, 1)

            def step(g, p, last):
                hidden(g, 0)
                if not isinstance(g, int) or g > 0:
                    largest(g - 1, 1)
                hidden(g, 1)
                largest(g, 0)

            over_groups(dve, step)
            largest(NG - 1, 1)
            dve.wait_ge(h_maxed, NH)
            top.vector(dve, maxima[:])
            small = Steps(dve, steps)
            small.done(dve.tensor_scalar(tiny["h_unit"][:], tiny["glu_scale"][:], tiny["up_scale"][:, 0:1], None, ALU.mult))
            small.quantiser(top.top, tiny["h_unit"], tiny["h_scale"], tiny["h_inv"])

        @block.tensor
        def _(pe):
            over_groups(pe, lambda g, p, last: products(pe, w_up, xh, bank, g, p, x_parts, product, up_q_done))
            top.tensor(pe)


def down(nc, out, x2_dram, x2T_all, w_up, w_down, wd, U, tiny):
    TG = GT // L
    AHEAD = 3
    with ExitStack() as ctx:
        def sb(name, shape, dt=F32):
            return ctx.enter_context(nc.sbuf_tensor(name, shape, dt))

        def sem(name):
            return ctx.enter_context(nc.semaphore(name))

        room = x2T_all[:].rearrange("p k n -> p (k n)")
        tiles = [room[0:L, k * D:(k + 1) * D] for k in range(TG + 4)]
        x2, r, res = tiles[:TG], tiles[TG:TG + 2], tiles[TG + 2:]
        hq = [sb(f"hq{q}", [P, FT, L], I16) for q in range(2)]
        spare = w_down[:].rearrange("p k n -> p (k n)")
        whole = [spare[:, q * FT * L:(q + 1) * FT * L].rearrange("p (m t) -> p m t", m=FT) for q in range(2)]
        free = [t[:].rearrange("p k n -> p (k n)") for t in w_up] + [sb(f"hh{t}", [P, 2 * FT * L], F32R)[:] for t in (2, 3)]
        hh = [[f[:, k * FT * L:(k + 1) * FT * L].rearrange("p (m t) -> p m t", m=FT) for k in range(2)] for f in free]
        carrier = sb("fcarrier", [1, 1])
        stats = [sb(f"fstats{p}", [L, 6]) for p in range(2)]
        mv = [sb(f"fmv{p}", [L, 2]) for p in range(2)]
        vare = [sb(f"fvare{p}", [L, 1]) for p in range(2)]
        rstd = [sb(f"frstd{p}", [L, 1]) for p in range(2)]
        half = sb("fhalf", [L, 1])
        obank = [ctx.enter_context(nc.psum_tensor(f"obank{p}", [P, BANK], F32)) for p in range(4)]
        half_done = sem("half_done")
        hq_done, whole_done, hi_halves, lo_halves = (sem(n) for n in ("hq_done", "whole_done", "hi_halves", "lo_halves"))
        down_done, resid_done, fbn_done, fmv_done = sem("down_done"), sem("resid_done"), sem("fbn_done"), sem("fmv_done")
        fvar_done, frstd_done, res_done = sem("fvar_done"), sem("frstd_done"), sem("res_done")
        x2_ld = [sem(f"x2_ld{t}") for t in range(TG)]
        out_st = [sem(f"out_st{p}") for p in range(2)]
        block = ctx.enter_context(nc.Block())
        @block.sync
        def _(sp):
            def load(n, par):
                sp.dma_start(x2[par], x2_dram[bass.ds(n, 1)].rearrange("o l d -> (o l) d")).then_inc(x2_ld[par], 16)

            def store(n, par, count):
                sp.wait_ge(res_done, count)
                sp.dma_start(out[bass.ds(n, 1)].rearrange("o l d -> (o l) d"), res[par]).then_inc(out_st[par], 16)

            for t in range(TG):
                load(t, t)
            with sp.Fori(0, NG - 1) as g:
                for t in range(TG):
                    sp.wait_ge(resid_done, g * TG + (t + 1))
                    load(g * TG + (t + TG), t)
                    store(g * TG + t, t % 2, g * TG + (t + 1))
            for t in range(TG):
                store(B - TG + t, t % 2, B - TG + t + 1)
            for p in range(2):
                sp.wait_ge(out_st[p], 16 * (B // 2))

        @block.gpsimd
        def _(pool):
            pool.memset(half[:], -0.5).then_inc(half_done, 1)
            pool.wait_ge(half_done, 1)

            def root(count, p):
                pool.wait_ge(fvar_done, count)
                pool.tensor_tensor(rstd[p][:], vare[p][:], half[:], ALU.pow).then_inc(frstd_done, 1)

            def lo_half(n, t):
                pool.wait_ge(hi_halves, n + 1)
                pool.tensor_tensor(hh[t][1], whole[t % 2], hh[t][0].bitcast(F32), ALU.subtract).then_inc(lo_halves, 1)

            for t in range(AHEAD):
                lo_half(t, t)
            with pool.Fori(0, NG - 1) as g:
                for t in range(TG):
                    lo_half(g * TG + (t + AHEAD), (t + AHEAD) % TG)
                    root(g * TG + (t + 1), t % 2)
            for t in range(TG):
                if t + AHEAD < TG:
                    lo_half(B - TG + t + AHEAD, t + AHEAD)
                root(B - TG + t + 1, t % 2)

        @block.scalar
        def _(act):
            def tile(n, t):
                p = t % 2
                act.wait_ge(hq_done, n + 1)
                wait(act, lo_halves, n - 1)
                act.activation(whole[p], hq[p][:], ACT.Copy).then_inc(whole_done, 1)
                wait(act, down_done, n - (TG - 1))
                act.activation(hh[t][0], hq[p][:], ACT.Copy).then_inc(hi_halves, 1)

            for t in range(TG):
                tile(t, t)
            with act.Fori(1, NG) as g:
                for t in range(TG):
                    tile(g * TG + t, t)

        @block.vector
        def _(dve):
            def hidden_ints(g, t, p, made):
                wait(dve, hi_halves, made - 1)
                dve.tensor_scalar(hq[p][:], U[:, bass.ds(g, 1), :, t * L:(t + 1) * L].rearrange("p o m t -> p (o m) t"),
                                  tiny["h_inv"][:, 0:1], None, ALU.mult).then_inc(hq_done, 1)

            def residual(count, loads, t):
                p = t % 2
                dve.wait_ge(down_done, count)
                dve.wait_ge(x2_ld[t], loads)
                wait(dve, res_done, count - 2)
                dve.scalar_tensor_tensor(r[p], obank[t][0:L, 0:D], tiny["h_scale"][:, 0:1][0:L], x2[t],
                                         ALU.mult, ALU.add).then_inc(resid_done, 1)
                dve.wait_ge(resid_done, count)
                dve.bn_stats(stats[p][:], r[p]).then_inc(fbn_done, 1)
                dve.wait_ge(fbn_done, count)
                dve.memset(carrier[:], 0.0)
                dve.bn_aggr(mv[p][:], stats[p][:]).then_inc(fmv_done, 1)
                dve.wait_ge(fmv_done, count)
                dve.tensor_scalar(vare[p][:], mv[p][:, 1:2], EPS, None, ALU.add).then_inc(fvar_done, 1)

            def norm(count, p, stored):
                dve.wait_ge(frstd_done, count)
                wait(dve, out_st[p], stored)
                dve.tensor_scalar(res[p], r[p], mv[p][:, 0:1], rstd[p][:, 0:1], ALU.subtract, ALU.mult)\
                    .then_inc(res_done, 1)

            def integers_ahead(g, t):
                later, u = divmod(t + AHEAD, TG)
                hidden_ints(g + later, u, u % 2, g * TG + (t + AHEAD))

            for t in range(AHEAD):
                hidden_ints(0, t, t % 2, t)
            for t in range(TG):
                integers_ahead(0, t)
                residual(t + 1, 16, t)
                if t:
                    norm(t, (t - 1) % 2, 16 * ((t - 1) // 2))
            with dve.Fori(1, NG - 1) as g:
                for t in range(TG):
                    integers_ahead(g, t)
                    residual(g * TG + (t + 1), g * 16 + 16, t)
                    norm(g * TG + t, (t - 1) % 2, g * (8 * TG) + 16 * ((t - 1) // 2))
            g = NG - 1
            for t in range(TG):
                if t + AHEAD < TG:
                    integers_ahead(g, t)
                residual(g * TG + t + 1, g * 16 + 16, t)
                norm(g * TG + t, (t - 1) % 2, g * (8 * TG) + 16 * ((t - 1) // 2))
            norm(B, 1, 16 * (B // 2 - 1))

        @block.tensor
        def _(pe):
            def tile(n, t):
                pe.wait_ge(lo_halves, n + 1)
                wait(pe, resid_done, n - (TG - 1))
                for m in range(FT):
                    lhs, rhs = [x[:, m, :] for x in hh[t]], [x[:, m, :] for x in wd]
                    dst = obank[t][0:L, 0:D]
                    pe.matmul(dst, lhs[0], rhs[0], start=(m == 0), stop=False)
                    pe.matmul(dst, lhs[0], rhs[1], start=False, stop=False)
                    ins = pe.matmul(dst, lhs[1], rhs[0], start=False, stop=(m == FT - 1))
                ins.then_inc(down_done, 1)

            for t in range(TG):
                tile(t, t)
            with pe.Fori(1, NG) as g:
                for t in range(TG):
                    tile(g * TG + t, t)


_INS = {"x": "x", "ctx_1024": "ctx",
        "L0_attn_Wq": "aWq", "L0_attn_Wk": "aWk", "L0_attn_Wv": "aWv", "L0_attn_Wo": "aWo",
        "L0_attn_bq": "a_bq", "L0_attn_bk": "a_bk", "L0_attn_bv": "a_bv", "L0_attn_bo": "a_bo",
        "L0_xattn_Wq": "xWq", "L0_xattn_Wk": "xWk", "L0_xattn_Wv": "xWv", "L0_xattn_Wo": "xWo",
        "L0_xattn_bq": "x_bq", "L0_xattn_bk": "x_bk", "L0_xattn_bv": "x_bv", "L0_xattn_bo": "x_bo",
        "L0_ffn_w_gate": "w_gate", "L0_ffn_w_up": "w_up", "L0_ffn_w_down": "w_down"}


def shape_constants():
    bf16 = mybir.dt.np(BF16)

    def pieces(v):
        got, rest = [], v.astype(np.float32)
        for _ in range(3):
            got.append(rest.astype(bf16))
            rest = (rest - got[-1].astype(np.float32)).astype(np.float32)
        return got

    row = np.arange(P)
    slopes = (np.float32(1.0) / np.float32(2.0) ** (np.arange(H, dtype=np.float32) / np.float32(H))).astype(np.float32)
    key = np.arange(L, dtype=np.float32)
    sel = np.zeros((P, OCT * L), np.float32)
    for h in range(OCT):
        sel[h, h * L:(h + 1) * L] = 1.0
    alibi_l = np.stack([np.ones(L)] * 3 + [-key] * 3).astype(bf16)
    alibi_r = np.stack([p.reshape(-1) for p in pieces(slopes[:, None] * key[None, :])]
                       + [np.repeat(p, L) for p in pieces(slopes)])
    return {"ident": np.eye(P, dtype=np.float32),
            "mask8": (row[:, None] // HD == np.arange(OCT)[None, :]).astype(np.float32),
            "even_odd": np.stack([(row // HD) % 2 == 0, (row // HD) % 2 == 1], 1).astype(np.float32),
            "sel": sel, "alibi_l": alibi_l, "alibi_r": alibi_r.astype(bf16)}


def kernel(**inputs):
    import concourse.bacc as _bacc
    from concourse.bass_utils import run_bass_kernel_spmd as _run

    nc = _bacc.Bacc("TRN2", target_bir_lowering=False, num_devices=1)
    arrays, aps = {}, {}
    given = {short: np.ascontiguousarray(inputs[name]) for name, short in _INS.items()}
    given.update(shape_constants())
    for short, v in given.items():
        arrays[f"in_{short}"] = v
        aps[short] = nc.dram_tensor(f"in_{short}", v.shape, mybir.dt.from_np(v.dtype), kind="ExternalInput").ap()
    out = nc.dram_tensor("out_0", (B, L, D), F32, kind="ExternalOutput").ap()
    x2_dram = nc.dram_tensor("x2_scratch", (B, L, D), F32, kind="Internal").ap()
    decoder(nc, aps, out, x2_dram)
    r = _run(nc, [arrays], core_ids=[0])
    return r.results[0]["out_0"]
```
